# Optimizing a Trainium2 kernel written in Bass

```python
import numpy as np
import jax
import jax.numpy as jnp

def _softmax(x, axis=-1):
    return jax.nn.softmax(x, axis=axis)

def _gelu(x):
    return jax.nn.gelu(x, approximate=True)

def _silu(x):
    return jax.nn.silu(x)

def _sigmoid(x):
    return jax.nn.sigmoid(x)

def _layernorm(x, axis=-1, eps=1e-05):
    m = jnp.mean(x, axis=axis, keepdims=True)
    v = jnp.var(x, axis=axis, keepdims=True)
    return (x - m) / jnp.sqrt(v + eps)

def _scatter_add(tgt, idx, src, axis=0):
    return tgt.at[idx].add(src)

def _segment_sum(src, seg, n):
    return jax.ops.segment_sum(src, seg, n)
kernel_name = 'mk_perceiver_d2_seqx_r4_64f019'

def setup_inputs(seed: int=0):
    np.random.seed(seed)
    _w = jnp.asarray

    def _rec_inputs():
        import jax
        import jax.numpy as jnp
        _rk = jax.random.key(seed)
        x = -0.000929 + 1 * jax.random.normal(jax.random.fold_in(_rk, 1), (16, 64, 256), jnp.float32)
        _lenS = 64 - jax.random.randint(jax.random.fold_in(_rk, 7), (16,), 0, max(1, 64 // 4) + 1, jnp.int32)
        _lenS2 = 256 - jax.random.randint(jax.random.fold_in(_rk, 8), (16,), 0, max(1, 256 // 4) + 1, jnp.int32)
        _ctx_1024P = jax.random.normal(jax.random.fold_in(_rk, 11), (16, 16, 256), jnp.float32)
        _ctx_1024c = jax.random.dirichlet(jax.random.fold_in(_rk, 511), 0.3 * jnp.ones((16,), jnp.float32), (16, 256))
        _ctx_1024t = jnp.einsum('bsk,bkd->bsd', _ctx_1024c, _ctx_1024P)
        _ctx_1024t = _ctx_1024t * jax.lax.rsqrt(jnp.mean(jnp.square(_ctx_1024t)) + 1e-12) * 0.953939
        ctx_1024 = -1.52775e-05 + 0.999936 * (_ctx_1024t + 0.3 * jax.random.normal(jax.random.fold_in(_rk, 611), (16, 256, 256), jnp.float32))
        _validS = jnp.arange(64)[None, :] < _lenS[:, None]
        _validS2 = jnp.arange(256)[None, :] < _lenS2[:, None]
        _causal = jnp.tril(jnp.ones((64, 64), dtype=bool))
        mask_BxS2_ik0 = jnp.where(jnp.broadcast_to(_validS2[:, :], (16, 256)), 0, 1).astype(jnp.int32)
        return (x, ctx_1024, mask_BxS2_ik0)
    x, ctx_1024, mask_BxS2_ik0 = _rec_inputs()

    def _L0_xattn_setup():
        import jax, jax.numpy as jnp
        import numpy as np
        DIM = 256
        H = 16
        D = 64
        INNER = H * D
        EPS = 1e-05

        def layernorm(x, w, b):
            mu = jnp.mean(x, axis=-1, keepdims=True)
            var = jnp.var(x, axis=-1, keepdims=True)
            return (x - mu) * jax.lax.rsqrt(var + EPS) * w + b
        key = jax.random.key(seed)
        ks = jax.random.split(key, 8)
        B, N, S = (4, 64, 2048)
        s = 1.0 / np.sqrt(DIM)
        return {'latents': jax.random.normal(ks[0], (B, N, DIM), jnp.float32), 'context': jax.random.normal(ks[1], (B, S, DIM), jnp.float32), 'ln_l_w': jnp.ones((DIM,), jnp.float32), 'ln_l_b': jnp.zeros((DIM,), jnp.float32), 'ln_c_w': jnp.ones((DIM,), jnp.float32), 'ln_c_b': jnp.zeros((DIM,), jnp.float32), 'Wq': jax.random.normal(ks[2], (DIM, INNER), jnp.float32) * s, 'Wkv': jax.random.normal(ks[3], (DIM, 2 * INNER), jnp.float32) * s, 'Wo': jax.random.normal(ks[4], (INNER, DIM), jnp.float32) * (1.0 / np.sqrt(INNER)), 'bo': jnp.zeros((DIM,), jnp.float32)}
    _L0_xattn_all = _L0_xattn_setup()
    _L0_xattn_in = {k: v for k, v in _L0_xattn_all.items() if k in ('ln_l_w', 'ln_l_b', 'ln_c_w', 'ln_c_b', 'Wq', 'Wkv', 'Wo', 'bo')}
    del _L0_xattn_all

    def _L0_attn_setup():
        import jax, jax.numpy as jnp
        import numpy as np
        import math
        B, S, E = (2, 512, 256)
        H, DC, DR = (16, 64, 128)
        HD = E // H

        def _linear_params(key, din, dout):
            k1, k2 = jax.random.split(key)
            bound = 1.0 / math.sqrt(din)
            w = jax.random.uniform(k1, (din, dout), minval=-bound, maxval=bound, dtype=jnp.float32)
            b = jax.random.uniform(k2, (dout,), minval=-bound, maxval=bound, dtype=jnp.float32)
            return (w, b)

        def _gelu(x):
            return jax.nn.gelu(x, approximate=False)

        def _rope_cos_sin(seq_len, d_rope):
            inv_freq = 1.0 / 10000.0 ** (jnp.arange(0, d_rope, 2, dtype=jnp.float32) / d_rope)
            t = jnp.arange(seq_len, dtype=jnp.float32)
            freqs = t[:, None] * inv_freq[None, :]
            emb = jnp.concatenate([freqs, freqs], axis=-1)
            return (jnp.cos(emb), jnp.sin(emb))

        def _apply_rope(x, cos, sin):
            d = x.shape[-1]
            x1, x2 = (x[..., :d // 2], x[..., d // 2:])
            rot = jnp.concatenate([-x2, x1], axis=-1)
            return x * cos + rot * sin
        key = jax.random.key(seed)
        ks = jax.random.split(key, 10)
        x = jax.random.normal(ks[0], (B, S, E), dtype=jnp.float32)
        wq, bq = _linear_params(ks[1], E, DC)
        wqc, bqc = _linear_params(ks[2], DC, E - DR)
        wqr, bqr = _linear_params(ks[3], E, DR)
        wkv, bkv = _linear_params(ks[4], E, DC)
        wkr, bkr = _linear_params(ks[5], E, DR)
        wkc, bkc = _linear_params(ks[6], DC, E - DR)
        wv, bv = _linear_params(ks[7], DC, E)
        wo, bo = _linear_params(ks[8], E, E)
        return dict(x=x, wq=wq, bq=bq, wqc=wqc, bqc=bqc, wqr=wqr, bqr=bqr, wkv=wkv, bkv=bkv, wkr=wkr, bkr=bkr, wkc=wkc, bkc=bkc, wv=wv, bv=bv, wo=wo, bo=bo)
    _L0_attn_all = _L0_attn_setup()
    _L0_attn_in = {k: v for k, v in _L0_attn_all.items() if k in ('wq', 'bq', 'wqc', 'bqc', 'wqr', 'bqr', 'wkv', 'bkv', 'wkr', 'bkr', 'wkc', 'bkc', 'wv', 'bv', 'wo', 'bo')}
    del _L0_attn_all

    def _L0_ffn_setup():
        import jax, jax.numpy as jnp
        import numpy as np
        B, S, D, H, E, F, K = (2, 256, 256, 16, 8, 1024, 2)
        EPS = 1e-05

        def _layernorm(x, g, b):
            mu = jnp.mean(x, axis=-1, keepdims=True)
            var = jnp.mean(jnp.square(x - mu), axis=-1, keepdims=True)
            return (x - mu) * jax.lax.rsqrt(var + EPS) * g + b
        key = jax.random.key(seed)
        ks = jax.random.split(key, 12)
        w = lambda k, shape: jax.random.normal(k, shape, dtype=jnp.float32) * 0.02
        return {'x': jax.random.normal(ks[0], (B, S, D), dtype=jnp.float32), 'ln1_g': jnp.ones((D,), jnp.float32), 'ln1_b': jnp.zeros((D,), jnp.float32), 'ln2_g': jnp.ones((D,), jnp.float32), 'ln2_b': jnp.zeros((D,), jnp.float32), 'Wq': w(ks[1], (D, D)), 'Wk': w(ks[2], (D, D)), 'Wv': w(ks[3], (D, D)), 'Wo': w(ks[4], (D, D)), 'Wg': w(ks[5], (D, E)), 'W1': w(ks[6], (E, D, F)), 'b1': jnp.zeros((E, F), jnp.float32), 'W2': w(ks[7], (E, F, D)), 'b2': jnp.zeros((E, D), jnp.float32)}
    _L0_ffn_all = _L0_ffn_setup()
    _L0_ffn_in = {k: v for k, v in _L0_ffn_all.items() if k in ('ln1_g', 'ln1_b', 'ln2_g', 'ln2_b', 'Wq', 'Wk', 'Wv', 'Wo', 'Wg', 'W1', 'b1', 'W2', 'b2')}
    del _L0_ffn_all

    def _L1_xattn_setup():
        import jax, jax.numpy as jnp
        import numpy as np
        H = 256
        NH = 16
        HD = H // NH
        key = jax.random.key(seed)
        ks = jax.random.split(key, 12)
        inp = {'query': jax.random.normal(ks[0], (4, 256, H), dtype=jnp.float32), 'key': jax.random.normal(ks[1], (4, 512, H), dtype=jnp.float32), 'value': jax.random.normal(ks[2], (4, 512, H), dtype=jnp.float32), 'key_padding_mask': jax.random.randint(ks[3], (4, 512), 0, 2, dtype=jnp.int32), 'Wq': jax.random.normal(ks[4], (H, H), dtype=jnp.float32) * (1.0 / np.sqrt(H)), 'bq': jnp.zeros((H,), dtype=jnp.float32), 'Wk': jax.random.normal(ks[5], (H, H), dtype=jnp.float32) * (1.0 / np.sqrt(H)), 'bk': jnp.zeros((H,), dtype=jnp.float32), 'Wv': jax.random.normal(ks[6], (H, H), dtype=jnp.float32) * (1.0 / np.sqrt(H)), 'bv': jnp.zeros((H,), dtype=jnp.float32), 'Wo': jax.random.normal(ks[7], (H, H), dtype=jnp.float32) * (1.0 / np.sqrt(H)), 'bo': jnp.zeros((H,), dtype=jnp.float32)}
        return inp
    _L1_xattn_all = _L1_xattn_setup()
    _L1_xattn_in = {k: v for k, v in _L1_xattn_all.items() if k in ('Wq', 'bq', 'Wk', 'bk', 'Wv', 'bv', 'Wo', 'bo')}
    del _L1_xattn_all

    def _L1_attn_setup():
        import jax, jax.numpy as jnp
        import numpy as np
        D_MODEL = 256
        NUM_HEADS = 16
        B, S = (1, 1024)
        key = jax.random.key(seed)
        kx, kq, kk, kv, ko = jax.random.split(key, 5)
        std = (1.0 / D_MODEL) ** 0.5

        def trunc(k):
            return std * jax.random.truncated_normal(k, -3.0, 3.0, (D_MODEL, D_MODEL), dtype=jnp.float32)
        return {'x': jax.random.normal(kx, (B, S, D_MODEL), dtype=jnp.float32), 'W_Q': trunc(kq), 'W_K': trunc(kk), 'W_V': trunc(kv), 'W_O': trunc(ko)}
    _L1_attn_all = _L1_attn_setup()
    _L1_attn_in = {k: v for k, v in _L1_attn_all.items() if k in ('W_Q', 'W_K', 'W_V', 'W_O')}
    del _L1_attn_all

    def _L1_ffn_setup():
        import jax, jax.numpy as jnp
        import numpy as np
        import math
        D_IN = 256
        FEATURES = (1024, 1024, 256)
        BATCH, SEQ = (8, 512)

        def _conn_dense(kernel_bool, x):
            w = jnp.where(kernel_bool, jnp.float32(1.0), jnp.float32(-1.0))
            return x @ w
        key = jax.random.key(seed)
        kx, kk0, kk1, kk2 = jax.random.split(key, 4)
        x = jax.random.normal(kx, (BATCH, SEQ, D_IN), dtype=jnp.float32)
        k0 = jax.random.randint(kk0, (2 * D_IN, FEATURES[0]), 0, 2).astype(jnp.bool_)
        k1 = jax.random.randint(kk1, (FEATURES[0], FEATURES[1]), 0, 2).astype(jnp.bool_)
        k2 = jax.random.randint(kk2, (FEATURES[1], FEATURES[2]), 0, 2).astype(jnp.bool_)
        s0 = jnp.asarray(1.0 / math.sqrt(2 * D_IN), dtype=jnp.float32)
        s1 = jnp.asarray(1.0 / math.sqrt(FEATURES[0]), dtype=jnp.float32)
        s2 = jnp.asarray(1.0 / math.sqrt(FEATURES[1]), dtype=jnp.float32)
        return {'x': x, 'k0': k0, 'k1': k1, 'k2': k2, 's0': s0, 's1': s1, 's2': s2}
    _L1_ffn_all = _L1_ffn_setup()
    _L1_ffn_in = {k: v for k, v in _L1_ffn_all.items() if k in ('k0', 'k1', 'k2', 's0', 's1', 's2')}
    del _L1_ffn_all
    return {'x': x, 'ctx_1024': ctx_1024, 'mask_BxS2_ik0': mask_BxS2_ik0, 'L0_xattn_ln_l_w': _L0_xattn_in['ln_l_w'], 'L0_xattn_ln_l_b': _L0_xattn_in['ln_l_b'], 'L0_xattn_ln_c_w': _L0_xattn_in['ln_c_w'], 'L0_xattn_ln_c_b': _L0_xattn_in['ln_c_b'], 'L0_xattn_Wq': _L0_xattn_in['Wq'], 'L0_xattn_Wkv': _L0_xattn_in['Wkv'], 'L0_xattn_Wo': _L0_xattn_in['Wo'], 'L0_xattn_bo': _L0_xattn_in['bo'], 'L0_attn_wq': _L0_attn_in['wq'], 'L0_attn_bq': _L0_attn_in['bq'], 'L0_attn_wqc': _L0_attn_in['wqc'], 'L0_attn_bqc': _L0_attn_in['bqc'], 'L0_attn_wqr': _L0_attn_in['wqr'], 'L0_attn_bqr': _L0_attn_in['bqr'], 'L0_attn_wkv': _L0_attn_in['wkv'], 'L0_attn_bkv': _L0_attn_in['bkv'], 'L0_attn_wkr': _L0_attn_in['wkr'], 'L0_attn_bkr': _L0_attn_in['bkr'], 'L0_attn_wkc': _L0_attn_in['wkc'], 'L0_attn_bkc': _L0_attn_in['bkc'], 'L0_attn_wv': _L0_attn_in['wv'], 'L0_attn_bv': _L0_attn_in['bv'], 'L0_attn_wo': _L0_attn_in['wo'], 'L0_attn_bo': _L0_attn_in['bo'], 'L0_ffn_ln1_g': _L0_ffn_in['ln1_g'], 'L0_ffn_ln1_b': _L0_ffn_in['ln1_b'], 'L0_ffn_ln2_g': _L0_ffn_in['ln2_g'], 'L0_ffn_ln2_b': _L0_ffn_in['ln2_b'], 'L0_ffn_Wq': _L0_ffn_in['Wq'], 'L0_ffn_Wk': _L0_ffn_in['Wk'], 'L0_ffn_Wv': _L0_ffn_in['Wv'], 'L0_ffn_Wo': _L0_ffn_in['Wo'], 'L0_ffn_Wg': _L0_ffn_in['Wg'], 'L0_ffn_W1': _L0_ffn_in['W1'], 'L0_ffn_b1': _L0_ffn_in['b1'], 'L0_ffn_W2': _L0_ffn_in['W2'], 'L0_ffn_b2': _L0_ffn_in['b2'], 'L1_xattn_Wq': _L1_xattn_in['Wq'], 'L1_xattn_bq': _L1_xattn_in['bq'], 'L1_xattn_Wk': _L1_xattn_in['Wk'], 'L1_xattn_bk': _L1_xattn_in['bk'], 'L1_xattn_Wv': _L1_xattn_in['Wv'], 'L1_xattn_bv': _L1_xattn_in['bv'], 'L1_xattn_Wo': _L1_xattn_in['Wo'], 'L1_xattn_bo': _L1_xattn_in['bo'], 'L1_attn_W_Q': _L1_attn_in['W_Q'], 'L1_attn_W_K': _L1_attn_in['W_K'], 'L1_attn_W_V': _L1_attn_in['W_V'], 'L1_attn_W_O': _L1_attn_in['W_O'], 'L1_ffn_k0': _L1_ffn_in['k0'], 'L1_ffn_k1': _L1_ffn_in['k1'], 'L1_ffn_k2': _L1_ffn_in['k2'], 'L1_ffn_s0': _L1_ffn_in['s0'], 'L1_ffn_s1': _L1_ffn_in['s1'], 'L1_ffn_s2': _L1_ffn_in['s2']}

def reference(x, ctx_1024, mask_BxS2_ik0, L0_xattn_ln_l_w, L0_xattn_ln_l_b, L0_xattn_ln_c_w, L0_xattn_ln_c_b, L0_xattn_Wq, L0_xattn_Wkv, L0_xattn_Wo, L0_xattn_bo, L0_attn_wq, L0_attn_bq, L0_attn_wqc, L0_attn_bqc, L0_attn_wqr, L0_attn_bqr, L0_attn_wkv, L0_attn_bkv, L0_attn_wkr, L0_attn_bkr, L0_attn_wkc, L0_attn_bkc, L0_attn_wv, L0_attn_bv, L0_attn_wo, L0_attn_bo, L0_ffn_ln1_g, L0_ffn_ln1_b, L0_ffn_ln2_g, L0_ffn_ln2_b, L0_ffn_Wq, L0_ffn_Wk, L0_ffn_Wv, L0_ffn_Wo, L0_ffn_Wg, L0_ffn_W1, L0_ffn_b1, L0_ffn_W2, L0_ffn_b2, L1_xattn_Wq, L1_xattn_bq, L1_xattn_Wk, L1_xattn_bk, L1_xattn_Wv, L1_xattn_bv, L1_xattn_Wo, L1_xattn_bo, L1_attn_W_Q, L1_attn_W_K, L1_attn_W_V, L1_attn_W_O, L1_ffn_k0, L1_ffn_k1, L1_ffn_k2, L1_ffn_s0, L1_ffn_s1, L1_ffn_s2):
    import jax
    import jax.numpy as jnp

    def _L0_xattn_ref(latents, context, ln_l_w, ln_l_b, ln_c_w, ln_c_b, Wq, Wkv, Wo, bo):
        import jax, jax.numpy as jnp
        import numpy as np
        DIM = 256
        H = 16
        D = 64
        INNER = H * D
        EPS = 1e-05

        def layernorm(x, w, b):
            mu = jnp.mean(x, axis=-1, keepdims=True)
            var = jnp.var(x, axis=-1, keepdims=True)
            return (x - mu) * jax.lax.rsqrt(var + EPS) * w + b
        b, n, _ = latents.shape
        s = context.shape[1]
        lat = layernorm(latents, ln_l_w, ln_l_b)
        ctx = layernorm(context, ln_c_w, ln_c_b)
        q = (lat @ Wq).reshape(b, n, H, D).transpose(0, 2, 1, 3)
        kv = ctx @ Wkv
        k, v = jnp.split(kv, 2, axis=-1)
        k = k.reshape(b, s, H, D).transpose(0, 2, 1, 3)
        v = v.reshape(b, s, H, D).transpose(0, 2, 1, 3)
        scale = D ** (-0.5)
        attn = jnp.einsum('bhnd,bhsd->bhns', q, k) * scale
        attn = jnp.clip(attn, -11.0, 11.0)
        attn = jax.nn.softmax(attn, axis=-1)
        out = jnp.einsum('bhns,bhsd->bhnd', attn, v)
        out = out.transpose(0, 2, 1, 3).reshape(b, n, INNER)
        return out @ Wo + bo

    def _L0_attn_ref(x, wq, bq, wqc, bqc, wqr, bqr, wkv, bkv, wkr, bkr, wkc, bkc, wv, bv, wo, bo):
        import jax, jax.numpy as jnp
        import numpy as np
        import math
        B, S, E = (2, 512, 256)
        H, DC, DR = (16, 64, 128)
        HD = E // H

        def _linear_params(key, din, dout):
            k1, k2 = jax.random.split(key)
            bound = 1.0 / math.sqrt(din)
            w = jax.random.uniform(k1, (din, dout), minval=-bound, maxval=bound, dtype=jnp.float32)
            b = jax.random.uniform(k2, (dout,), minval=-bound, maxval=bound, dtype=jnp.float32)
            return (w, b)

        def _gelu(x):
            return jax.nn.gelu(x, approximate=False)

        def _rope_cos_sin(seq_len, d_rope):
            inv_freq = 1.0 / 10000.0 ** (jnp.arange(0, d_rope, 2, dtype=jnp.float32) / d_rope)
            t = jnp.arange(seq_len, dtype=jnp.float32)
            freqs = t[:, None] * inv_freq[None, :]
            emb = jnp.concatenate([freqs, freqs], axis=-1)
            return (jnp.cos(emb), jnp.sin(emb))

        def _apply_rope(x, cos, sin):
            d = x.shape[-1]
            x1, x2 = (x[..., :d // 2], x[..., d // 2:])
            rot = jnp.concatenate([-x2, x1], axis=-1)
            return x * cos + rot * sin
        b, s, _ = x.shape
        cq = _gelu(x @ wq + bq)
        q_c = cq @ wqc + bqc
        q_r = x @ wqr + bqr
        ckv = _gelu(x @ wkv + bkv)
        k_r = x @ wkr + bkr
        k_c = ckv @ wkc + bkc
        v = (ckv @ wv + bv).reshape(b, s, H, HD).transpose(0, 2, 1, 3)
        cos, sin = _rope_cos_sin(s, DR)
        q_r = _apply_rope(q_r, cos, sin)
        k_r = _apply_rope(k_r, cos, sin)
        q = _gelu(jnp.concatenate([q_c, q_r], axis=-1)).reshape(b, s, H, HD).transpose(0, 2, 1, 3)
        k = _gelu(jnp.concatenate([k_c, k_r], axis=-1)).reshape(b, s, H, HD).transpose(0, 2, 1, 3)
        scale = 1.0 / math.sqrt(HD)
        scores = jnp.einsum('bhqd,bhkd->bhqk', q, k) * scale
        causal = jnp.triu(jnp.ones((s, s), dtype=bool), k=1)
        scores = jnp.where(causal[None, None], -jnp.inf, scores)
        attn = jax.nn.softmax(scores, axis=-1)
        out = jnp.einsum('bhqk,bhkd->bhqd', attn, v)
        out = out.transpose(0, 2, 1, 3).reshape(b, s, E)
        return out @ wo + bo

    def _L0_ffn_ref(x, ln1_g, ln1_b, ln2_g, ln2_b, Wq, Wk, Wv, Wo, Wg, W1, b1, W2, b2):
        import jax, jax.numpy as jnp
        import numpy as np
        B, S, D, H, E, F, K = (2, 256, 256, 16, 8, 1024, 2)
        EPS = 1e-05

        def _layernorm(x, g, b):
            mu = jnp.mean(x, axis=-1, keepdims=True)
            var = jnp.mean(jnp.square(x - mu), axis=-1, keepdims=True)
            return (x - mu) * jax.lax.rsqrt(var + EPS) * g + b
        Bb, Ss, Dd = x.shape
        Dh = Dd // H
        h = _layernorm(x, ln1_g, ln1_b)
        q = (h @ Wq).reshape(Bb, Ss, H, Dh)
        k = (h @ Wk).reshape(Bb, Ss, H, Dh)
        v = (h @ Wv).reshape(Bb, Ss, H, Dh)
        scores = jnp.einsum('bqhd,bkhd->bhqk', q, k) / jnp.sqrt(jnp.float32(Dh))
        attn = jax.nn.softmax(scores, axis=-1)
        ctx = jnp.einsum('bhqk,bkhd->bqhd', attn, v).reshape(Bb, Ss, Dd)
        x = x + ctx @ Wo
        m = _layernorm(x, ln2_g, ln2_b)
        xt = m.reshape(-1, Dd)
        T = xt.shape[0]
        probs = jax.nn.softmax(xt @ Wg, axis=-1)
        wts, idx = jax.lax.top_k(probs, K)
        wts = wts / jnp.sum(wts, axis=-1, keepdims=True)
        h1 = jax.nn.gelu(jnp.einsum('td,edf->etf', xt, W1) + b1[:, None, :])
        ye = jnp.einsum('etf,efd->etd', h1, W2) + b2[:, None, :]
        sel = ye[idx, jnp.arange(T)[:, None], :]
        moe_out = jnp.sum(wts[..., None] * sel, axis=1).reshape(Bb, Ss, Dd)
        return x + moe_out

    def _L1_xattn_ref(query, key, value, key_padding_mask, Wq, bq, Wk, bk, Wv, bv, Wo, bo):
        import jax, jax.numpy as jnp
        import numpy as np
        H = 256
        NH = 16
        HD = H // NH
        B, Sq, _ = query.shape
        Sk = key.shape[1]
        scaling = HD ** (-0.5)
        q = (query @ Wq + bq).reshape(B, Sq, NH, HD).transpose(0, 2, 1, 3)
        k = (key @ Wk + bk).reshape(B, Sk, NH, HD).transpose(0, 2, 1, 3)
        v = (value @ Wv + bv).reshape(B, Sk, NH, HD).transpose(0, 2, 1, 3)
        scores = jnp.einsum('bhqd,bhkd->bhqk', q, k) * scaling
        scores = jnp.where((key_padding_mask == 0)[:, None, None, :], -jnp.inf, scores)
        attn = jax.nn.softmax(scores, axis=-1)
        out = jnp.einsum('bhqk,bhkd->bhqd', attn, v)
        out = out.transpose(0, 2, 1, 3).reshape(B, Sq, H)
        return out @ Wo + bo

    def _L1_attn_ref(x, W_Q, W_K, W_V, W_O):
        import jax, jax.numpy as jnp
        import numpy as np
        D_MODEL = 256
        NUM_HEADS = 16
        B, S = (1, 1024)
        Bx, Sx, Dm = x.shape
        H = NUM_HEADS
        d_attn = Dm // H
        Q = x @ W_Q.T
        K = x @ W_K.T
        V = x @ W_V.T
        Q = Q.reshape(Bx, Sx, H, d_attn).transpose(0, 2, 1, 3)
        K = K.reshape(Bx, Sx, H, d_attn).transpose(0, 2, 1, 3)
        V = V.reshape(Bx, Sx, H, d_attn).transpose(0, 2, 1, 3)
        scale = 1.0 / jnp.sqrt(jnp.asarray(d_attn, dtype=x.dtype))
        attn = jnp.einsum('bhqd,bhkd->bhqk', Q, K) * scale
        causal = jnp.tril(jnp.ones((Sx, Sx), dtype=bool))
        attn = jnp.where(causal, attn, jnp.asarray(-jnp.inf, dtype=attn.dtype))
        probs = jax.nn.softmax(attn, axis=-1)
        y = jnp.einsum('bhqk,bhkd->bhqd', probs, V)
        y = y.transpose(0, 2, 1, 3).reshape(Bx, Sx, Dm)
        return y @ W_O.T

    def _L1_ffn_ref(x, k0, k1, k2, s0, s1, s2):
        import jax, jax.numpy as jnp
        import numpy as np
        import math
        D_IN = 256
        FEATURES = (1024, 1024, 256)
        BATCH, SEQ = (8, 512)

        def _conn_dense(kernel_bool, x):
            w = jnp.where(kernel_bool, jnp.float32(1.0), jnp.float32(-1.0))
            return x @ w
        h = jnp.concatenate([x, -x], axis=-1)
        h = s0 * _conn_dense(k0, h)
        h = jax.nn.relu(h) * 2
        h = s1 * _conn_dense(k1, h)
        h = jax.nn.relu(h) * 2
        h = s2 * _conn_dense(k2, h)
        return h
    x = x + _L0_xattn_ref(_layernorm(x, axis=-1), ctx_1024, L0_xattn_ln_l_w, L0_xattn_ln_l_b, L0_xattn_ln_c_w, L0_xattn_ln_c_b, L0_xattn_Wq, L0_xattn_Wkv, L0_xattn_Wo, L0_xattn_bo)
    x = x + _L0_attn_ref(_layernorm(x, axis=-1), L0_attn_wq, L0_attn_bq, L0_attn_wqc, L0_attn_bqc, L0_attn_wqr, L0_attn_bqr, L0_attn_wkv, L0_attn_bkv, L0_attn_wkr, L0_attn_bkr, L0_attn_wkc, L0_attn_bkc, L0_attn_wv, L0_attn_bv, L0_attn_wo, L0_attn_bo)
    x = x + _L0_ffn_ref(_layernorm(x, axis=-1), L0_ffn_ln1_g, L0_ffn_ln1_b, L0_ffn_ln2_g, L0_ffn_ln2_b, L0_ffn_Wq, L0_ffn_Wk, L0_ffn_Wv, L0_ffn_Wo, L0_ffn_Wg, L0_ffn_W1, L0_ffn_b1, L0_ffn_W2, L0_ffn_b2)
    x = x + _L1_xattn_ref(_layernorm(x, axis=-1), ctx_1024, ctx_1024, mask_BxS2_ik0, L1_xattn_Wq, L1_xattn_bq, L1_xattn_Wk, L1_xattn_bk, L1_xattn_Wv, L1_xattn_bv, L1_xattn_Wo, L1_xattn_bo)
    x = x + _L1_attn_ref(_layernorm(x, axis=-1), L1_attn_W_Q, L1_attn_W_K, L1_attn_W_V, L1_attn_W_O)
    x = x + _L1_ffn_ref(_layernorm(x, axis=-1), L1_ffn_k0, L1_ffn_k1, L1_ffn_k2, L1_ffn_s0, L1_ffn_s1, L1_ffn_s2)
    return x

_drawn_inputs = setup_inputs


def setup_inputs(seed=0):
    import zlib

    import numpy as np

    out = dict(_drawn_inputs(seed))
    spreads = {'L0_xattn_ln_l_w': (1.0, 0.2),
     'L0_xattn_ln_l_b': (0.0, 0.456),
     'L0_xattn_ln_c_w': (1.0, 0.2),
     'L0_xattn_ln_c_b': (0.0, 0.1),
     'L0_xattn_bo': (0.0, 0.1),
     'L0_ffn_ln1_g': (1.0, 0.6),
     'L0_ffn_ln1_b': (0.0, 0.8),
     'L0_ffn_ln2_g': (1.0, 0.6),
     'L0_ffn_ln2_b': (0.0, 0.474),
     'L0_ffn_b1': (0.0, 0.685),
     'L0_ffn_b2': (0.0, 0.1),
     'L1_xattn_bq': (0.0, 0.62),
     'L1_xattn_bk': (0.0, 2.0),
     'L1_xattn_bv': (0.0, 0.1),
     'L1_xattn_bo': (0.0, 0.1)}
    factors = {'L0_attn_wq': 8.0,
     'L0_attn_bq': 40.247,
     'L0_attn_wqc': 8.0,
     'L0_attn_bqc': 49.631,
     'L0_attn_wqr': 8.0,
     'L0_attn_bqr': 40.435,
     'L0_attn_bkv': 8.0,
     'L0_attn_wkr': 8.0,
     'L0_attn_bkr': 41.576,
     'L0_attn_wkc': 8.0,
     'L0_attn_bkc': 23.328,
     'L0_ffn_Wq': 8.0,
     'L0_ffn_Wk': 8.0}
    for name, (base, spread) in spreads.items():
        noise = np.random.default_rng([zlib.crc32(name.encode()), seed]).standard_normal(out[name].shape)
        drawn = base * np.exp(spread * noise) if base else spread * noise
        out[name] = jnp.asarray(drawn.astype(out[name].dtype))
    for name, factor in factors.items():
        out[name] = (out[name] * factor).astype(out[name].dtype)
    return out
```

```python
from contextlib import ExitStack

import numpy as np

import concourse.bass as bass
from concourse import mybir

F32 = mybir.dt.float32
F32R = mybir.dt.float32r
BF16 = mybir.dt.bfloat16
U8 = mybir.dt.uint8
U32 = mybir.dt.uint32
I32 = mybir.dt.int32
ALU = mybir.AluOpType
ACT = mybir.ActivationFunctionType
AX_X = mybir.AxisListType.X

P = 128
B, N, D, S = 16, 64, 256, 256
T = B * N // P
KD = D // P
H = 16
INNER = 1024
E, F = 8, 1024
FT = F // P
NEG = -1e30
EPS = 1e-5

C_IDENT, C_HEAD, C_PAR, C_CAUSAL, C_COS, C_SIN, C_IOTA, C_ROW0 = np.cumsum([0, 128, 8, 2, 64, 128, 128, 8])
C_ALL = C_ROW0 + 128
COLS = {}
for _name, _k in [("ln_l_w", 2), ("ln_l_b", 2), ("ln_c_w", 2), ("ln_c_b", 2), ("bqkv", 1), ("bqc", 1), ("bkc", 1),
                  ("bqr", 1), ("bqs", 1), ("bkr", 1), ("bks", 1), ("bv0", 2), ("ln1_g", 2), ("ln1_b", 2), ("ln2_g", 2), ("ln2_b", 2),
                  ("xbq", 2), ("xbk", 2), ("xbv", 2), ("b1", E * FT), ("s0", 1), ("s1", 1), ("s2", 1)]:
    COLS[_name] = (sum(k for _, k in COLS.values()), _k)
COL_ALL = sum(k for _, k in COLS.values())


def build(nc, a, out):
    with ExitStack() as ctx:
        at = [(nc.sbuf_base + 31) // 32 * 32]

        def sb(name, shape, dt=F32):
            size = int(np.prod(shape[1:])) * (1 if dt == U8 else 2 if dt == BF16 else 4)
            here = at[0]
            at[0] += (size + 31) // 32 * 32
            assert at[0] <= nc.sbuf_usable_end, (name, at[0])
            return nc.alloc_sbuf_tensor_at(name, shape, dt, offset=here)

        def sem(name):
            return ctx.enter_context(nc.semaphore(name))

        ps = ctx.enter_context(nc.psum_tensor("ps", [P, 8, 512], F32))

        x = sb("x_res", [P, T, D])
        cst = sb("cst", [P, C_ALL])
        col = sb("col", [P, COL_ALL])
        rows = sb("rows", [P, 3, D])
        ident = cst[:, C_IDENT:C_IDENT + P]
        identb = sb("identb", [P, P], BF16)
        causalb = sb("causalb", [P, N], BF16)
        row0b = sb("row0b", [P, P], BF16)
        padneg = sb("padneg", [P, B, S], BF16)
        head_of = cst[:, C_HEAD:C_HEAD + 8]
        par_of = cst[:, C_PAR:C_PAR + 2]
        w_sq = [sb(f"w_sq{i}", [P, KD, 4, D]) for i in range(2)]
        w_mla = sb("w_mla", [P, KD, 128 + 4 * 128])
        w_mlac = sb("w_mlac", [P, 128 + 128 + D])
        w_mlao = sb("w_mlao", [P, KD, D])
        wg = sb("wg", [P, KD, P])
        ln_st = sb("ln_st", [P, 5, 6])
        ln_mv = sb("ln_mv", [P, 5, 2])
        ln_ve = sb("ln_ve", [P, 5])
        ln_rs = sb("ln_rs", [P, 5])
        neghalf = sb("neghalf", [P, 5])
        eps = sb("eps", [P, 5])

        def vec(name, i=0):
            at0, _ = COLS[name]
            return col[:, at0 + i:at0 + i + 1]

        mark = at[0]

        def cross_buffers(tag, kg, vw, probs_at=None):
            g = {}
            g["cin"] = sb(tag + "cin", [P, 2, 4, D])
            g["cT"] = sb(tag + "cT", [P, KD, 512])
            g["lat"] = sb(tag + "lat", [P, D])
            g["latT"] = sb(tag + "latT", [P, KD, P])
            g["qbd"] = [sb(f"{tag}qbd{i}", [P, 2, 8, P]) for i in range(2)]
            g["kT"] = [sb(f"{tag}kT{i}", [P, kg, 512]) for i in range(2)]
            g["v"] = [sb(f"{tag}v{i}", [P, 4, vw]) for i in range(2)]
            after, at[0] = at[0], at[0] if probs_at is None else probs_at
            g["p"] = [sb(f"{tag}p{i}", [P, 4, S]) for i in range(2)]
            g["pT"] = [sb(f"{tag}pT{i}", [P, 8, P]) for i in range(2)]
            at[0] = at[0] if probs_at is None else after
            g["attT"] = sb(tag + "attT", [P, kg, P])
            g["sum"] = sb(tag + "sum", [P, 2, 4])
            g["rinv"] = sb(tag + "rinv", [P, 2, 4])
            g["nmax"] = sb(tag + "nmax", [P, 2, 4])
            return g

        X0 = cross_buffers("x0", 8, INNER)
        X0["cn"] = sb("x0cn", [P, 4, D])
        X0["wq"] = sb("x0wq", [P, KD, INNER])
        X0["wkv"] = sb("x0wkv", [P, KD, 2 * INNER])
        X0["wo"] = sb("x0wo", [P, 8, D])

        at[0] = mark
        h = sb("h", [P, D])
        hT = sb("hT", [P, KD, P])
        qT = sb("qT", [P, KD, P])
        kTs = sb("kTs", [P, KD, P])
        cqkvT = sb("cqkvT", [P, P])
        rope = sb("rope", [P, 4, P])
        h1_at = at[0]
        kbd = sb("kbd", [P, KD, 2, 8, N])
        pr = sb("pr", [P, H, N])
        prT = sb("prT", [P, 8, P])
        vbd = [sb(f"vbd{i}", [P, 2, 8, 2, 16]) for i in range(2)]
        smax = sb("smax", [P, H])
        ssum = sb("ssum", [P, H])
        srinv = sb("srinv", [P, H])
        sattT = sb("sattT", [P, KD, P])
        u = sb("u", [P, T, D])
        ffw0 = sb("ffw0", [P, KD, F], F32R)
        ffw1 = sb("ffw1", [P, FT, F], F32R)
        ffw2 = sb("ffw2", [P, FT, D], F32R)
        ffraw = sb("ffraw", [P, 2, 2, F], U8)
        ffs = sb("ffs", [P, 2])
        xw = sb("xw", [P, KD, 4, D])
        mark2 = at[0]
        mT = sb("mT", [P, KD, T * P])
        ew1 = [sb(f"ew1_{i}", [P, KD, F]) for i in range(2)]
        ew2 = [sb(f"ew2_{i}", [P, FT, D]) for i in range(2)]
        h1_at0 = at[0]
        h1 = [sb("h1_0", [P, FT, 512]), nc.alloc_sbuf_tensor_at("h1_1", [P, FT, 512], F32, offset=h1_at)]
        logit = sb("logit", [P, T, E])
        top = sb("top", [P, T, 8])
        topi = sb("topi", [P, T, 8], U32)
        topf = sb("topf", [P, T, 2])
        gexp = sb("gexp", [P, T])
        gw = sb("gw", [P, T, 4])
        gsel = sb("gsel", [P, T, 2, E])
        gate = sb("gate", [P, T, P])
        b2 = sb("b2", [P, D])
        gate_T = h1[0][:, 0:2, :].rearrange("p a n -> p (a n)")
        maskrow = nc.alloc_sbuf_tensor_at("maskrow", [P, B, S], I32, offset=h1_at0)
        at[0] = mark2
        X1 = cross_buffers("x1", KD, D, h1_at)
        X1["qs"] = sb("x1qs", [P, KD, P])
        X1["pv0"] = sb("x1pv0", [P, N])
        X1["wq"], X1["wkv"], X1["wo"] = xw[:, :, 0, :], None, xw[:, :, 3, :]
        at[0] = mark2
        fxT = [sb(f"fxT{i}", [P, KD, 512], F32R) for i in range(2)]
        fh = [sb(f"fh{i}", [P, 512]) for i in range(2)]
        f0 = [sb(f"f0_{i}", [P, FT, 512], F32R) for i in range(2)]
        f1 = [sb("f1_0", [P, FT, 512], F32R), nc.alloc_sbuf_tensor_at("f1_1", [P, FT, 512], F32R, offset=h1_at)]

        ld = {k: sem("ld_" + k) for k in ("x", "const", "x0w", "mla", "sq0", "sq1", "xw", "pad", "wg", "b2")}
        ld_ctx = [[sem(f"ld_ctx{l}{i}") for i in range(2)] for l in range(2)]
        ld_e = [sem(f"ld_e{i}") for i in range(2)]
        ld_ff = [sem(f"ld_ff{i}") for i in range(2)]
        setup = sem("setup")
        pool_setup = sem("pool_setup")
        ln_stats, ln_aggr, ln_eps, ln_rstd = (sem(k) for k in ("ln_stats", "ln_aggr", "ln_eps", "ln_rstd"))
        ln_done = sem("ln_done")
        dve_go, act_go = sem("dve_go"), sem("act_go")
        stored = sem("stored")

        block = ctx.enter_context(nc.Block())

        def tiles(e, step):
            with e.Fori(0, T // 2 - 1) as i:
                for s in range(2):
                    step(2 * i + s, s, True)
            step(T - 2, 0, True)
            step(T - 1, 1, False)

        def ln_statistics(dve, srcs, idx):
            dve.sem_inc(dve_go, 1)
            for i, src in enumerate(srcs):
                last = nc.vector.bn_stats(ln_st[:, i, :], src)
            last.then_inc(ln_stats, 1)
            dve.wait_ge(ln_stats, idx + 1)
            dve.sem_inc(dve_go, 1)
            for i in range(len(srcs)):
                last = nc.vector.bn_aggr(ln_mv[:, i, :], ln_st[:, i, :])
            last.then_inc(ln_aggr, 1)

        def ln_rstd_pool(pool, k, idx):
            pool.wait_ge(ln_aggr, idx + 1)
            nc.gpsimd.tensor_tensor(ln_ve[:, 0:k], ln_mv[:, 0:k, 1], eps[:, 0:k], ALU.add).then_inc(ln_eps, 1)
            pool.wait_ge(ln_eps, idx + 1)
            nc.gpsimd.tensor_tensor(ln_rs[:, 0:k], ln_ve[:, 0:k], neghalf[:, 0:k], ALU.pow).then_inc(ln_rstd, 1)

        def ln_apply(dve, srcs, dsts, idx):
            dve.wait_ge(ln_rstd, idx + 1)
            for i, (src, dst) in enumerate(zip(srcs, dsts)):
                last = nc.vector.tensor_scalar(dst, src, ln_mv[:, i, 0:1], ln_rs[:, i:i + 1], ALU.subtract, ALU.mult)
            last.then_inc(ln_done, 1)

        XS, XF, XT, XV, XY = 0, (2, 3), (4, 5), 6, 7

        def cross(l):
            class c:
                fill_done0 = sem(f"x{l}_fill_done0")
                fill_done1 = sem(f"x{l}_fill_done1")
                fill_free0 = sem(f"x{l}_fill_free0")
                fill_free1 = sem(f"x{l}_fill_free1")
                s_done = sem(f"x{l}_s_done")
                s_free = sem(f"x{l}_s_free")
                max_done = sem(f"x{l}_max_done")
                clip_done = sem(f"x{l}_clip_done")
                exp_done = sem(f"x{l}_exp_done")
                rinv_done = sem(f"x{l}_rinv_done")
                norm_done = sem(f"x{l}_norm_done")
                pT_done0 = sem(f"x{l}_pT_done0")
                pT_done1 = sem(f"x{l}_pT_done1")
                pT_free0 = sem(f"x{l}_pT_free0")
                pT_free1 = sem(f"x{l}_pT_free1")
                p_free = sem(f"x{l}_p_free")
                pv_done = sem(f"x{l}_pv_done")
                pv0_done = sem(f"x{l}_pv0_done")
                pv_free = sem(f"x{l}_pv_free")
                y_done = sem(f"x{l}_y_done")
                y_free = sem(f"x{l}_y_free")
                x_done = sem(f"x{l}_x_done")
                q_spread = sem(f"x{l}_q_spread")

            c.l, c.g = l, (X0, X1)[l]
            c.fills = (["cT"] * 2 + ["lat"] * 2 + ["k"] * 8 + ["v"] * 8 + ["q"] * 2) if l == 0 else \
                ["cT", "cT", "lat", "lat", "k", "k", "v", "v", "q", "q"]
            c.groups = ((4, 8), (8, 12), (12, 16), (16, 22)) if l == 0 else ((4, 6), (6, 8), (8, 10), (10, 10))
            c.per = len(c.fills) // 2
            c.first = {k: c.fills.index(k) for k in ("cT", "lat", "k", "v", "q")}
            c.kg = 8 if l == 0 else KD
            c.fill_done, c.fill_free = (c.fill_done0, c.fill_done1), (c.fill_free0, c.fill_free1)
            c.pT_done, c.pT_free = (c.pT_done0, c.pT_done1), (c.pT_free0, c.pT_free1)
            return c

        X = [cross(0), cross(1)]

        LN_BASE = {"x0": 0, "mla": 2 * T, "ffn": 3 * T, "moe": 5 * T, "x1": 6 * T, "attn": 7 * T, "mlp": 8 * T}
        LN_COUNT = 9 * T

        def pe_cross(pe, c):
            g, l = c.g, c.l

            def fill(t, s, j):
                kind, i, bank, m = c.fills[j], j - c.first[c.fills[j]], j % 2, c.per * t + j // 2
                dst = ps[:, XF[bank], :]
                if j == 0:
                    if l == 0:
                        pe.wait_ge(ln_done, LN_BASE["x0"] + 2 * t + 2)
                    else:
                        pe.wait_ge(ld_ctx[1][s], 8 * (t - s) + 16)
                        pe.wait_ge(ln_done, LN_BASE["x1"] + t + 1)
                if kind == "k" and i == 0:
                    pe.wait_ge(c.fill_free[1], c.per * t + 2)
                pe.wait_ge(c.fill_free[bank], m + 1)
                if kind == "cT":
                    src = g["cn"] if l == 0 else g["cin"][:, s]
                    for tok in range(4):
                        last = nc.tensor.transpose(dst[:, tok * P:tok * P + P], src[:, tok, i * P:i * P + P], ident)
                elif kind == "lat":
                    last = nc.tensor.transpose(dst[:, 0:P], g["lat"][:, i * P:i * P + P], ident)
                elif kind == "k":
                    for k in range(KD):
                        w = g["wkv"][:, k, i * P:i * P + P] if l == 0 else xw[:, k, 1, i * P:i * P + P]
                        last = nc.tensor.matmul(dst, w, g["cT"][:, k, :], start=(k == 0), stop=(k == KD - 1))
                elif kind == "v":
                    if l == 0:
                        tok, half = i // 2, i % 2
                        for k in range(KD):
                            last = nc.tensor.matmul(dst, g["cT"][:, k, tok * P:tok * P + P],
                                                    g["wkv"][:, k, INNER + half * 512:INNER + half * 512 + 512],
                                                    start=(k == 0), stop=(k == KD - 1))
                    else:
                        for tok in (2 * i, 2 * i + 1):
                            for k in range(KD):
                                last = nc.tensor.matmul(dst[:, (tok % 2) * D:(tok % 2) * D + D], g["cT"][:, k, tok * P:tok * P + P],
                                                        xw[:, k, 2, :], start=(k == 0), stop=(k == KD - 1))
                else:
                    if i == 0:
                        pe.wait_ge(c.fill_free[1], c.per * t + 3)
                    for j4 in range(4 if l == 0 else 1):
                        grp = 4 * i + j4 if l == 0 else i
                        for k in range(KD):
                            last = nc.tensor.matmul(dst[:, j4 * P:j4 * P + P], g["wq"][:, k, grp * P:grp * P + P], g["latT"][:, k, :],
                                                    start=(k == 0), stop=(k == KD - 1))
                last.then_inc(c.fill_done[bank], 1)

            def scores(t, s, un):
                n, b, hf = 4 * t + un, un // 2, un % 2
                if un == 0:
                    for bank in range(2):
                        pe.wait_ge(c.fill_free[bank], c.per * (t + 1) + 1)
                    if l == 1:
                        pe.wait_ge(c.q_spread, 2 * t + 2)
                pe.wait_ge(c.s_free, n + 1)
                if l == 1:
                    for two in range(2):
                        nc.tensor.matmul(ps[:, XS + two, :], row0b[:, :],
                                         pad2(t, b), start=True, stop=False, skip_group_check=True)
                for j in range(4):
                    p = 4 * hf + j
                    last = nc.tensor.matmul(ps[:, XS + j // 2, (j % 2) * S:(j % 2) * S + S], g["qbd"][s][:, b, p, :],
                                            g["kT"][s][:, p if l == 0 else hf, b * S:b * S + S],
                                            start=(l == 0), stop=True, skip_group_check=True)
                last.then_inc(c.s_done, 1)

            def pad2(t, b):
                one = padneg[:, bass.ds(2 * t + b, 1), :]
                return one.broadcast_to((P, 2, S))

            def transposed(t, un):
                n = 4 * t + un
                pe.wait_ge(c.norm_done, n + 1)
                for bank in range(2):
                    pe.wait_ge(c.pT_free[bank], n + 1)
                    for i in range(4):
                        j, kt = 2 * bank + i // 2, i % 2
                        last = nc.tensor.transpose(ps[:, XT[bank], i * P:i * P + P], g["p"][un % 2][:, j, kt * P:kt * P + P], ident)
                    last.then_inc(c.pT_done[bank], 1)

            def values(t, s, un):
                n, b, hf = 4 * t + un, un // 2, un % 2
                for bank in range(2):
                    pe.wait_ge(c.pT_free[bank], n + 2)
                pe.wait_ge(c.pv_free, n + 1)
                for j in range(4):
                    p = 4 * hf + j
                    for kt in range(2):
                        if l == 0:
                            dst, w = ps[:, XV, j * P:j * P + P], g["v"][s][:, 2 * b + kt, p * P:p * P + P]
                        else:
                            dst, w = ps[32 * j:32 * j + 32, XV, 0:P], g["v"][s][:, 2 * b + kt, p * 32:p * 32 + 32]
                        last = nc.tensor.matmul(dst, w, g["pT"][un % 2][:, 2 * j + kt, :], start=(kt == 0), stop=(kt == 1))
                last.then_inc(c.pv_done, 1)

            def project(t):
                pe.wait_ge(c.y_free, t + 1)
                pe.wait_ge(c.pv_free, 4 * t + 5)
                for k in range(c.kg):
                    last = nc.tensor.matmul(ps[:, XY, 0:D], g["attT"][:, k, :], g["wo"][:, k, :], start=(k == 0), stop=(k == c.kg - 1))
                last.then_inc(c.y_done, 1)

            pe.wait_ge(ld["x0w" if l == 0 else "xw"], 48 if l == 0 else 64)
            if l == 1:
                pe.wait_ge(pool_setup, 7)
            for j in range(len(c.fills)):
                fill(0, 0, j)

            def step(t, s, nxt):
                scores(t, s, 0)
                if nxt:
                    for j in range(4):
                        fill(t + 1, 1 - s, j)
                for un in range(4):
                    if nxt:
                        for j in range(*c.groups[un]):
                            fill(t + 1, 1 - s, j)
                    transposed(t, un)
                    if un < 3:
                        scores(t, s, un + 1)
                    values(t, s, un)
                project(t)

            tiles(pe, step)

        def evacuate(eng, c, t, s, j):
            g, l = c.g, c.l
            kind, i, bank, m = c.fills[j], j - c.first[c.fills[j]], j % 2, c.per * t + j // 2
            src = ps[:, XF[bank], :]

            def put(dst, src, scale=None, bias=None):
                if bank == 0:
                    if scale is None and bias is None:
                        return nc.scalar.activation(dst, src, ACT.Copy)
                    return nc.scalar.activation(dst, src, ACT.Identity, bias=bias, scale=1.0 if scale is None else scale)
                if scale is None and bias is None:
                    return nc.vector.tensor_copy(dst, src)
                if scale is None:
                    return nc.vector.tensor_scalar(dst, src, bias, None, ALU.add)
                return nc.vector.tensor_scalar(dst, src, scale, bias, ALU.mult, ALU.add)

            eng.wait_ge(c.fill_done[bank], m + 1)
            if kind == "cT":
                last = put(g["cT"][:, i, :], src, vec("ln_c_w", i), vec("ln_c_b", i)) if l == 0 else put(g["cT"][:, i, :], src)
            elif kind == "lat":
                last = put(g["latT"][:, i, :], src[:, 0:P], vec("ln_l_w", i), vec("ln_l_b", i)) if l == 0 else put(g["latT"][:, i, :], src[:, 0:P])
            elif kind == "k":
                last = put(g["kT"][s][:, i, :], src) if l == 0 else put(g["kT"][s][:, i, :], src, None, vec("xbk", i))
            elif kind == "v":
                if l == 0:
                    last = put(g["v"][s][:, i // 2, (i % 2) * 512:(i % 2) * 512 + 512], src)
                else:
                    last = put(g["v"][s][:, 2 * i:2 * i + 2, :], src)
            elif l == 0:
                for par in range(2):
                    r = slice(64 * par, 64 * par + 64)
                    last = put(g["qbd"][s][r, :, 4 * i:4 * i + 4, 64 * par:64 * par + 64].rearrange("p b j n -> p j b n"),
                               src[r, :].rearrange("p (j b n) -> p j b n", j=4, b=2))
            else:
                last = put(g["qs"][:, i, :], src[:, 0:P], None, vec("xbq", i))
            last.then_inc(c.fill_free[bank], 1)

        def act_cross(act, c):
            g, l = c.g, c.l

            def exps(t, un):
                n, slot = 4 * t + un, un % 2
                act.wait_ge(c.clip_done, n + 1)
                for j in range(4):
                    if l == 0:
                        last = nc.scalar.activation(g["p"][slot][:, j, :], g["p"][slot][:, j, :], ACT.Exp, scale=64.0 ** -0.5,
                                                    accum_out=g["sum"][:, slot, j:j + 1])
                    else:
                        if j == 0:
                            act.wait_ge(c.p_free, n + 1)
                        last = nc.scalar.activation(g["p"][slot][:, j, :], ps[:, XS + j // 2, (j % 2) * S:(j % 2) * S + S], ACT.Exp,
                                                    bias=g["nmax"][:, slot, j:j + 1], scale=0.25, accum_out=g["sum"][:, slot, j:j + 1])
                last.then_inc(c.exp_done, 1)

            def move_pT(t, un):
                n = 4 * t + un
                act.wait_ge(c.pT_done[0], n + 1)
                nc.scalar.activation(g["pT"][un % 2][:, 0:4, :], ps[:, XT[0], :], ACT.Copy).then_inc(c.pT_free[0], 1)

            act.sem_inc(c.fill_free[0], 1)
            act.sem_inc(c.pT_free[0], 1)
            for j in range(0, len(c.fills), 2):
                evacuate(act, c, 0, 0, j)

            def step(t, s, nxt):
                exps(t, 0)
                if nxt:
                    for j in (0, 2):
                        evacuate(act, c, t + 1, 1 - s, j)
                for un in range(4):
                    if nxt:
                        for j in range(c.groups[un][0], c.groups[un][1], 2):
                            evacuate(act, c, t + 1, 1 - s, j)
                    move_pT(t, un)
                    if un < 3:
                        exps(t, un + 1)

            tiles(act, step)

        def dve_cross(dve, c):
            g, l = c.g, c.l
            base = LN_BASE["x0" if l == 0 else "x1"]

            def norm(t, s):
                xt = x[:, bass.ds(t, 1), :].rearrange("p a d -> p (a d)")
                if l == 0:
                    dve.wait_ge(ld_ctx[0][s], 8 * (t - s) + 16)
                    srcs = [g["cin"][:, s, k, :] for k in range(4)] + [xt]
                    dsts = [g["cn"][:, k, :] for k in range(4)] + [g["lat"][:, :]]
                    ln_statistics(dve, srcs, base + 2 * t)
                    ln_apply(dve, srcs, dsts, base + 2 * t)
                    dve.wait_ge(ln_done, base + 2 * t + 1)
                    ln_statistics(dve, [g["lat"][:, :]], base + 2 * t + 1)
                    ln_apply(dve, [g["lat"][:, :]], [g["lat"][:, :]], base + 2 * t + 1)
                else:
                    ln_statistics(dve, [xt], base + t)
                    ln_apply(dve, [xt], [g["lat"][:, :]], base + t)

            def spread_q(t, s):
                for i in range(KD):
                    if i == 0:
                        dve.wait_ge(c.fill_free[0], c.per * (t + 1) + 1)
                        dve.wait_ge(c.fill_free[1], c.per * (t + 1) + 1)
                    q = g["qs"][:, i, :].rearrange("p (b n) -> p b n", b=2)
                    for b in range(2):
                        last = nc.vector.tensor_tensor(g["qbd"][s][:, b, 4 * i:4 * i + 4, :].rearrange("p j (a n) -> p (j a) n", a=2),
                                                q[:, b:b + 1, :].broadcast_to((P, 8, N)),
                                                head_of.rearrange("p (h o) -> p h o", o=1).broadcast_to((P, 8, N)), ALU.mult)
                    last.then_inc(c.q_spread, 1)

            def read_scores(t, un):
                n, slot = 4 * t + un, un % 2
                dve.wait_ge(c.s_done, n + 1)
                sc = ps[:, XS:XS + 2, :].rearrange("p a (j k) -> p (a j) k", j=2)
                if l == 0:
                    nc.vector.tensor_scalar(g["p"][slot][:, :, :], sc, 11.0 * 8.0, -11.0 * 8.0, ALU.min, ALU.max).then_inc(c.clip_done, 1)
                    dve.wait_ge(c.clip_done, n + 1)
                    dve.sem_inc(c.s_free, 1)
                else:
                    nc.vector.tensor_reduce(g["sum"][:, slot, :], sc, AX_X, ALU.max).then_inc(c.max_done, 1)
                    dve.wait_ge(c.max_done, n + 1)
                    nc.vector.tensor_scalar(g["nmax"][:, slot, :], g["sum"][:, slot, :], -0.25, None, ALU.mult).then_inc(c.clip_done, 1)

            def invert(t, un):
                n, slot = 4 * t + un, un % 2
                dve.wait_ge(c.exp_done, n + 1)
                if l == 1:
                    dve.sem_inc(c.s_free, 1)
                nc.vector.reciprocal(g["rinv"][:, slot, :], g["sum"][:, slot, :]).then_inc(c.rinv_done, 1)

            def move_pT(t, un):
                n = 4 * t + un
                dve.wait_ge(c.pT_done[1], n + 1)
                dve.sem_inc(c.p_free, 1)
                nc.vector.tensor_copy(g["pT"][un % 2][:, 4:8, :], ps[:, XT[1], :]).then_inc(c.pT_free[1], 1)

            def pick(t, un):
                n, b, hf = 4 * t + un, un // 2, un % 2
                dve.wait_ge(c.pv_done, n + 1)
                cols = slice(64 * b, 64 * b + 64)
                if l == 0:
                    for par in range(2):
                        r = slice(64 * par, 64 * par + 64)
                        last = nc.vector.tensor_copy(g["attT"][r, 4 * hf:4 * hf + 4, cols],
                                                     ps[r, XV, :].rearrange("p (j m) -> p j m", j=4)[:, :, 64 * par:64 * par + 64])
                else:
                    nc.vector.tensor_scalar(g["pv0"][:, :], ps[:, XV, 0:N], par_of[:, 0:1], vec("xbv", hf), ALU.mult, ALU.add).then_inc(c.pv0_done, 1)
                    dve.wait_ge(c.pv0_done, n + 1)
                    last = nc.vector.scalar_tensor_tensor(g["attT"][:, hf, cols], ps[:, XV, N:2 * N], par_of[:, 1:2], g["pv0"][:, :], ALU.mult, ALU.add)
                last.then_inc(c.pv_free, 1)

            def residual(t):
                xt = x[:, bass.ds(t, 1), :].rearrange("p a d -> p (a d)")
                dve.wait_ge(c.y_done, t + 1)
                nc.vector.tensor_tensor(xt, ps[:, XY, 0:D], xt, ALU.add).then_inc(c.y_free, 1)
                dve.wait_ge(c.y_free, t + 2)
                nc.vector.tensor_tensor(xt, xt, rows[:, 0 if l == 0 else 2, :], ALU.add).then_inc(c.x_done, 1)

            for k, v in ((c.fill_free[1], 1), (c.s_free, 1), (c.pT_free[1], 1), (c.pv_free, 1), (c.y_free, 1), (c.p_free, 2)):
                dve.sem_inc(k, v)
            if l == 0:
                for s in range(2):
                    nc.vector.memset(g["qbd"][s][:, :, :, :], 0.0).then_inc(c.q_spread, 1)
                dve.wait_ge(c.q_spread, 2)
            norm(0, 0)
            for j in range(1, len(c.fills), 2):
                evacuate(dve, c, 0, 0, j)
            if l == 1:
                spread_q(0, 0)
            dve.wait_ge(c.fill_done[0], 2)
            norm(1, 1)

            def step(t, s, nxt):
                read_scores(t, 0)
                if nxt:
                    for j in (1, 3):
                        evacuate(dve, c, t + 1, 1 - s, j)
                for un in range(4):
                    todo = list(range(c.groups[un][0] + 1, c.groups[un][1], 2)) if nxt else []
                    for j in todo[:1]:
                        evacuate(dve, c, t + 1, 1 - s, j)
                    invert(t, un)
                    for j in todo[1:]:
                        evacuate(dve, c, t + 1, 1 - s, j)
                    move_pT(t, un)
                    if un < 3:
                        read_scores(t, un + 1)
                    if l == 1 and nxt and un == 2:
                        spread_q(t + 1, 1 - s)
                    pick(t, un)
                residual(t)

            def full(t, s, nxt, more):
                step(t, s, nxt)
                if more:
                    dve.wait_ge(c.fill_done[0], c.per * (t + 1) + 2)
                    norm(t + 2, s)

            with dve.Fori(0, T // 2 - 1) as i:
                for s in range(2):
                    full(2 * i + s, s, True, True)
            full(T - 2, 0, True, False)
            full(T - 1, 1, False, False)

        def pool_cross(pool, c):
            g, l = c.g, c.l
            base = LN_BASE["x0" if l == 0 else "x1"]

            def norm(t):
                if l == 0:
                    ln_rstd_pool(pool, 5, base + 2 * t)
                    ln_rstd_pool(pool, 1, base + 2 * t + 1)
                else:
                    ln_rstd_pool(pool, 1, base + t)

            def scale_p(t, un):
                n, slot = 4 * t + un, un % 2
                pool.wait_ge(c.rinv_done, n + 1)
                nc.gpsimd.tensor_tensor(g["p"][slot][:, :, :], g["p"][slot][:, :, :],
                                        g["rinv"][:, slot, :].rearrange("p (j o) -> p j o", o=1).broadcast_to((P, 4, S)),
                                        ALU.mult).then_inc(c.norm_done, 1)

            norm(0)
            norm(1)
            with pool.Fori(0, T // 2 - 1) as i:
                for s in range(2):
                    t = 2 * i + s
                    for un in range(4):
                        scale_p(t, un)
                    norm(t + 2)
            for t in (T - 2, T - 1):
                for un in range(4):
                    scale_p(t, un)

        y_at = ctx_views(a["ctx_1024"])

        LAYERS = ("mla", "ffn", "attn")
        class SA:
            hT_ps = sem("sa_hT_ps")
            hT = sem("sa_hT")
            lat_ps = sem("sa_lat_ps")
            lat = sem("sa_lat")
            rope_ps = sem("sa_rope_ps")
            roped0 = sem("sa_roped0")
            roped1 = sem("sa_roped1")
            rope = sem("sa_rope")
            qk_ps = sem("sa_qk_ps")
            q_ps = sem("sa_q_ps")
            q = sem("sa_q")
            kv_ps = sem("sa_kv_ps")
            kbd = sem("sa_kbd")
            vbd = sem("sa_vbd")
            s_ps = sem("sa_s_ps")
            max = sem("sa_max")
            sub = sem("sa_sub")
            exp = sem("sa_exp")
            sum = sem("sa_sum")
            rinv = sem("sa_rinv")
            norm = sem("sa_norm")
            pT_ps = sem("sa_pT_ps")
            pT = sem("sa_pT")
            att_ps = sem("sa_att_ps")
            att = sem("sa_att")
            y_ps = sem("sa_y_ps")
            y_free = sem("sa_y_free")
            x_done = sem("sa_x_done")

        def pe_self(pe, L):
            sq = w_sq[0 if L == 1 else 1]
            per = 2 if L == 1 else 1
            base, g0 = LN_BASE[LAYERS[L]], T * L

            def rows_T(t):
                pe.wait_ge(ln_done, base + per * t + per)
                for k in range(KD):
                    last = nc.tensor.transpose(ps[:, 0, k * P:k * P + P], h[:, k * P:k * P + P], ident)
                last.then_inc(SA.hT_ps, 1)

            def project(t, s):
                g = g0 + t
                pe.wait_ge(SA.hT, g + 1)
                pe.wait_ge(SA.vbd, g + 1)
                if L == 0:
                    for k in range(KD):
                        last = nc.tensor.matmul(ps[:, 0, 256:384], w_mla[:, k, 0:P], hT[:, k, :], start=(k == 0), stop=(k == 1))
                    last.then_inc(SA.lat_ps, 1)
                    for i in range(4):
                        for k in range(KD):
                            last = nc.tensor.matmul(ps[:, 2, i * P:i * P + P], w_mla[:, k, P + i * P:2 * P + i * P], hT[:, k, :],
                                                    start=(k == 0), stop=(k == 1))
                    last.then_inc(SA.rope_ps, 1)
                    pe.wait_ge(SA.lat, g + 1)
                    nc.tensor.matmul(ps[:, 0, 384:512], w_mlac[:, 0:P], cqkvT[:, :], start=True, stop=True)
                    nc.tensor.matmul(ps[:, 0, 0:P], w_mlac[:, P:2 * P], cqkvT[:, :], start=True, stop=True).then_inc(SA.q_ps, 1)
                else:
                    for i in range(KD):
                        for k in range(KD):
                            last = nc.tensor.matmul(ps[:, 0, 256 + i * P:384 + i * P], sq[:, k, 0, i * P:i * P + P], hT[:, k, :],
                                                    start=(k == 0), stop=(k == 1))
                    last.then_inc(SA.q_ps, 1)
                    for i in range(KD):
                        for k in range(KD):
                            nc.tensor.matmul(ps[:, 1, i * P:i * P + P], sq[:, k, 1, i * P:i * P + P], hT[:, k, :],
                                             start=(k == 0), stop=(k == 1))
                ks = 1 if L == 0 else KD
                for b in range(2):
                    for k in range(ks):
                        for par in range(2):
                            w = w_mlac[:, 2 * P:2 * P + D] if L == 0 else sq[:, k, 2, :]
                            v_in = cqkvT[:, 64 * b:64 * b + 64] if L == 0 else hT[:, k, 64 * b:64 * b + 64]
                            last = nc.tensor.matmul(ps[64 * par:64 * par + 64, 1, 256 + P * b:256 + P * b + P], v_in,
                                                    w.rearrange("p (j a d) -> p a j d", a=2, d=16)[:, par, :, :],
                                                    start=(k == 0), stop=(k == ks - 1), skip_group_check=True)
                last.then_inc(SA.kv_ps, 1)

            def scores(t):
                g = g0 + t
                pe.wait_ge(SA.q, g + 1)
                pe.wait_ge(SA.kbd, g + 1)
                for hf in range(KD):
                    if L != 1:
                        nc.tensor.matmul(ps[:, 3 + hf, :], identb[:, :], causalb[:, :].rearrange("p (o n) -> p o n", o=1).broadcast_to((P, 8, N)),
                                         start=True, stop=False, skip_group_check=True)
                    for b in range(2):
                        last = nc.tensor.matmul(ps[64 * b:64 * b + 64, 3 + hf, :], qT[:, hf, 64 * b:64 * b + 64],
                                                kbd[:, hf, b, :, :].rearrange("p h n -> p (h n)"), start=(L == 1), stop=True, skip_group_check=True)
                last.then_inc(SA.s_ps, 1)

            def probs_T(t):
                g = g0 + t
                pe.wait_ge(SA.norm, g + 1)
                for j in range(8):
                    last = nc.tensor.transpose(ps[:, 5 + j // 4, (j % 4) * P:(j % 4) * P + P],
                                               pr[:, 2 * j:2 * j + 2, :].rearrange("p h n -> p (h n)"), ident)
                last.then_inc(SA.pT_ps, 1)

            def values(t, s):
                g = g0 + t
                pe.wait_ge(SA.pT, g + 1)
                pe.wait_ge(SA.vbd, g + 2)
                pe.wait_ge(SA.y_free, g + 1)
                for j in range(8):
                    for b in range(2):
                        last = nc.tensor.matmul(ps[32 * (j % 4):32 * (j % 4) + 32, 7, (j // 4) * P + 64 * b:(j // 4) * P + 64 * b + 64],
                                                vbd[s][:, b, j, :, :].rearrange("p a d -> p (a d)"), prT[:, j, 64 * b:64 * b + 64],
                                                start=True, stop=True, skip_group_check=True)
                last.then_inc(SA.att_ps, 1)

            def output(t):
                g = g0 + t
                pe.wait_ge(SA.att, g + 1)
                for k in range(KD):
                    w = w_mlao[:, k, :] if L == 0 else sq[:, k, 3, :]
                    last = nc.tensor.matmul(ps[:, 7, 256:512], sattT[:, k, :], w, start=(k == 0), stop=(k == 1))
                last.then_inc(SA.y_ps, 1)

            pe.wait_ge(ld["mla"] if L == 0 else ld["sq0"] if L == 1 else ld["sq1"], 160 if L == 0 else 64)
            pe.wait_ge(setup, 5)
            rows_T(0)
            project(0, 0)
            scores(0)

            def step(t, s, nxt):
                if nxt:
                    rows_T(t + 1)
                probs_T(t)
                if nxt:
                    project(t + 1, 1 - s)
                values(t, s)
                if nxt:
                    scores(t + 1)
                output(t)

            tiles(pe, step)

        def act_self(act, L):
            g0 = T * L

            def rows_T(t):
                act.wait_ge(SA.hT_ps, g0 + t + 1)
                if L == 1:
                    for k in range(KD):
                        last = nc.scalar.activation(hT[:, k, :], ps[:, 0, k * P:k * P + P], ACT.Identity, bias=vec("ln1_b", k), scale=vec("ln1_g", k))
                else:
                    last = nc.scalar.activation(hT[:, :, :], ps[:, 0, 0:256], ACT.Copy)
                last.then_inc(SA.hT, 1)

            def project(t):
                g = g0 + t
                if L == 0:
                    act.wait_ge(SA.lat_ps, g + 1)
                    nc.scalar.activation(cqkvT[:, :], ps[:, 0, 256:384], ACT.Gelu, bias=vec("bqkv")).then_inc(SA.lat, 1)
                    act.wait_ge(SA.q_ps, g + 1)
                    nc.scalar.activation(qT[:, 0, :], ps[:, 0, 384:512], ACT.Gelu, bias=vec("bqc"))
                    nc.scalar.activation(kTs[:, 0, :], ps[:, 0, 0:P], ACT.Gelu, bias=vec("bkc"))
                    act.wait_ge(SA.rope, g + 1)
                    nc.scalar.activation(qT[:, 1, :], rope[:, 0, :], ACT.Gelu)
                    nc.scalar.activation(kTs[:, 1, :], rope[:, 2, :], ACT.Gelu).then_inc(SA.q, 1)
                else:
                    act.wait_ge(SA.q_ps, g + 1)
                    nc.scalar.activation(qT[:, :, :], ps[:, 0, 256:512], ACT.Copy).then_inc(SA.q, 1)

            def exps(t):
                act.wait_ge(SA.sub, g0 + t + 1)
                nc.scalar.activation(pr[:, :, :], pr[:, :, :], ACT.Exp, scale=0.25).then_inc(SA.exp, 1)

            def probs_T(t):
                act.wait_ge(SA.pT_ps, g0 + t + 1)
                for i in range(2):
                    last = nc.scalar.activation(prT[:, 4 * i:4 * i + 4, :], ps[:, 5 + i, :], ACT.Copy)
                last.then_inc(SA.pT, 1)

            rows_T(0)
            project(0)
            exps(0)

            def step(t, s, nxt):
                if nxt:
                    rows_T(t + 1)
                probs_T(t)
                if nxt:
                    project(t + 1)
                    exps(t + 1)

            tiles(act, step)

        def dve_self(dve, L, x_sem, x_val):
            per = 2 if L == 1 else 1
            base, g0 = LN_BASE[LAYERS[L]], T * L

            def norm_a(t):
                xt = x[:, bass.ds(t, 1), :].rearrange("p a d -> p (a d)")
                ln_statistics(dve, [xt], base + per * t)

            def norm_b(t):
                xt = x[:, bass.ds(t, 1), :].rearrange("p a d -> p (a d)")
                ut = u[:, bass.ds(t, 1), :].rearrange("p a d -> p (a d)")
                if not isinstance(t, int) or g0 + t > 0:
                    dve.wait_ge(SA.hT_ps, g0 + t)
                ln_apply(dve, [xt], [ut if L == 1 else h[:, :]], base + per * t)
                if L == 1:
                    dve.wait_ge(ln_done, base + per * t + 1)
                    ln_statistics(dve, [ut], base + per * t + 1)
                    ln_apply(dve, [ut], [h[:, :]], base + per * t + 1)

            def rotate(t):
                g = g0 + t
                dve.wait_ge(SA.rope_ps, g + 1)
                cos, sin = cst[:, C_COS:C_COS + P], cst[:, C_SIN:C_SIN + P]
                for i, (bias, tab) in enumerate((("bqr", cos), ("bqs", sin), ("bkr", cos), ("bks", sin))):
                    last = nc.vector.scalar_tensor_tensor(rope[:, i, :], ps[:, 2, i * P:i * P + P], vec(bias), tab, ALU.add, ALU.mult)
                last.then_inc(SA.roped0, 1)
                dve.wait_ge(SA.roped0, g + 1)
                nc.vector.tensor_tensor(rope[:, 0, :], rope[:, 0, :], rope[:, 1, :], ALU.add)
                nc.vector.tensor_tensor(rope[:, 2, :], rope[:, 2, :], rope[:, 3, :], ALU.add).then_inc(SA.rope, 1)

            def spread_v(t, s):
                dve.wait_ge(SA.kv_ps, g0 + t + 1)
                v = ps[:, 1, 256:512].rearrange("p (b j d) -> p b j d", b=2, j=8)
                for par in range(2):
                    r = slice(64 * par, 64 * par + 64)
                    last = nc.vector.tensor_copy(vbd[s][r, :, :, par, :], v[r, :, :, :])
                last.then_inc(SA.vbd, 1)

            def spread_k(t):
                if L == 0:
                    dve.wait_ge(SA.q, g0 + t + 1)
                else:
                    dve.wait_ge(SA.kv_ps, g0 + t + 1)
                for hf in range(KD):
                    for b in range(2):
                        src = kTs[:, hf, 64 * b:64 * b + 64] if L == 0 else ps[:, 1, hf * P + 64 * b:hf * P + 64 * b + 64]
                        last = nc.vector.tensor_tensor(kbd[:, hf, b, :, :], src.rearrange("p (o n) -> p o n", o=1).broadcast_to((P, 8, N)),
                                                       head_of.rearrange("p (h o) -> p h o", o=1).broadcast_to((P, 8, N)), ALU.mult)
                last.then_inc(SA.kbd, 1)

            def softmax_a(t):
                g = g0 + t
                sc = ps[:, 3:5, :].rearrange("p a (h n) -> p (a h) n", n=N)
                dve.wait_ge(SA.s_ps, g + 1)
                nc.vector.tensor_reduce(smax[:, :], sc, AX_X, ALU.max).then_inc(SA.max, 1)
                dve.wait_ge(SA.max, g + 1)
                nc.vector.tensor_tensor(pr[:, :, :], sc, smax[:, :].rearrange("p (h o) -> p h o", o=1).broadcast_to((P, H, N)),
                                        ALU.subtract).then_inc(SA.sub, 1)

            def softmax_b(t):
                g = g0 + t
                dve.wait_ge(SA.exp, g + 1)
                nc.vector.tensor_reduce(ssum[:, :], pr[:, :, :], AX_X, ALU.add).then_inc(SA.sum, 1)
                dve.wait_ge(SA.sum, g + 1)
                nc.vector.reciprocal(srinv[:, :], ssum[:, :]).then_inc(SA.rinv, 1)

            def attention(t):
                dve.wait_ge(SA.att_ps, g0 + t + 1)
                if L == 0:
                    for k in range(KD):
                        last = nc.vector.tensor_scalar(sattT[:, k, :], ps[:, 7, k * P:k * P + P], vec("bv0", k), None, ALU.add)
                else:
                    last = nc.vector.tensor_copy(sattT[:, :, :], ps[:, 7, 0:256])
                last.then_inc(SA.att, 1)

            def residual(t):
                g = g0 + t
                xt = x[:, bass.ds(t, 1), :].rearrange("p a d -> p (a d)")
                ut = u[:, bass.ds(t, 1), :].rearrange("p a d -> p (a d)")
                dve.wait_ge(SA.y_ps, g + 1)
                first = ut if L == 1 else xt
                nc.vector.tensor_tensor(first, ps[:, 7, 256:512], first, ALU.add).then_inc(SA.y_free, 1)
                dve.wait_ge(SA.y_free, g + 2)
                if L == 0:
                    nc.vector.tensor_tensor(xt, xt, rows[:, 1, :], ALU.add).then_inc(SA.x_done, 1)
                elif L == 1:
                    nc.vector.tensor_tensor(xt, xt, ut, ALU.add).then_inc(SA.x_done, 1)
                else:
                    dve.sem_inc(SA.x_done, 1)

            dve.wait_ge(x_sem, x_val)
            if L == 0:
                dve.sem_inc(SA.vbd, 1)
                dve.sem_inc(SA.y_free, 1)
                for s in range(2):
                    nc.vector.memset(vbd[s][:, :, :, :, :], 0.0).then_inc(setup, 1)

            def prepare(t, s):
                if L == 0:
                    rotate(t)
                    spread_v(t, s)
                    spread_k(t)
                else:
                    spread_k(t)
                    spread_v(t, s)

            norm_a(0)
            norm_b(0)
            prepare(0, 0)
            softmax_a(0)
            norm_a(1)
            norm_b(1)
            softmax_b(0)

            def step(t, s, nxt, more):
                if more:
                    norm_a(t + 2)
                if nxt:
                    prepare(t + 1, 1 - s)
                attention(t)
                if nxt:
                    softmax_a(t + 1)
                if more:
                    norm_b(t + 2)
                residual(t)
                if nxt:
                    softmax_b(t + 1)

            with dve.Fori(0, T // 2 - 1) as i:
                for s in range(2):
                    step(2 * i + s, s, True, True)
            step(T - 2, 0, True, False)
            step(T - 1, 1, False, False)

        def pool_self(pool, L):
            per = 2 if L == 1 else 1
            base, g0 = LN_BASE[LAYERS[L]], T * L

            def norm(t):
                for i in range(per):
                    ln_rstd_pool(pool, 1, base + per * t + i)

            def scale_p(t):
                pool.wait_ge(SA.rinv, g0 + t + 1)
                nc.gpsimd.tensor_tensor(pr[:, :, :], pr[:, :, :], srinv[:, :].rearrange("p (h o) -> p h o", o=1).broadcast_to((P, H, N)),
                                        ALU.mult).then_inc(SA.norm, 1)

            norm(0)
            norm(1)
            scale_p(0)
            with pool.Fori(0, T // 2 - 1) as i:
                for s in range(2):
                    norm(2 * i + s + 2)
                    scale_p(2 * i + s + 1)
            scale_p(T - 1)

        class MO:
            mT_ps = sem("mo_mT_ps")
            mT = sem("mo_mT")
            router_ps = sem("mo_router_ps")
            logit = sem("mo_logit")
            top = sem("mo_top")
            topi = sem("mo_topi")
            diff = sem("mo_diff")
            exp = sem("mo_exp")
            w = sem("mo_w")
            sel = sem("mo_sel")
            gate = sem("mo_gate")
            gT_ps = sem("mo_gT_ps")
            gT = sem("mo_gT")
            b2_ps = sem("mo_b2_ps")
            b2 = sem("mo_b2")
            w1_ps = sem("mo_w1_ps")
            w1_free = sem("mo_w1_free")
            w2_ps = sem("mo_w2_ps")
            w2_free = sem("mo_w2_free")

        def pe_moe(pe):
            base = LN_BASE["moe"]

            def rows_T(t, s):
                pe.wait_ge(ln_done, base + t + 1)
                pe.wait_ge(MO.mT, t + 1)
                for k in range(KD):
                    last = nc.tensor.transpose(ps[:, s, k * P:k * P + P], h[:, k * P:k * P + P], ident)
                last.then_inc(MO.mT_ps, 1)

            tiles(pe, lambda t, s, nxt: rows_T(t, s))
            pe.wait_ge(MO.mT, T + 2)
            pe.wait_ge(ld["wg"], 16)
            for t in range(T):
                for k in range(KD):
                    last = nc.tensor.matmul(ps[:, 2 + t // 4, (t % 4) * P:(t % 4) * P + P], mT[:, k, t * P:t * P + P], wg[:, k, :],
                                            start=(k == 0), stop=(k == 1), skip_group_check=True)
            last.then_inc(MO.router_ps, 1)
            pe.wait_ge(MO.gate, 1)
            for t in range(T):
                last = nc.tensor.transpose(ps[:, t // 4, (t % 4) * P:(t % 4) * P + P], gate[:, t, :], ident)
            last.then_inc(MO.gT_ps, 1)
            pe.wait_ge(MO.gT, 1)
            pe.wait_ge(ld["b2"], 16)
            for t in range(T):
                last = nc.tensor.matmul(ps[:, 4 + t // 2, (t % 2) * D:(t % 2) * D + D], gate_T[:, t * P:t * P + P], b2[:, :],
                                        start=True, stop=True, skip_group_check=True)
            last.then_inc(MO.b2_ps, 1)

            def hidden(e, s, c):
                if c == 0:
                    pe.wait_ge(ld_e[s], 16 * (e - s) + 32)
                for f in range(FT):
                    pe.wait_ge(MO.w1_free, 16 * e + 8 * c + f + 1)
                    for k in range(KD):
                        last = nc.tensor.matmul(ps[:, f % 4, :], ew1[s][:, k, f * P:f * P + P], mT[:, k, 512 * c:512 * c + 512],
                                                start=(k == 0), stop=(k == 1))
                    last.then_inc(MO.w1_ps, 1)

            def outputs(e, s, c):
                pe.wait_ge(MO.w1_free, 16 * e + 8 * c + 8 + 4)
                for i in range(4):
                    pe.wait_ge(MO.w2_free, 8 * e + 4 * c + i + 1)
                    for f in range(FT):
                        last = nc.tensor.matmul(ps[:, 4 + i, 0:D], h1[c][:, f, i * P:i * P + P], ew2[s][:, f, :],
                                                start=(f == 0), stop=(f == FT - 1))
                    last.then_inc(MO.w2_ps, 1)

            pe.wait_ge(MO.b2, 1)
            hidden(0, 0, 0)

            def step(e, s, nxt):
                hidden(e, s, 1)
                outputs(e, s, 0)
                if nxt:
                    hidden(e + 1, 1 - s, 0)
                outputs(e, s, 1)

            tiles(pe, step)

        def act_moe(act):
            act.sem_inc(MO.mT, 2)
            act.sem_inc(MO.w1_free, 4)

            def rows_T(t, s, nxt):
                act.wait_ge(MO.mT_ps, t + 1)
                act.sem_inc(act_go, 1)
                for k in range(KD):
                    last = nc.scalar.activation(mT[:, k, bass.ds(t * P, P)], ps[:, s, k * P:k * P + P], ACT.Identity,
                                                bias=vec("ln2_b", k), scale=vec("ln2_g", k))
                last.then_inc(MO.mT, 1)

            tiles(act, rows_T)
            act.wait_ge(MO.diff, 1)
            nc.scalar.activation(gexp[:, :], gexp[:, :], ACT.Exp).then_inc(MO.exp, 1)
            act.wait_ge(MO.gT_ps, 1)
            act.wait_ge(pool_setup, 7)
            for i in range(2):
                last = nc.scalar.activation(gate_T[:, 512 * i:512 * i + 512], ps[:, i, :], ACT.Copy)
            last.then_inc(MO.gT, 1)

            def hidden(e, s, c):
                for f in range(FT):
                    act.wait_ge(MO.w1_ps, 16 * e + 8 * c + f + 1)
                    act.sem_inc(act_go, 1)
                    nc.scalar.activation(h1[c][:, f, :], ps[:, f % 4, :], ACT.Gelu_apprx_tanh,
                                         bias=col[:, bass.ds(e * FT + (COLS["b1"][0] + f), 1)]).then_inc(MO.w1_free, 1)

            def step(e, s, nxt):
                for c in range(2):
                    hidden(e, s, c)

            tiles(act, step)

        def dve_moe(dve):
            base = LN_BASE["moe"]

            def norm(t):
                ut = u[:, bass.ds(t, 1), :].rearrange("p a d -> p (a d)")
                ln_statistics(dve, [ut], base + t)
                ln_apply(dve, [ut], [h[:, :]], base + t)

            dve.wait_ge(SA.x_done, 2 * T)
            norm(0)

            def step_norm(t, s, nxt):
                if nxt:
                    dve.wait_ge(MO.mT_ps, t + 1)
                    norm(t + 1)

            tiles(dve, step_norm)
            dve.wait_ge(MO.router_ps, 1)
            for i in range(2):
                last = nc.vector.tensor_copy(logit[:, 4 * i:4 * i + 4, :], ps[:, 2 + i, :].rearrange("p (t e) -> p t e", e=P)[:, :, 0:E])
            last.then_inc(MO.logit, 1)
            dve.wait_ge(MO.logit, 1)
            for t in range(T):
                last = nc.vector.max(top[:, t, :], logit[:, t, :])
            last.then_inc(MO.top, 1)
            dve.wait_ge(MO.top, 1)
            nc.vector.tensor_tensor(gexp[:, :], top[:, :, 1], top[:, :, 0], ALU.subtract).then_inc(MO.diff, 1)
            for t in range(T):
                last = nc.vector.max_index(topi[:, t, :], top[:, t, :], logit[:, t, :])
            last.then_inc(MO.topi, 1)
            dve.wait_ge(MO.topi, 1)
            nc.vector.tensor_copy(topf[:, :, :], topi[:, :, 0:2]).then_inc(MO.topi, 1)
            dve.wait_ge(MO.exp, 1)
            nc.vector.tensor_scalar(gw[:, :, 2], gexp[:, :], 1.0, None, ALU.add).then_inc(MO.w, 1)
            dve.wait_ge(MO.w, 1)
            nc.vector.reciprocal(gw[:, :, 0], gw[:, :, 2]).then_inc(MO.w, 1)
            dve.wait_ge(MO.w, 2)
            nc.vector.tensor_tensor(gw[:, :, 1], gexp[:, :], gw[:, :, 0], ALU.mult).then_inc(MO.w, 1)
            dve.wait_ge(MO.topi, 2)
            iota = cst[:, C_IOTA:C_IOTA + E].rearrange("p (o e) -> p o e", o=1).broadcast_to((P, T, E))
            for i in range(2):
                last = nc.vector.tensor_tensor(gsel[:, :, i, :], iota, topf[:, :, i:i + 1].broadcast_to((P, T, E)), ALU.is_equal)
            last.then_inc(MO.sel, 1)
            dve.wait_ge(MO.sel, 1)
            dve.wait_ge(MO.w, 3)
            for i in range(2):
                last = nc.vector.tensor_tensor(gsel[:, :, i, :], gsel[:, :, i, :], gw[:, :, i:i + 1].broadcast_to((P, T, E)), ALU.mult)
            last.then_inc(MO.sel, 1)
            dve.wait_ge(MO.sel, 2)
            dve.wait_ge(pool_setup, 8)
            nc.vector.tensor_tensor(gate[:, :, 0:E], gsel[:, :, 0, :], gsel[:, :, 1, :], ALU.add).then_inc(MO.gate, 1)
            dve.wait_ge(MO.b2_ps, 1)
            for i in range(4):
                last = nc.vector.tensor_tensor(x[:, 2 * i:2 * i + 2, :], ps[:, 4 + i, :].rearrange("p (t d) -> p t d", t=2), x[:, 2 * i:2 * i + 2, :], ALU.add)
            last.then_inc(MO.b2, 1)
            dve.wait_ge(MO.b2, 1)
            dve.sem_inc(MO.w2_free, 4)

            def step(e, s, nxt):
                for c in range(2):
                    for i in range(4):
                        n = 8 * e + 4 * c + i
                        dve.wait_ge(MO.w2_ps, n + 1)
                        dve.wait_ge(MO.w2_free, n + 1)
                        nc.vector.scalar_tensor_tensor(x[:, 4 * c + i, :], ps[:, 4 + i, 0:D], gate[:, 4 * c + i, bass.ds(e, 1)], x[:, 4 * c + i, :],
                                                       ALU.mult, ALU.add).then_inc(MO.w2_free, 1)

            tiles(dve, step)

        def pool_moe(pool):
            tiles(pool, lambda t, s, nxt: ln_rstd_pool(pool, 1, LN_BASE["moe"] + t))

        class FF:
            raw_free = sem("ff_raw_free")
            w = sem("ff_w")
            scale = sem("ff_scale")
            xT_ps = sem("ff_xT_ps")
            xT_hi = sem("ff_xT_hi")
            xT = sem("ff_xT")
            r_ps = sem("ff_r_ps")
            r_free = sem("ff_r_free")
            h_free = sem("ff_h_free")
            hi = sem("ff_hi")
            split = sem("ff_split")
            y_ps = sem("ff_y_ps")
            y_free = sem("ff_y_free")
        PIECES = [("w0", 0), ("w0", 1), ("w1", 0), ("w1", 1), ("w1", 2), ("w1", 3), ("w2", 0)]

        def pool_ff_weights(pool):
            for n, (w, i) in enumerate(PIECES):
                if w == "w0":
                    continue
                pool.wait_ge(ld_ff[n % 2], 32 + 16 * (n // 2))
                raw = ffraw[:, n % 2, :, :]
                if w == "w1":
                    last = nc.gpsimd.tensor_scalar(ffw1[:, 2 * i:2 * i + 2, :], raw[:, :, :], 2.0, -1.0, ALU.mult, ALU.add)
                else:
                    last = nc.gpsimd.tensor_scalar(ffw2[:, :, :], raw.rearrange("p a n -> p (a n)").rearrange("p (k d) -> p k d", d=D), 2.0, -1.0, ALU.mult, ALU.add)
                last.then_inc(FF.w, 1)
                pool.wait_ge(FF.w, n + 1)
                pool.sem_inc(FF.raw_free, 1)

        def dve_ff_weights(dve):
            dve.sem_inc(FF.raw_free, 2)
            for n in range(KD):
                dve.wait_ge(ld_ff[n], 32)
                nc.vector.tensor_tensor(ffw0[:, n, :], ffraw[:, n, 0, :], ffraw[:, n, 1, :], ALU.subtract).then_inc(FF.w, 1)
                dve.wait_ge(FF.w, n + 1)
                dve.sem_inc(FF.raw_free, 1)

        def pe_ff(pe):
            pe.wait_ge(FF.w, len(PIECES))
            with pe.Fori(0, 2) as c:
                for i in range(4):
                    pe.wait_ge(ln_done, LN_BASE["mlp"] + 4 * c + i + 1)
                    pe.wait_ge(FF.xT, 4 * c + i + 1)
                    for k in range(KD):
                        last = nc.tensor.transpose(ps[:, i % 2, k * P:k * P + P], h[:, k * P:k * P + P], ident)
                    last.then_inc(FF.xT_ps, 1)
                pe.wait_ge(FF.xT, 4 * c + 6)
                for layer, (w, src, ks) in enumerate(((ffw0, fxT, KD), (ffw1, f0, FT))):
                    if layer == 1:
                        pe.wait_ge(FF.split, 16 * c + 8)
                    for f in range(FT):
                        n = 16 * c + 8 * layer + f
                        pe.wait_ge(FF.r_free, n + 1)
                        for k in range(ks):
                            for part in range(2):
                                last = nc.tensor.matmul(ps[:, 2 + f % 4, :], w[:, k, f * P:f * P + P], src[part][:, k, :],
                                                        start=(k == 0 and part == 0), stop=(k == ks - 1 and part == 1))
                        last.then_inc(FF.r_ps, 1)
                pe.wait_ge(FF.split, 16 * c + 16)
                for i in range(4):
                    pe.wait_ge(FF.y_free, 4 * c + i + 1)
                    for k in range(FT):
                        for part in range(2):
                            last = nc.tensor.matmul(ps[:, 6 + i % 2, 0:D], f1[part][:, k, i * P:i * P + P], ffw2[:, k, :],
                                                    start=(k == 0 and part == 0), stop=(k == FT - 1 and part == 1))
                    last.then_inc(FF.y_ps, 1)

        def act_ff(act):
            act.sem_inc(FF.r_free, 4)
            act.wait_ge(FF.scale, 2)
            with act.Fori(0, 2) as c:
                for i in range(4):
                    act.wait_ge(FF.xT_ps, 4 * c + i + 1)
                    nc.scalar.activation(fxT[0][:, :, i * P:i * P + P], ps[:, i % 2, 0:D].rearrange("p (k n) -> p k n", k=2), ACT.Copy).then_inc(FF.xT_hi, 1)
                for layer in range(2):
                    for f in range(FT):
                        n = 16 * c + 8 * layer + f
                        act.wait_ge(FF.r_ps, n + 1)
                        act.wait_ge(FF.h_free, n + 1)
                        nc.scalar.activation(fh[f % 2][:, :], ps[:, 2 + f % 4, :], ACT.Relu, scale=ffs[:, layer:layer + 1]).then_inc(FF.r_free, 1)

        def dve_ff(dve):
            base = LN_BASE["mlp"]
            nc.vector.tensor_scalar(ffs[:, 0:1], vec("s0"), 4.0, None, ALU.mult).then_inc(FF.scale, 1)
            nc.vector.tensor_scalar(ffs[:, 1:2], vec("s1"), 2.0, None, ALU.mult).then_inc(FF.scale, 1)
            for k, v in ((FF.xT, 2), (FF.h_free, 2), (FF.y_free, 2)):
                dve.sem_inc(k, v)
            dve.wait_ge(SA.y_free, 3 * T + 1)
            with dve.Fori(0, 2) as c:
                for i in range(4):
                    xt = x[:, bass.ds(4 * c + i, 1), :].rearrange("p a d -> p (a d)")
                    ln_statistics(dve, [xt], base + 4 * c + i)
                    if i > 0:
                        dve.wait_ge(FF.xT_ps, 4 * c + i)
                    ln_apply(dve, [xt], [h[:, :]], base + 4 * c + i)
                    dve.wait_ge(FF.xT_hi, 4 * c + i + 1)
                    nc.vector.tensor_tensor(fxT[1][:, :, i * P:i * P + P], ps[:, i % 2, 0:D].rearrange("p (k n) -> p k n", k=2),
                                            fxT[0][:, :, i * P:i * P + P].bitcast(F32), ALU.subtract).then_inc(FF.xT, 1)
                for layer, dst in enumerate((f0, f1)):
                    for f in range(FT):
                        n = 16 * c + 8 * layer + f
                        dve.wait_ge(FF.r_free, n + 5)
                        nc.vector.tensor_copy(dst[0][:, f, :], fh[f % 2][:, :]).then_inc(FF.hi, 1)
                        dve.wait_ge(FF.hi, n + 1)
                        nc.vector.tensor_tensor(dst[1][:, f, :], fh[f % 2][:, :], dst[0][:, f, :].bitcast(F32), ALU.subtract).then_inc(FF.split, 1)
                        dve.wait_ge(FF.split, n + 1)
                        dve.sem_inc(FF.h_free, 1)
                for i in range(4):
                    xt = x[:, bass.ds(4 * c + i, 1), :].rearrange("p a d -> p (a d)")
                    dve.wait_ge(FF.y_ps, 4 * c + i + 1)
                    nc.vector.scalar_tensor_tensor(xt, ps[:, 6 + i % 2, 0:D], vec("s2"), xt, ALU.mult, ALU.add).then_inc(FF.y_free, 1)

        def pool_ff(pool):
            tiles(pool, lambda t, s, nxt: ln_rstd_pool(pool, 1, LN_BASE["mlp"] + t))

        @block.sync
        def _(sp):
            def whole(dst, src, s):
                sp.dma_start(dst, src).then_inc(s, 16)

            def weight(name):
                return a[name].rearrange("(k p) n -> p k n", p=P)

            def ctx_tile(l, t, s):
                sp.dma_start((X0, X1)[l]["cin"][:, s, :, :], y_at[bass.ds(t, 1), :, :, :].rearrange("o p k d -> p (o k) d")).then_inc(ld_ctx[l][s], 16)

            def expert(e, s):
                sp.dma_start(ew1[s][:, :, :], a["L0_ffn_W1"][bass.ds(e, 1), :, :].rearrange("o (k p) n -> p (o k) n", p=P)).then_inc(ld_e[s], 16)
                sp.dma_start(ew2[s][:, :, :], a["L0_ffn_W2"][bass.ds(e, 1), :, :].rearrange("o (k p) n -> p (o k) n", p=P)).then_inc(ld_e[s], 16)

            whole(x[:, :, :], a["x"].rearrange("b n d -> (b n) d").rearrange("(t p) d -> p t d", p=P), ld["x"])
            ctx_tile(0, 0, 0)
            whole(cst[:, :], a["consts"], ld["const"])
            whole(col[:, :], a["cols"], ld["const"])
            for k, w in (("wkv", "L0_xattn_Wkv"), ("wq", "L0_xattn_Wq"), ("wo", "L0_xattn_Wo")):
                whole(X0[k][:, :, :], weight(w), ld["x0w"])
            ctx_tile(0, 1, 1)
            whole(rows[:, :, :], a["rows"], ld["const"])
            for i, w in enumerate(("wq", "wkv")):
                whole(w_mla[:, :, 64 * i:64 * i + 64], weight("L0_attn_" + w), ld["mla"])
            for i, w in enumerate(("wqr", "wqr_swapped", "wkr", "wkr_swapped")):
                whole(w_mla[:, :, P + P * i:2 * P + P * i], weight("L0_attn_" + w), ld["mla"])
            whole(w_mlao[:, :, :], weight("L0_attn_wo"), ld["mla"])
            sp.wait_ge(pool_setup, 4)
            whole(w_mlac[0:64, 0:P], a["L0_attn_wqc"], ld["mla"])
            whole(w_mlac[64:P, P:2 * P], a["L0_attn_wkc"], ld["mla"])
            whole(w_mlac[64:P, 2 * P:2 * P + D], a["L0_attn_wv"], ld["mla"])
            whole(wg[:, :, 0:E], weight("L0_ffn_Wg"), ld["wg"])
            for i, w in enumerate(("Wq", "Wk", "Wv", "Wo")):
                whole(w_sq[0][:, :, i, :], weight("L0_ffn_" + w), ld["sq0"])
            for i, w in enumerate("QKVO"):
                whole(w_sq[1][:, :, i, :], weight("L1_attn_W_" + w), ld["sq1"])
            with sp.Fori(0, T // 2 - 1) as i:
                for s in range(2):
                    sp.wait_ge(ln_done, LN_BASE["x0"] + 2 * (2 * i + s) + 2)
                    ctx_tile(0, 2 * i + s + 2, s)
            sp.wait_ge(X[0].x_done, T)
            whole(maskrow[0:1, :, :], a["mask_BxS2_ik0"].rearrange("(o b) s -> o b s", o=1), ld["pad"])
            sp.wait_ge(pool_setup, 6)
            whole(b2[0:E, :], a["L0_ffn_b2"], ld["b2"])
            for i, w in enumerate(("Wq", "Wk", "Wv", "Wo")):
                whole(xw[:, :, i, :], weight("L1_xattn_" + w), ld["xw"])
            for e in range(2):
                expert(e, e)
            for n, (w, i) in enumerate(PIECES):
                sp.wait_ge(FF.raw_free, n + 1)
                if w == "w0":
                    for half in range(2):
                        whole(ffraw[:, n % 2, half, :], a["L1_ffn_k0"][half * D + i * P:half * D + i * P + P, :], ld_ff[n % 2])
                elif w == "w1":
                    whole(ffraw[:, n % 2, :, :], weight("L1_ffn_k1")[:, 2 * i:2 * i + 2, :], ld_ff[n % 2])
                else:
                    whole(ffraw[:, n % 2, :, :].rearrange("p a n -> p (a n)").rearrange("p (k d) -> p k d", d=D), weight("L1_ffn_k2"), ld_ff[n % 2])
            with sp.Fori(0, E // 2 - 1) as i:
                for s in range(2):
                    sp.wait_ge(MO.w2_ps, 8 * (2 * i + s) + 8)
                    expert(2 * i + s + 2, s)
            sp.wait_ge(MO.w2_ps, 8 * E)
            ctx_tile(1, 0, 0)
            ctx_tile(1, 1, 1)
            with sp.Fori(0, T // 2 - 1) as i:
                for s in range(2):
                    for bank in range(2):
                        sp.wait_ge(X[1].fill_done[bank], X[1].per * (2 * i + s) + 1)
                    ctx_tile(1, 2 * i + s + 2, s)
            out_v = out.rearrange("b n d -> (b n) d").rearrange("(t p) d -> p t d", p=P)
            for c in range(2):
                sp.wait_ge(FF.y_free, 4 * c + 6)
                sp.dma_start(out_v[:, 4 * c:4 * c + 4, :], x[:, 4 * c:4 * c + 4, :]).then_inc(stored, 16)
            sp.wait_ge(stored, 32)
            sp.wait_ge(dve_go, 2 * LN_COUNT)
            sp.wait_ge(act_go, T + 2 * E * FT)

        @block.gpsimd
        def _(pool):
            nc.gpsimd.memset(neghalf[:, :], -0.5).then_inc(pool_setup, 1)
            nc.gpsimd.memset(eps[:, :], EPS).then_inc(pool_setup, 1)
            nc.gpsimd.memset(w_mlac[:, :], 0.0).then_inc(pool_setup, 1)
            nc.gpsimd.memset(wg[:, :, :], 0.0).then_inc(pool_setup, 1)
            nc.gpsimd.memset(padneg[:, :, :], 0.0).then_inc(pool_setup, 1)
            pool.wait_ge(pool_setup, 5)
            pool_cross(pool, X[0])
            pool.wait_ge(X[0].x_done, T)
            nc.gpsimd.memset(b2[:, :], 0.0).then_inc(pool_setup, 1)
            pool.wait_ge(ld["pad"], 16)
            nc.gpsimd.tensor_scalar(padneg[0:1, :, :], maskrow[0:1, :, :], 0.0, NEG, ALU.is_equal, ALU.mult).then_inc(pool_setup, 1)
            nc.gpsimd.memset(gate[:, :, :], 0.0).then_inc(pool_setup, 1)
            pool_self(pool, 0)
            pool_self(pool, 1)
            pool_moe(pool)
            pool_ff_weights(pool)
            pool_cross(pool, X[1])
            pool_self(pool, 2)
            pool_ff(pool)

        @block.scalar
        def _(act):
            act.wait_ge(ld["const"], 48)
            act_cross(act, X[0])
            act_self(act, 0)
            act_self(act, 1)
            act_moe(act)
            act_cross(act, X[1])
            act_self(act, 2)
            act_ff(act)

        @block.vector
        def _(dve):
            dve.wait_ge(ld["const"], 48)
            dve.wait_ge(ld["x"], 16)
            nc.vector.tensor_copy(identb[:, :], ident).then_inc(setup, 1)
            nc.vector.tensor_copy(causalb[:, :], cst[:, C_CAUSAL:C_CAUSAL + N]).then_inc(setup, 1)
            nc.vector.tensor_copy(row0b[:, :], cst[:, C_ROW0:C_ROW0 + P]).then_inc(setup, 1)
            dve_cross(dve, X[0])
            dve_ff_weights(dve)
            dve_self(dve, 0, X[0].x_done, T)
            dve_self(dve, 1, SA.x_done, T)
            dve_moe(dve)
            dve.wait_ge(MO.w2_free, 8 * E + 4)
            dve_cross(dve, X[1])
            dve_self(dve, 2, X[1].x_done, T)
            dve_ff(dve)

        @block.tensor
        def _(pe):
            pe.wait_ge(ld["const"], 48)
            pe_cross(pe, X[0])
            pe_self(pe, 0)
            pe_self(pe, 1)
            pe_moe(pe)
            pe_cross(pe, X[1])
            pe_self(pe, 2)
            pe_ff(pe)


def ctx_views(ctx):
    return ctx.rearrange("b s d -> (b s) d").rearrange("(t k p) d -> t p k d", k=4, p=P)


def _tables(i):
    p = np.arange(P)
    cst = np.zeros((P, C_ALL), np.float32)
    cst[:, C_IDENT:C_IDENT + P] = np.eye(P)
    cst[:, C_HEAD:C_HEAD + 8] = p[:, None] // 16 == np.arange(8)
    cst[:, C_PAR:C_PAR + 2] = p[:, None] // 16 % 2 == np.arange(2)
    cst[:, C_CAUSAL:C_CAUSAL + N] = np.where(np.arange(N)[None, :] > (p % N)[:, None], NEG, 0.0)
    inv = (1.0 / np.float32(10000.0) ** (np.arange(0, P, 2, dtype=np.float32) / np.float32(P))).astype(np.float32)
    ang = np.tile(np.arange(N, dtype=np.float32)[None, :] * inv[:, None], (2, 2))
    cst[:, C_COS:C_COS + P] = np.cos(ang)
    cst[:, C_SIN:C_SIN + P] = np.sin(ang) * np.where(p < 64, -1, 1)[:, None]
    cst[:, C_IOTA:C_IOTA + E] = np.arange(E)
    cst[0, C_ROW0:C_ROW0 + P] = 1.0
    half = lambda v: np.concatenate([v[64:], v[:64]])
    vecs = {"ln_l_w": i["L0_xattn_ln_l_w"], "ln_l_b": i["L0_xattn_ln_l_b"], "ln_c_w": i["L0_xattn_ln_c_w"], "ln_c_b": i["L0_xattn_ln_c_b"],
            "bqkv": np.concatenate([i["L0_attn_bq"], i["L0_attn_bkv"]]), "bqc": i["L0_attn_bqc"], "bkc": i["L0_attn_bkc"],
            "bqr": i["L0_attn_bqr"], "bqs": half(i["L0_attn_bqr"]), "bkr": i["L0_attn_bkr"], "bks": half(i["L0_attn_bkr"]),
            "bv0": i["L0_attn_bv"], "ln1_g": i["L0_ffn_ln1_g"], "ln1_b": i["L0_ffn_ln1_b"], "ln2_g": i["L0_ffn_ln2_g"], "ln2_b": i["L0_ffn_ln2_b"],
            "xbq": i["L1_xattn_bq"], "xbk": i["L1_xattn_bk"], "xbv": i["L1_xattn_bv"], "b1": i["L0_ffn_b1"].reshape(-1),
            "s0": np.broadcast_to(i["L1_ffn_s0"], (P,)), "s1": np.broadcast_to(i["L1_ffn_s1"], (P,)), "s2": np.broadcast_to(i["L1_ffn_s2"], (P,))}
    cols = np.concatenate([np.reshape(vecs[k], (-1, P)).T for k in COLS], 1)
    rows = np.stack([np.broadcast_to(i[k], (P, D)) for k in ("L0_xattn_bo", "L0_attn_bo", "L1_xattn_bo")], 1)
    return {"consts": cst, "cols": cols, "rows": rows}


def _inputs(i):
    ins = {k: v for k, v in i.items() if k in ("x", "ctx_1024", "mask_BxS2_ik0") or v.ndim >= 2}
    for k in "QKVO":
        ins[f"L1_attn_W_{k}"] = ins[f"L1_attn_W_{k}"].T
    for k in ("wqr", "wkr"):
        w = ins[f"L0_attn_{k}"]
        ins[f"L0_attn_{k}_swapped"] = np.concatenate([w[:, 64:], w[:, :64]], 1)
    ins.update(_tables(i))
    return {k: np.ascontiguousarray(v) for k, v in ins.items()}


def kernel(**inputs):
    import concourse.bacc as bacc
    from concourse.bass_utils import run_bass_kernel_spmd

    arrays = _inputs({k: np.asarray(v) for k, v in inputs.items()})
    nc = bacc.Bacc("TRN2", target_bir_lowering=False, num_devices=1)
    aps = {k: nc.dram_tensor(k + "_dram", v.shape, mybir.dt.from_np(v.dtype), kind="ExternalInput").ap() for k, v in arrays.items()}
    out = nc.dram_tensor("out_dram", (B, N, D), F32, kind="ExternalOutput").ap()
    build(nc, aps, out)
    r = run_bass_kernel_spmd(nc, [{k + "_dram": v for k, v in arrays.items()}], core_ids=[0])
    return r.results[0]["out_dram"]
```

```python
from contextlib import ExitStack

import numpy as np

import concourse.bass as bass
from concourse import mybir

F32 = mybir.dt.float32
F32R = mybir.dt.float32r
BF16 = mybir.dt.bfloat16
U8 = mybir.dt.uint8
U32 = mybir.dt.uint32
I32 = mybir.dt.int32
ALU = mybir.AluOpType
ACT = mybir.ActivationFunctionType
AX_X = mybir.AxisListType.X

P = 128
B, N, D, S = 16, 64, 256, 256
T = B * N // P
KD = D // P
H = 16
INNER = 1024
E, F = 8, 1024
FT = F // P
NEG = -1e30
EPS = 1e-5

C_IDENT, C_HEAD, C_PAR, C_CAUSAL, C_COS, C_SIN, C_IOTA, C_ROW0 = np.cumsum([0, 128, 8, 2, 64, 128, 128, 8])
C_ALL = C_ROW0 + 128
COLS = {}
for _name, _k in [("ln_l_w", 2), ("ln_l_b", 2), ("ln_c_w", 2), ("ln_c_b", 2), ("bqkv", 1), ("bqc", 1), ("bkc", 1),
                  ("bqr", 1), ("bqs", 1), ("bkr", 1), ("bks", 1), ("bv0", 2), ("ln1_g", 2), ("ln1_b", 2), ("ln2_g", 2), ("ln2_b", 2),
                  ("xbq", 2), ("xbk", 2), ("xbv", 2), ("b1", E * FT), ("s0", 1), ("s1", 1), ("s2", 1)]:
    COLS[_name] = (sum(k for _, k in COLS.values()), _k)
COL_ALL = sum(k for _, k in COLS.values())


def build(nc, a, out):
    with ExitStack() as ctx:
        at = [(nc.sbuf_base + 31) // 32 * 32]

        def sb(name, shape, dt=F32):
            size = int(np.prod(shape[1:])) * (1 if dt == U8 else 2 if dt == BF16 else 4)
            here = at[0]
            at[0] += (size + 31) // 32 * 32
            assert at[0] <= nc.sbuf_usable_end, (name, at[0])
            return nc.alloc_sbuf_tensor_at(name, shape, dt, offset=here)

        def sem(name):
            return ctx.enter_context(nc.semaphore(name))

        ps = ctx.enter_context(nc.psum_tensor("ps", [P, 8, 512], F32))

        x = sb("x_res", [P, T, D])
        cst = sb("cst", [P, C_ALL])
        col = sb("col", [P, COL_ALL])
        rows = sb("rows", [P, 3, D])
        ident = cst[:, C_IDENT:C_IDENT + P]
        identb = sb("identb", [P, P], BF16)
        causalb = sb("causalb", [P, N], BF16)
        row0b = sb("row0b", [P, P], BF16)
        padneg = sb("padneg", [P, B, S], BF16)
        head_of = cst[:, C_HEAD:C_HEAD + 8]
        par_of = cst[:, C_PAR:C_PAR + 2]
        w_sq_at = at[0]
        w_sq = [sb(f"w_sq{i}", [P, KD, 4, D]) for i in range(2)]
        w_mla = sb("w_mla", [P, KD, 128 + 4 * 128])
        w_mlac = sb("w_mlac", [P, 128 + 128 + D])
        w_mlao = sb("w_mlao", [P, KD, D])
        wg = sb("wg", [P, KD, P])
        ln_st = sb("ln_st", [P, 5, 6])
        ln_mv = sb("ln_mv", [P, 5, 2])
        ln_ve = sb("ln_ve", [P, 5])
        ln_rs = sb("ln_rs", [P, 5])
        neghalf = sb("neghalf", [P, 5])
        eps = sb("eps", [P, 5])
        rn_st = sb("rn_st", [P, 6])
        rn_cur = sb("rn_cur", [P, 2, 2])
        rn_tmp = sb("rn_tmp", [P, 2, 4])
        rn_mean = sb("rn_mean", [P, T])
        rn_rs = sb("rn_rs", [P, T])
        rn_rs2 = sb("rn_rs2", [P, T])

        def vec(name, i=0):
            at0, _ = COLS[name]
            return col[:, at0 + i:at0 + i + 1]

        mark = at[0]

        def cross_buffers(tag, kg, vw, probs_at=None):
            g = {}
            g["cin"] = sb(tag + "cin", [P, 2, 4, D])
            g["cT"] = sb(tag + "cT", [P, KD, 512])
            g["lat"] = sb(tag + "lat", [P, D])
            g["latT"] = sb(tag + "latT", [P, KD, P])
            g["qbd"] = [sb(f"{tag}qbd{i}", [P, 2, 8, P]) for i in range(2)]
            g["kT"] = [sb(f"{tag}kT{i}", [P, kg, 512]) for i in range(2)]
            g["v"] = [sb(f"{tag}v{i}", [P, 4, vw]) for i in range(2)]
            after, at[0] = at[0], at[0] if probs_at is None else probs_at
            g["p"] = [sb(f"{tag}p{i}", [P, 4, S]) for i in range(2)]
            g["pT"] = [sb(f"{tag}pT{i}", [P, 8, P]) for i in range(2)]
            at[0] = at[0] if probs_at is None else after
            g["attT"] = sb(tag + "attT", [P, kg, P])
            g["sum"] = sb(tag + "sum", [P, 2, 4])
            g["rinv"] = sb(tag + "rinv", [P, 2, 4])
            g["nmax"] = sb(tag + "nmax", [P, 2, 4])
            return g

        X0 = cross_buffers("x0", 8, INNER)
        X0["cn"] = sb("x0cn", [P, 4, D])
        X0["wq"] = sb("x0wq", [P, KD, INNER])
        X0["wkv"] = sb("x0wkv", [P, KD, 2 * INNER])
        X0["wo"] = sb("x0wo", [P, 8, D])

        at[0] = mark
        h = sb("h", [P, D])
        hT = sb("hT", [P, KD, P])
        qT = sb("qT", [P, KD, P])
        kTs = sb("kTs", [P, KD, P])
        cqkvT = sb("cqkvT", [P, P])
        rope = sb("rope", [P, 4, P])
        h1_at = at[0]
        kbd = sb("kbd", [P, KD, 2, 8, N])
        pr = sb("pr", [P, H, N])
        prT = sb("prT", [P, 8, P])
        vbd = [sb(f"vbd{i}", [P, 2, 8, 2, 16]) for i in range(2)]
        smax = sb("smax", [P, H])
        ssum = sb("ssum", [P, H])
        srinv = sb("srinv", [P, H])
        sattT = sb("sattT", [P, KD, P])
        u_at = at[0]
        u = sb("u", [P, T, D])
        ffw0 = sb("ffw0", [P, KD, F], F32R)
        ffw1 = sb("ffw1", [P, FT, F], F32R)
        ffw2 = sb("ffw2", [P, FT, D], F32R)
        ffraw = sb("ffraw", [P, 2, 2, F], U8)
        ffs = sb("ffs", [P, 2])
        xw = sb("xw", [P, KD, 4, D])
        mark2 = at[0]
        mT = sb("mT", [P, KD, T * P])
        ew1 = [sb(f"ew1_{i}", [P, KD, F]) for i in range(2)]
        ew2 = [sb(f"ew2_{i}", [P, FT, D]) for i in range(2)]
        h1_at0 = at[0]
        h1 = [sb("h1_0", [P, FT, 512]), nc.alloc_sbuf_tensor_at("h1_1", [P, FT, 512], F32, offset=h1_at)]
        logit = sb("logit", [P, T, E])
        top = sb("top", [P, T, 8])
        topi = sb("topi", [P, T, 8], U32)
        topf = sb("topf", [P, T, 2])
        gexp = sb("gexp", [P, T])
        gw = sb("gw", [P, T, 4])
        gsel = sb("gsel", [P, T, 2, E])
        gate = sb("gate", [P, T, P])
        b2 = sb("b2", [P, D])
        gate_T = h1[0][:, 0:2, :].rearrange("p a n -> p (a n)")
        maskrow = [nc.alloc_sbuf_tensor_at(f"maskrow{i}", [P, B // 2, S], I32, offset=o) for i, o in enumerate((u_at, w_sq_at))]
        at[0] = mark2
        X1 = cross_buffers("x1", KD, D, h1_at)
        X1["qs"] = sb("x1qs", [P, KD, P])
        X1["pv0"] = sb("x1pv0", [P, N])
        X1["wq"], X1["wkv"], X1["wo"] = xw[:, :, 0, :], None, xw[:, :, 3, :]
        at[0] = mark2
        fxT = [sb(f"fxT{i}", [P, KD, 512], F32R) for i in range(2)]
        fh = [sb(f"fh{i}", [P, 512]) for i in range(2)]
        f0 = [sb(f"f0_{i}", [P, FT, 512], F32R) for i in range(2)]
        f1 = [sb("f1_0", [P, FT, 512], F32R), nc.alloc_sbuf_tensor_at("f1_1", [P, FT, 512], F32R, offset=h1_at)]

        ld = {k: sem("ld_" + k) for k in ("x", "x_rest", "const", "rows", "x0q", "x0k", "x0v", "x0o", "mla", "sq0", "sq1", "xw", "pad", "wg", "b2")}
        ld_ctx = [[sem(f"ld_ctx{l}{i}") for i in range(2)] for l in range(2)]
        ld_e = [sem(f"ld_e{i}") for i in range(2)]
        ld_ff = [sem(f"ld_ff{i}") for i in range(2)]
        setup = sem("setup")
        pool_setup = sem("pool_setup")
        ln_stats, ln_aggr, ln_eps, ln_rstd = (sem(k) for k in ("ln_stats", "ln_aggr", "ln_eps", "ln_rstd"))
        ln_done = sem("ln_done")
        dve_go, act_go, pool_go = sem("dve_go"), sem("act_go"), sem("pool_go")
        rn_stats, rn_aggr, rn_eps, rn_twice, rn_rstd, rn_done = (sem(k) for k in ("rn_stats", "rn_aggr", "rn_eps", "rn_twice", "rn_rstd", "rn_done"))
        stored = sem("stored")

        block = ctx.enter_context(nc.Block())

        def tiles(e, step):
            with e.Fori(0, T // 2 - 1) as i:
                for s in range(2):
                    step(2 * i + s, s, True)
            step(T - 2, 0, True)
            step(T - 1, 1, False)

        def tiles2(e, step):
            with e.Fori(0, T // 2 - 1) as i:
                for s in range(2):
                    step(2 * i + s, s, True, True)
            step(T - 2, 0, True, False)
            step(T - 1, 1, False, False)

        def ln_statistics(dve, srcs, idx):
            dve.sem_inc(dve_go, 1)
            for i, src in enumerate(srcs):
                last = nc.vector.bn_stats(ln_st[:, i, :], src)
            last.then_inc(ln_stats, 1)
            dve.wait_ge(ln_stats, idx + 1)
            dve.sem_inc(dve_go, 1)
            for i in range(len(srcs)):
                last = nc.vector.bn_aggr(ln_mv[:, i, :], ln_st[:, i, :])
            last.then_inc(ln_aggr, 1)

        def ln_rstd_pool(pool, k, idx):
            pool.wait_ge(ln_aggr, idx + 1)
            nc.gpsimd.tensor_tensor(ln_ve[:, 0:k], ln_mv[:, 0:k, 1], eps[:, 0:k], ALU.add).then_inc(ln_eps, 1)
            pool.wait_ge(ln_eps, idx + 1)
            nc.gpsimd.tensor_tensor(ln_rs[:, 0:k], ln_ve[:, 0:k], neghalf[:, 0:k], ALU.pow).then_inc(ln_rstd, 1)

        def ln_apply(dve, srcs, dsts, idx):
            dve.wait_ge(ln_rstd, idx + 1)
            for i, (src, dst) in enumerate(zip(srcs, dsts)):
                last = nc.vector.tensor_scalar(dst, src, ln_mv[:, i, 0:1], ln_rs[:, i:i + 1], ALU.subtract, ALU.mult)
            last.then_inc(ln_done, 1)

        ROW_BASE = {k: i * T for i, k in enumerate(("mla", "ffn", "moe", "x1", "attn", "mlp"))}

        def row_statistics(dve, src, s, idx):
            dve.wait_ge(rn_rstd, idx + 1)
            dve.sem_inc(dve_go, 1)
            nc.vector.bn_stats(rn_st[:, :], src).then_inc(rn_stats, 1)
            dve.wait_ge(rn_stats, idx + 1)
            dve.sem_inc(dve_go, 1)
            nc.vector.bn_aggr(rn_cur[:, s, :], rn_st[:, :]).then_inc(rn_aggr, 1)

        def row_rstd(pool, t, s, phase):
            idx = ROW_BASE[phase] + t
            var, one, tmp = rn_cur[:, s, 1:2], bass.ds(t, 1), rn_tmp[:, s, :]
            pool.wait_ge(rn_aggr, idx + 1)
            nc.gpsimd.tensor_tensor(tmp[:, 0:1], var, eps[:, 0:1], ALU.add).then_inc(rn_eps, 1)
            nc.gpsimd.tensor_copy(rn_mean[:, one], rn_cur[:, s, 0:1])
            pool.wait_ge(rn_eps, idx + 1)
            if phase != "ffn":
                pool.sem_inc(pool_go, 1)
                nc.gpsimd.tensor_tensor(rn_rs[:, one], tmp[:, 0:1], neghalf[:, 0:1], ALU.pow).then_inc(rn_rstd, 1)
                return
            rs, v2, rs2 = tmp[:, 1:2], tmp[:, 2:3], tmp[:, 3:4]
            for i, (dst, p, q, op) in enumerate(((rs, tmp[:, 0:1], neghalf[:, 0:1], ALU.pow), (v2, var, rs, ALU.mult), (v2, v2, rs, ALU.mult),
                                                 (v2, v2, eps[:, 0:1], ALU.add), (rs2, v2, neghalf[:, 0:1], ALU.pow))):
                nc.gpsimd.tensor_tensor(dst, p, q, op).then_inc(rn_twice, 1)
                pool.wait_ge(rn_twice, 5 * t + i + 1)
            pool.sem_inc(pool_go, 1)
            nc.gpsimd.tensor_copy(rn_rs[:, one], rs)
            nc.gpsimd.tensor_tensor(rn_rs2[:, one], rs2, rs, ALU.mult).then_inc(rn_rstd, 1)

        def row_apply(dve, t, src, dsts, phase):
            idx, one = ROW_BASE[phase] + t, bass.ds(t, 1)
            dve.wait_ge(rn_rstd, idx + 3)
            for dst, rs in zip(dsts, (rn_rs, rn_rs2)):
                last = nc.vector.tensor_scalar(dst, src, rn_mean[:, one], rs[:, one], ALU.subtract, ALU.mult)
            last.then_inc(rn_done, 1)

        XS, XF, XT, XV, XY = 0, (2, 3), (4, 5), 6, 7

        def cross(l):
            class c:
                fill_done0 = sem(f"x{l}_fill_done0")
                fill_done1 = sem(f"x{l}_fill_done1")
                fill_free0 = sem(f"x{l}_fill_free0")
                fill_free1 = sem(f"x{l}_fill_free1")
                s_done = sem(f"x{l}_s_done")
                s_free = sem(f"x{l}_s_free")
                max_done = sem(f"x{l}_max_done")
                clip_done = sem(f"x{l}_clip_done")
                exp_done = sem(f"x{l}_exp_done")
                rinv_done = sem(f"x{l}_rinv_done")
                norm_done = sem(f"x{l}_norm_done")
                pT_done0 = sem(f"x{l}_pT_done0")
                pT_done1 = sem(f"x{l}_pT_done1")
                pT_free0 = sem(f"x{l}_pT_free0")
                pT_free1 = sem(f"x{l}_pT_free1")
                p_free = sem(f"x{l}_p_free")
                pv_done = sem(f"x{l}_pv_done")
                pv0_done = sem(f"x{l}_pv0_done")
                pv_free = sem(f"x{l}_pv_free")
                y_done = sem(f"x{l}_y_done")
                y_free = sem(f"x{l}_y_free")
                x_done = sem(f"x{l}_x_done")
                q_spread = sem(f"x{l}_q_spread")

            c.l, c.g, c.next = l, (X0, X1)[l], ("mla", "attn")[l]
            c.fills = ["cT"] * 2 + ["lat"] * 2 + ["q"] * 2 + ["k"] * 8 + ["v"] * 8 if l == 0 else \
                ["lat"] * 2 + ["q"] * 2 + ["cT"] * 2 + ["k"] * 2 + ["v"] * 2
            c.groups = ((0, 8), (8, 14), (14, 18), (18, 22)) if l == 0 else ((0, 4), (4, 8), (8, 9), (9, 10))
            c.per = len(c.fills) // 2
            c.first = {k: c.fills.index(k) for k in ("cT", "lat", "k", "v", "q")}
            c.kg = 8 if l == 0 else KD
            c.fill_done, c.fill_free = (c.fill_done0, c.fill_done1), (c.fill_free0, c.fill_free1)
            c.pT_done, c.pT_free = (c.pT_done0, c.pT_done1), (c.pT_free0, c.pT_free1)
            return c

        X = [cross(0), cross(1)]


        def pe_cross(pe, c):
            g, l = c.g, c.l

            def fill(t, s, j):
                kind, i, bank, m = c.fills[j], j - c.first[c.fills[j]], j % 2, c.per * t + j // 2
                dst = ps[:, XF[bank], :]
                if j == 0:
                    if l == 0:
                        pe.wait_ge(ln_done, 2 * t + 2)
                    else:
                        pe.wait_ge(ld_ctx[1][s], 8 * (t - s) + 16)
                        pe.wait_ge(rn_done, ROW_BASE["x1"] + t + 1)
                if kind == "k" and i == 0:
                    pe.wait_ge(c.fill_free[1], c.per * t + c.first["cT"] // 2 + 2)
                pe.wait_ge(c.fill_free[bank], m + 1)
                if kind == "cT":
                    src = g["cn"] if l == 0 else g["cin"][:, s]
                    for tok in range(4):
                        last = nc.tensor.transpose(dst[:, tok * P:tok * P + P], src[:, tok, i * P:i * P + P], ident)
                elif kind == "lat":
                    last = nc.tensor.transpose(dst[:, 0:P], g["lat"][:, i * P:i * P + P], ident)
                elif kind == "k":
                    for k in range(KD):
                        w = g["wkv"][:, k, i * P:i * P + P] if l == 0 else xw[:, k, 1, i * P:i * P + P]
                        last = nc.tensor.matmul(dst, w, g["cT"][:, k, :], start=(k == 0), stop=(k == KD - 1))
                elif kind == "v":
                    if l == 0:
                        tok, half = i // 2, i % 2
                        for k in range(KD):
                            last = nc.tensor.matmul(dst, g["cT"][:, k, tok * P:tok * P + P],
                                                    g["wkv"][:, k, INNER + half * 512:INNER + half * 512 + 512],
                                                    start=(k == 0), stop=(k == KD - 1))
                    else:
                        for tok in (2 * i, 2 * i + 1):
                            for k in range(KD):
                                last = nc.tensor.matmul(dst[:, (tok % 2) * D:(tok % 2) * D + D], g["cT"][:, k, tok * P:tok * P + P],
                                                        xw[:, k, 2, :], start=(k == 0), stop=(k == KD - 1))
                else:
                    if i == 0:
                        pe.wait_ge(c.fill_free[1], c.per * t + c.first["lat"] // 2 + 2)
                    for j4 in range(4 if l == 0 else 1):
                        grp = 4 * i + j4 if l == 0 else i
                        for k in range(KD):
                            last = nc.tensor.matmul(dst[:, j4 * P:j4 * P + P], g["wq"][:, k, grp * P:grp * P + P], g["latT"][:, k, :],
                                                    start=(k == 0), stop=(k == KD - 1))
                last.then_inc(c.fill_done[bank], 1)

            def scores(t, s, un):
                n, b, hf = 4 * t + un, un // 2, un % 2
                if un == 0:
                    for bank in range(2):
                        pe.wait_ge(c.fill_free[bank], c.per * t + c.first["v"] // 2 + 1)
                    if l == 1:
                        pe.wait_ge(c.q_spread, 2 * t + 2)
                pe.wait_ge(c.s_free if l == 0 else c.exp_done, n + 1)
                if l == 1:
                    for two in range(2):
                        nc.tensor.matmul(ps[:, XS + two, :], row0b[:, :],
                                         pad2(t, b), start=True, stop=False, skip_group_check=True)
                for j in range(4):
                    p = 4 * hf + j
                    last = nc.tensor.matmul(ps[:, XS + j // 2, (j % 2) * S:(j % 2) * S + S], g["qbd"][s][:, b, p, :],
                                            g["kT"][s][:, p if l == 0 else hf, b * S:b * S + S],
                                            start=(l == 0), stop=True, skip_group_check=True)
                last.then_inc(c.s_done, 1)

            def pad2(t, b):
                one = padneg[:, bass.ds(2 * t + b, 1), :]
                return one.broadcast_to((P, 2, S))

            def transposed(t, un):
                n = 4 * t + un
                pe.wait_ge(c.norm_done, n + 1)
                for bank in range(2):
                    pe.wait_ge(c.pT_free[bank], n + 1)
                    for i in range(4):
                        j, kt = 2 * bank + i // 2, i % 2
                        last = nc.tensor.transpose(ps[:, XT[bank], i * P:i * P + P], g["p"][un % 2][:, j, kt * P:kt * P + P], ident)
                    last.then_inc(c.pT_done[bank], 1)

            def values(t, s, un):
                n, b, hf = 4 * t + un, un // 2, un % 2
                for bank in range(2):
                    if un == 0:
                        pe.wait_ge(c.fill_free[bank], c.per * (t + 1) + 1)
                    pe.wait_ge(c.pT_free[bank], n + 2)
                pe.wait_ge(c.pv_free, n + 1)
                for j in range(4):
                    p = 4 * hf + j
                    for kt in range(2):
                        if l == 0:
                            dst, w = ps[:, XV, j * P:j * P + P], g["v"][s][:, 2 * b + kt, p * P:p * P + P]
                        else:
                            dst, w = ps[32 * j:32 * j + 32, XV, 0:P], g["v"][s][:, 2 * b + kt, p * 32:p * 32 + 32]
                        last = nc.tensor.matmul(dst, w, g["pT"][un % 2][:, 2 * j + kt, :], start=(kt == 0), stop=(kt == 1))
                last.then_inc(c.pv_done, 1)

            def project(t):
                pe.wait_ge(c.y_free, t + 1)
                pe.wait_ge(c.pv_free, 4 * t + 5)
                for k in range(c.kg):
                    last = nc.tensor.matmul(ps[:, XY, 0:D], g["attT"][:, k, :], g["wo"][:, k, :], start=(k == 0), stop=(k == c.kg - 1))
                last.then_inc(c.y_done, 1)

            if l == 1:
                pe.wait_ge(ld["xw"], 64)
                pe.wait_ge(MO.pad, 2)
            for j in range(len(c.fills)):
                if l == 0 and c.fills[j] in "qkv" and j == c.first[c.fills[j]]:
                    pe.wait_ge(ld["x0" + c.fills[j]], 16)
                fill(0, 0, j)
            scores(0, 0, 0)
            scores(0, 0, 1)
            if l == 0:
                pe.wait_ge(ld["x0o"], 16)

            def step(t, s, nxt):
                for un in range(4):
                    transposed(t, un)
                    if un < 2:
                        scores(t, s, un + 2)
                    elif nxt:
                        scores(t + 1, 1 - s, un - 2)
                    values(t, s, un)
                    if nxt:
                        for j in range(*c.groups[un]):
                            fill(t + 1, 1 - s, j)
                project(t)

            tiles(pe, step)

        def evacuate(eng, c, t, s, j):
            g, l = c.g, c.l
            kind, i, bank, m = c.fills[j], j - c.first[c.fills[j]], j % 2, c.per * t + j // 2
            src = ps[:, XF[bank], :]

            def put(dst, src, scale=None, bias=None):
                if bank == 0:
                    if scale is None and bias is None:
                        return nc.scalar.activation(dst, src, ACT.Copy)
                    return nc.scalar.activation(dst, src, ACT.Identity, bias=bias, scale=1.0 if scale is None else scale)
                if scale is None and bias is None:
                    return nc.vector.tensor_copy(dst, src)
                if scale is None:
                    return nc.vector.tensor_scalar(dst, src, bias, None, ALU.add)
                return nc.vector.tensor_scalar(dst, src, scale, bias, ALU.mult, ALU.add)

            eng.wait_ge(c.fill_done[bank], m + 1)
            if kind == "cT":
                last = put(g["cT"][:, i, :], src, vec("ln_c_w", i), vec("ln_c_b", i)) if l == 0 else put(g["cT"][:, i, :], src)
            elif kind == "lat":
                last = put(g["latT"][:, i, :], src[:, 0:P], vec("ln_l_w", i), vec("ln_l_b", i)) if l == 0 else put(g["latT"][:, i, :], src[:, 0:P])
            elif kind == "k":
                last = put(g["kT"][s][:, i, :], src) if l == 0 else put(g["kT"][s][:, i, :], src, None, vec("xbk", i))
            elif kind == "v":
                if l == 0:
                    last = put(g["v"][s][:, i // 2, (i % 2) * 512:(i % 2) * 512 + 512], src)
                else:
                    last = put(g["v"][s][:, 2 * i:2 * i + 2, :], src)
            elif l == 0:
                for par in range(2):
                    r = slice(64 * par, 64 * par + 64)
                    last = put(g["qbd"][s][r, :, 4 * i:4 * i + 4, 64 * par:64 * par + 64].rearrange("p b j n -> p j b n"),
                               src[r, :].rearrange("p (j b n) -> p j b n", j=4, b=2))
            else:
                last = put(g["qs"][:, i, :], src[:, 0:P], None, vec("xbq", i))
            last.then_inc(c.fill_free[bank], 1)

        def act_cross(act, c):
            g, l = c.g, c.l

            def exps(t, un):
                n, slot = 4 * t + un, un % 2
                act.wait_ge(c.clip_done, n + 1)
                for j in range(4):
                    if l == 0:
                        last = nc.scalar.activation(g["p"][slot][:, j, :], g["p"][slot][:, j, :], ACT.Exp, scale=64.0 ** -0.5,
                                                    accum_out=g["sum"][:, slot, j:j + 1])
                    else:
                        if j == 0:
                            act.wait_ge(c.p_free, n + 1)
                        last = nc.scalar.activation(g["p"][slot][:, j, :], ps[:, XS + j // 2, (j % 2) * S:(j % 2) * S + S], ACT.Exp,
                                                    bias=g["nmax"][:, slot, j:j + 1], scale=0.25, accum_out=g["sum"][:, slot, j:j + 1])
                last.then_inc(c.exp_done, 1)

            def move_pT(t, un):
                n = 4 * t + un
                act.wait_ge(c.pT_done[0], n + 1)
                nc.scalar.activation(g["pT"][un % 2][:, 0:4, :], ps[:, XT[0], :], ACT.Copy).then_inc(c.pT_free[0], 1)

            act.sem_inc(c.fill_free[0], 1)
            act.sem_inc(c.pT_free[0], 1)
            if l == 1:
                act.sem_inc(c.exp_done, 1)
            for j in range(0, len(c.fills), 2):
                evacuate(act, c, 0, 0, j)
            exps(0, 0)
            exps(0, 1)

            def step(t, s, nxt):
                for un in range(4):
                    move_pT(t, un)
                    todo = [j for j in range(*c.groups[un]) if j % 2 == 0] if nxt else []
                    early = 1 if l == 0 or un < 2 else 0
                    for j in todo[:early]:
                        evacuate(act, c, t + 1, 1 - s, j)
                    if un < 2:
                        exps(t, un + 2)
                    elif nxt:
                        exps(t + 1, un - 2)
                    for j in todo[early:]:
                        evacuate(act, c, t + 1, 1 - s, j)

            tiles(act, step)

        def dve_cross(dve, c):
            g, l = c.g, c.l

            def norm(t, s, part):
                xt = x[:, bass.ds(t, 1), :].rearrange("p a d -> p (a d)")
                if l == 0:
                    srcs = [g["cin"][:, s, k, :] for k in range(4)] + [xt]
                    dsts = [g["cn"][:, k, :] for k in range(4)] + [g["lat"][:, :]]
                    if part == 0:
                        dve.wait_ge(ld_ctx[0][s], 8 * (t - s) + 16)
                        ln_statistics(dve, srcs, 2 * t)
                    elif part == 1:
                        ln_apply(dve, srcs, dsts, 2 * t)
                        dve.wait_ge(ln_done, 2 * t + 1)
                        ln_statistics(dve, [g["lat"][:, :]], 2 * t + 1)
                    else:
                        ln_apply(dve, [g["lat"][:, :]], [g["lat"][:, :]], 2 * t + 1)
                elif part == 1:
                    row_apply(dve, t, xt, [g["lat"][:, :]], "x1")

            def spread_q(t, s):
                for i in range(KD):
                    if i == 0:
                        for bank in range(2):
                            dve.wait_ge(c.fill_free[bank], c.per * t + c.first["q"] // 2 + 2)
                    q = g["qs"][:, i, :].rearrange("p (b n) -> p b n", b=2)
                    for b in range(2):
                        last = nc.vector.tensor_tensor(g["qbd"][s][:, b, 4 * i:4 * i + 4, :].rearrange("p j (a n) -> p (j a) n", a=2),
                                                q[:, b:b + 1, :].broadcast_to((P, 8, N)),
                                                head_of.rearrange("p (h o) -> p h o", o=1).broadcast_to((P, 8, N)), ALU.mult)
                    last.then_inc(c.q_spread, 1)

            def read_scores(t, un):
                n, slot = 4 * t + un, un % 2
                dve.wait_ge(c.s_done, n + 1)
                sc = ps[:, XS:XS + 2, :].rearrange("p a (j k) -> p (a j) k", j=2)
                if l == 0:
                    nc.vector.tensor_scalar(g["p"][slot][:, :, :], sc, 11.0 * 8.0, -11.0 * 8.0, ALU.min, ALU.max).then_inc(c.clip_done, 1)
                    dve.wait_ge(c.clip_done, n + 1)
                    dve.sem_inc(c.s_free, 1)
                else:
                    nc.vector.tensor_reduce(g["sum"][:, slot, :], sc, AX_X, ALU.max).then_inc(c.max_done, 1)
                    dve.wait_ge(c.max_done, n + 1)
                    nc.vector.tensor_scalar(g["nmax"][:, slot, :], g["sum"][:, slot, :], -0.25, None, ALU.mult).then_inc(c.clip_done, 1)

            def invert(t, un):
                n, slot = 4 * t + un, un % 2
                dve.wait_ge(c.exp_done, n + 1 + l)
                nc.vector.reciprocal(g["rinv"][:, slot, :], g["sum"][:, slot, :]).then_inc(c.rinv_done, 1)

            def move_pT(t, un):
                n = 4 * t + un
                dve.wait_ge(c.pT_done[1], n + 1)
                dve.sem_inc(c.p_free, 1)
                nc.vector.tensor_copy(g["pT"][un % 2][:, 4:8, :], ps[:, XT[1], :]).then_inc(c.pT_free[1], 1)

            def pick(t, un):
                n, b, hf = 4 * t + un, un // 2, un % 2
                dve.wait_ge(c.pv_done, n + 1)
                cols = slice(64 * b, 64 * b + 64)
                if l == 0:
                    for par in range(2):
                        r = slice(64 * par, 64 * par + 64)
                        last = nc.vector.tensor_copy(g["attT"][r, 4 * hf:4 * hf + 4, cols],
                                                     ps[r, XV, :].rearrange("p (j m) -> p j m", j=4)[:, :, 64 * par:64 * par + 64])
                else:
                    nc.vector.tensor_scalar(g["pv0"][:, :], ps[:, XV, 0:N], par_of[:, 0:1], vec("xbv", hf), ALU.mult, ALU.add).then_inc(c.pv0_done, 1)
                    dve.wait_ge(c.pv0_done, n + 1)
                    last = nc.vector.scalar_tensor_tensor(g["attT"][:, hf, cols], ps[:, XV, N:2 * N], par_of[:, 1:2], g["pv0"][:, :], ALU.mult, ALU.add)
                last.then_inc(c.pv_free, 1)

            def residual(t, s):
                xt = x[:, bass.ds(t, 1), :].rearrange("p a d -> p (a d)")
                dve.wait_ge(c.y_done, t + 1)
                nc.vector.tensor_tensor(xt, ps[:, XY, 0:D], xt, ALU.add).then_inc(c.y_free, 1)
                dve.wait_ge(c.y_free, t + 2)
                nc.vector.tensor_tensor(xt, xt, rows[:, 0 if l == 0 else 2, :], ALU.add).then_inc(c.x_done, 1)
                dve.wait_ge(c.x_done, t + 1)
                row_statistics(dve, xt, s, ROW_BASE[c.next] + t)

            if l == 0:
                dve.sem_inc(rn_rstd, 2)
            for k, v in ((c.fill_free[1], 1), (c.s_free, 1), (c.pT_free[1], 1), (c.pv_free, 1), (c.y_free, 1), (c.p_free, 2)):
                dve.sem_inc(k, v)
            if l == 0:
                for s in range(2):
                    nc.vector.memset(g["qbd"][s][:, :, :, :], 0.0).then_inc(c.q_spread, 1)
                dve.wait_ge(c.q_spread, 2)
            for part in range(3):
                norm(0, 0, part)
            for j in range(1, len(c.fills), 2):
                evacuate(dve, c, 0, 0, j)
            if l == 1:
                spread_q(0, 0)
            read_scores(0, 0)
            dve.wait_ge(c.fill_done[0], 2)
            dve.wait_ge(c.fill_done[1], 2)
            for part in range(3):
                norm(1, 1, part)
            invert(0, 0)
            read_scores(0, 1)
            if l == 0:
                dve.wait_ge(ld["x_rest"], 16)
                dve.wait_ge(ld["rows"], 16)

            def step(t, s, nxt, more):
                for un in range(4):
                    move_pT(t, un)
                    if un < 3:
                        invert(t, un + 1)
                    elif nxt:
                        invert(t + 1, 0)
                    if un < 2:
                        read_scores(t, un + 2)
                    elif nxt:
                        read_scores(t + 1, un - 2)
                    pick(t, un)
                    if nxt:
                        for j in range(*c.groups[un]):
                            if j % 2 == 1:
                                evacuate(dve, c, t + 1, 1 - s, j)
                    if l == 1 and nxt and un == 1:
                        spread_q(t + 1, 1 - s)
                    if more and un < 3:
                        if un == 1:
                            dve.wait_ge(c.fill_done[0], c.per * (t + 1) + 2)
                            dve.wait_ge(c.fill_done[1], c.per * (t + 1) + 2)
                        norm(t + 2, s, un)
                residual(t, s)

            tiles2(dve, step)

        def pool_cross(pool, c):
            g, l = c.g, c.l

            def norm(t, part):
                if l == 0:
                    ln_rstd_pool(pool, (5, 1)[part], 2 * t + part)

            def scale_p(t, un):
                n, slot = 4 * t + un, un % 2
                pool.wait_ge(c.rinv_done, n + 1)
                nc.gpsimd.tensor_tensor(g["p"][slot][:, :, :], g["p"][slot][:, :, :],
                                        g["rinv"][:, slot, :].rearrange("p (j o) -> p j o", o=1).broadcast_to((P, 4, S)),
                                        ALU.mult).then_inc(c.norm_done, 1)

            norm(0, 0)
            norm(0, 1)
            norm(1, 0)
            norm(1, 1)
            scale_p(0, 0)
            with pool.Fori(0, T // 2 - 1) as i:
                for s in range(2):
                    t = 2 * i + s
                    scale_p(t, 1)
                    norm(t + 2, 0)
                    scale_p(t, 2)
                    norm(t + 2, 1)
                    scale_p(t, 3)
                    scale_p(t + 1, 0)
                    row_rstd(pool, t, s, c.next)
            for un in range(1, 8):
                scale_p(T - 2 + un // 4, un % 4)
                if un == 4:
                    row_rstd(pool, T - 2, 0, c.next)
            row_rstd(pool, T - 1, 1, c.next)

        y_at = ctx_views(a["ctx_1024"])

        LAYERS, NEXT = ("mla", "ffn", "attn"), ("ffn", "moe", "mlp")
        class SA:
            hT_ps = sem("sa_hT_ps")
            hT = sem("sa_hT")
            lat_ps = sem("sa_lat_ps")
            lat = sem("sa_lat")
            rope_ps = sem("sa_rope_ps")
            roped0 = sem("sa_roped0")
            roped1 = sem("sa_roped1")
            rope = sem("sa_rope")
            qk_ps = sem("sa_qk_ps")
            q_ps = sem("sa_q_ps")
            q = sem("sa_q")
            k_ps = sem("sa_k_ps")
            v_ps = sem("sa_v_ps")
            kbd = sem("sa_kbd")
            vbd = sem("sa_vbd")
            s_ps = sem("sa_s_ps")
            max = sem("sa_max")
            sub = sem("sa_sub")
            exp = sem("sa_exp")
            sum = sem("sa_sum")
            rinv = sem("sa_rinv")
            norm = sem("sa_norm")
            pT_ps = sem("sa_pT_ps")
            pT = sem("sa_pT")
            att_ps = sem("sa_att_ps")
            att = sem("sa_att")
            y_ps = sem("sa_y_ps")
            y_free = sem("sa_y_free")
            x_done = sem("sa_x_done")

        def pe_self(pe, L):
            sq = w_sq[0 if L == 1 else 1]
            g0, v_bank = T * L, 1 if L == 0 else 2

            def rows_T(t):
                pe.wait_ge(rn_done, ROW_BASE[LAYERS[L]] + t + 1)
                if not isinstance(t, int) or t > 0:
                    pe.wait_ge(SA.q, g0 + t)
                for k in range(KD):
                    last = nc.tensor.transpose(ps[:, 0, k * P:k * P + P], h[:, k * P:k * P + P], ident)
                last.then_inc(SA.hT_ps, 1)

            def project_qk(t):
                g = g0 + t
                pe.wait_ge(SA.hT, g + 1)
                if L == 0:
                    for k in range(KD):
                        last = nc.tensor.matmul(ps[:, 0, 256:384], w_mla[:, k, 0:P], hT[:, k, :], start=(k == 0), stop=(k == 1))
                    last.then_inc(SA.lat_ps, 1)
                    for i in range(4):
                        for k in range(KD):
                            last = nc.tensor.matmul(ps[:, 2, i * P:i * P + P], w_mla[:, k, P + i * P:2 * P + i * P], hT[:, k, :],
                                                    start=(k == 0), stop=(k == 1))
                    last.then_inc(SA.rope_ps, 1)
                    pe.wait_ge(SA.lat, g + 1)
                    nc.tensor.matmul(ps[:, 0, 384:512], w_mlac[:, 0:P], cqkvT[:, :], start=True, stop=True)
                    nc.tensor.matmul(ps[:, 0, 0:P], w_mlac[:, P:2 * P], cqkvT[:, :], start=True, stop=True).then_inc(SA.q_ps, 1)
                else:
                    for bank, at0, w, done in ((1, 0, 1, SA.k_ps), (0, 256, 0, SA.q_ps)):
                        for i in range(KD):
                            for k in range(KD):
                                last = nc.tensor.matmul(ps[:, bank, at0 + i * P:at0 + i * P + P], sq[:, k, w, i * P:i * P + P], hT[:, k, :],
                                                        start=(k == 0), stop=(k == 1))
                        last.then_inc(done, 1)

            def project_v(t):
                g = g0 + t
                pe.wait_ge(SA.vbd, g + 1)
                ks = 1 if L == 0 else KD
                for b in range(2):
                    for k in range(ks):
                        for par in range(2):
                            w = w_mlac[:, 2 * P:2 * P + D] if L == 0 else sq[:, k, 2, :]
                            v_in = cqkvT[:, 64 * b:64 * b + 64] if L == 0 else hT[:, k, 64 * b:64 * b + 64]
                            last = nc.tensor.matmul(ps[64 * par:64 * par + 64, v_bank, 256 + P * b:256 + P * b + P], v_in,
                                                    w.rearrange("p (j a d) -> p a j d", a=2, d=16)[:, par, :, :],
                                                    start=(k == 0), stop=(k == ks - 1), skip_group_check=True)
                last.then_inc(SA.v_ps, 1)

            def scores(t):
                g = g0 + t
                pe.wait_ge(SA.q, g + 1)
                pe.wait_ge(SA.kbd, g + 1)
                for hf in range(KD):
                    if L != 1:
                        nc.tensor.matmul(ps[:, 3 + hf, :], identb[:, :], causalb[:, :].rearrange("p (o n) -> p o n", o=1).broadcast_to((P, 8, N)),
                                         start=True, stop=False, skip_group_check=True)
                    for b in range(2):
                        last = nc.tensor.matmul(ps[64 * b:64 * b + 64, 3 + hf, :], qT[:, hf, 64 * b:64 * b + 64],
                                                kbd[:, hf, b, :, :].rearrange("p h n -> p (h n)"), start=(L == 1), stop=True, skip_group_check=True)
                last.then_inc(SA.s_ps, 1)

            def probs_T(t):
                g = g0 + t
                pe.wait_ge(SA.norm, g + 1)
                for j in range(8):
                    last = nc.tensor.transpose(ps[:, 5 + j // 4, (j % 4) * P:(j % 4) * P + P],
                                               pr[:, 2 * j:2 * j + 2, :].rearrange("p h n -> p (h n)"), ident)
                last.then_inc(SA.pT_ps, 1)

            def values(t, s):
                g = g0 + t
                pe.wait_ge(SA.pT, g + 1)
                pe.wait_ge(SA.vbd, g + 2)
                pe.wait_ge(SA.y_free, g + 1)
                for j in range(8):
                    for b in range(2):
                        last = nc.tensor.matmul(ps[32 * (j % 4):32 * (j % 4) + 32, 7, (j // 4) * P + 64 * b:(j // 4) * P + 64 * b + 64],
                                                vbd[s][:, b, j, :, :].rearrange("p a d -> p (a d)"), prT[:, j, 64 * b:64 * b + 64],
                                                start=True, stop=True, skip_group_check=True)
                last.then_inc(SA.att_ps, 1)

            def output(t):
                g = g0 + t
                pe.wait_ge(SA.att, g + 1)
                for k in range(KD):
                    w = w_mlao[:, k, :] if L == 0 else sq[:, k, 3, :]
                    last = nc.tensor.matmul(ps[:, 7, 256:512], sattT[:, k, :], w, start=(k == 0), stop=(k == 1))
                last.then_inc(SA.y_ps, 1)

            pe.wait_ge(ld["mla"] if L == 0 else ld["sq0"] if L == 1 else ld["sq1"], 160 if L == 0 else 64)
            pe.wait_ge(setup, 5)
            rows_T(0)
            project_qk(0)
            project_v(0)
            rows_T(1)
            scores(0)
            project_qk(1)
            project_v(1)

            def step(t, s, nxt, more):
                probs_T(t)
                if nxt:
                    scores(t + 1)
                values(t, s)
                output(t)
                if more:
                    rows_T(t + 2)
                    project_qk(t + 2)
                    project_v(t + 2)

            tiles2(pe, step)

        def act_self(act, L):
            g0 = T * L

            def rows_T(t):
                act.wait_ge(SA.hT_ps, g0 + t + 1)
                if L == 1:
                    for k in range(KD):
                        last = nc.scalar.activation(hT[:, k, :], ps[:, 0, k * P:k * P + P], ACT.Identity, bias=vec("ln1_b", k), scale=vec("ln1_g", k))
                else:
                    last = nc.scalar.activation(hT[:, :, :], ps[:, 0, 0:256], ACT.Copy)
                last.then_inc(SA.hT, 1)

            def latent(t):
                act.wait_ge(SA.lat_ps, g0 + t + 1)
                nc.scalar.activation(cqkvT[:, :], ps[:, 0, 256:384], ACT.Gelu, bias=vec("bqkv")).then_inc(SA.lat, 1)

            def project(t):
                g = g0 + t
                act.wait_ge(SA.q_ps, g + 1)
                if L == 0:
                    nc.scalar.activation(qT[:, 0, :], ps[:, 0, 384:512], ACT.Gelu, bias=vec("bqc"))
                    nc.scalar.activation(kTs[:, 0, :], ps[:, 0, 0:P], ACT.Gelu, bias=vec("bkc"))
                    act.wait_ge(SA.rope, g + 1)
                    nc.scalar.activation(qT[:, 1, :], rope[:, 0, :], ACT.Gelu)
                    nc.scalar.activation(kTs[:, 1, :], rope[:, 2, :], ACT.Gelu).then_inc(SA.q, 1)
                else:
                    nc.scalar.activation(qT[:, :, :], ps[:, 0, 256:512], ACT.Copy).then_inc(SA.q, 1)

            def exps(t):
                act.wait_ge(SA.sub, g0 + t + 1)
                nc.scalar.activation(pr[:, :, :], pr[:, :, :], ACT.Exp, scale=0.25).then_inc(SA.exp, 1)

            def probs_T(t):
                act.wait_ge(SA.pT_ps, g0 + t + 1)
                for i in range(2):
                    last = nc.scalar.activation(prT[:, 4 * i:4 * i + 4, :], ps[:, 5 + i, :], ACT.Copy)
                last.then_inc(SA.pT, 1)

            def spread_v(t, s):
                act.wait_ge(SA.v_ps, g0 + t + 1)
                v = ps[:, 1 if L == 0 else 2, 256:512].rearrange("p (b j d) -> p b j d", b=2, j=8)
                for par in range(2):
                    r = slice(64 * par, 64 * par + 64)
                    last = nc.scalar.activation(vbd[s][r, :, :, par, :], v[r, :, :, :], ACT.Copy)
                last.then_inc(SA.vbd, 1)

            def attention(t):
                act.wait_ge(SA.att_ps, g0 + t + 1)
                if L == 0:
                    for k in range(KD):
                        last = nc.scalar.activation(sattT[:, k, :], ps[:, 7, k * P:k * P + P], ACT.Identity, bias=vec("bv0", k))
                else:
                    last = nc.scalar.activation(sattT[:, :, :], ps[:, 7, 0:256], ACT.Copy)
                last.then_inc(SA.att, 1)

            if L == 0:
                act.sem_inc(SA.vbd, 1)
                act.wait_ge(setup, 5)
            for t in range(2):
                rows_T(t)
                if L == 0:
                    latent(t)
                project(t)
                spread_v(t, t)
                if t == 0:
                    exps(t)

            def step(t, s, nxt, more):
                probs_T(t)
                attention(t)
                if nxt:
                    exps(t + 1)
                if more:
                    rows_T(t + 2)
                    if L == 0:
                        latent(t + 2)
                    project(t + 2)
                    spread_v(t + 2, s)

            tiles2(act, step)

        def dve_self(dve, L, x_sem, x_val):
            g0 = T * L

            def norm(t):
                xt = x[:, bass.ds(t, 1), :].rearrange("p a d -> p (a d)")
                ut = u[:, bass.ds(t, 1), :].rearrange("p a d -> p (a d)")
                if not isinstance(t, int) or g0 + t > 0:
                    dve.wait_ge(SA.hT_ps, g0 + t)
                row_apply(dve, t, xt, [ut, h[:, :]] if L == 1 else [h[:, :]], LAYERS[L])

            def rotate(t):
                g = g0 + t
                dve.wait_ge(SA.rope_ps, g + 1)
                cos, sin = cst[:, C_COS:C_COS + P], cst[:, C_SIN:C_SIN + P]
                for i, (bias, tab) in enumerate((("bqr", cos), ("bqs", sin), ("bkr", cos), ("bks", sin))):
                    last = nc.vector.scalar_tensor_tensor(rope[:, i, :], ps[:, 2, i * P:i * P + P], vec(bias), tab, ALU.add, ALU.mult)
                last.then_inc(SA.roped0, 1)
                dve.wait_ge(SA.roped0, g + 1)
                nc.vector.tensor_tensor(rope[:, 0, :], rope[:, 0, :], rope[:, 1, :], ALU.add)
                nc.vector.tensor_tensor(rope[:, 2, :], rope[:, 2, :], rope[:, 3, :], ALU.add).then_inc(SA.rope, 1)

            def spread_k(t):
                if L == 0:
                    dve.wait_ge(SA.q, g0 + t + 1)
                else:
                    dve.wait_ge(SA.k_ps, g0 - T + t + 1)
                for hf in range(KD):
                    for b in range(2):
                        src = kTs[:, hf, 64 * b:64 * b + 64] if L == 0 else ps[:, 1, hf * P + 64 * b:hf * P + 64 * b + 64]
                        last = nc.vector.tensor_tensor(kbd[:, hf, b, :, :], src.rearrange("p (o n) -> p o n", o=1).broadcast_to((P, 8, N)),
                                                       head_of.rearrange("p (h o) -> p h o", o=1).broadcast_to((P, 8, N)), ALU.mult)
                last.then_inc(SA.kbd, 1)

            def softmax_a(t):
                g = g0 + t
                sc = ps[:, 3:5, :].rearrange("p a (h n) -> p (a h) n", n=N)
                dve.wait_ge(SA.s_ps, g + 1)
                nc.vector.tensor_reduce(smax[:, :], sc, AX_X, ALU.max).then_inc(SA.max, 1)
                dve.wait_ge(SA.max, g + 1)
                nc.vector.tensor_tensor(pr[:, :, :], sc, smax[:, :].rearrange("p (h o) -> p h o", o=1).broadcast_to((P, H, N)),
                                        ALU.subtract).then_inc(SA.sub, 1)

            def softmax_b(t):
                g = g0 + t
                dve.wait_ge(SA.exp, g + 1)
                nc.vector.tensor_reduce(ssum[:, :], pr[:, :, :], AX_X, ALU.add).then_inc(SA.sum, 1)
                dve.wait_ge(SA.sum, g + 1)
                nc.vector.reciprocal(srinv[:, :], ssum[:, :]).then_inc(SA.rinv, 1)

            def residual(t, s):
                g = g0 + t
                xt = x[:, bass.ds(t, 1), :].rearrange("p a d -> p (a d)")
                ut = u[:, bass.ds(t, 1), :].rearrange("p a d -> p (a d)")
                dve.wait_ge(SA.y_ps, g + 1)
                first = ut if L == 1 else xt
                nc.vector.tensor_tensor(first, ps[:, 7, 256:512], first, ALU.add).then_inc(SA.y_free, 1)
                dve.wait_ge(SA.y_free, g + 2)
                if L == 0:
                    nc.vector.tensor_tensor(xt, xt, rows[:, 1, :], ALU.add).then_inc(SA.x_done, 1)
                elif L == 2:
                    dve.sem_inc(SA.x_done, 1)
                if L == 0:
                    dve.wait_ge(SA.x_done, g + 1)
                row_statistics(dve, ut if L == 1 else xt, s, ROW_BASE[NEXT[L]] + t)

            dve.wait_ge(x_sem, x_val)
            if L == 0:
                dve.sem_inc(SA.y_free, 1)
                for s in range(2):
                    nc.vector.memset(vbd[s][:, :, :, :, :], 0.0).then_inc(setup, 1)

            for t in range(2):
                norm(t)
                if t == 1:
                    softmax_a(0)
                if L == 0:
                    rotate(t)
                spread_k(t)
                if t == 1:
                    softmax_b(0)

            def step(t, s, nxt, more):
                if nxt:
                    softmax_a(t + 1)
                if more:
                    norm(t + 2)
                if nxt:
                    softmax_b(t + 1)
                if more:
                    if L == 0:
                        rotate(t + 2)
                    spread_k(t + 2)
                residual(t, s)

            tiles2(dve, step)

        def pool_self(pool, L):
            def scale_p(t):
                pool.wait_ge(SA.rinv, T * L + t + 1)
                nc.gpsimd.tensor_tensor(pr[:, :, :], pr[:, :, :], srinv[:, :].rearrange("p (h o) -> p h o", o=1).broadcast_to((P, H, N)),
                                        ALU.mult).then_inc(SA.norm, 1)

            def add_u(t):
                xt = x[:, bass.ds(t, 1), :].rearrange("p a d -> p (a d)")
                ut = u[:, bass.ds(t, 1), :].rearrange("p a d -> p (a d)")
                pool.wait_ge(SA.y_free, T * L + t + 2)
                pool.sem_inc(pool_go, 1)
                nc.gpsimd.tensor_tensor(xt, xt, ut, ALU.add).then_inc(SA.x_done, 1)

            def step(t, s, nxt):
                if nxt:
                    scale_p(t + 1)
                if L == 1:
                    add_u(t)
                row_rstd(pool, t, s, NEXT[L])

            scale_p(0)
            tiles(pool, step)

        class MO:
            mT_ps = sem("mo_mT_ps")
            mT = sem("mo_mT")
            router_ps = sem("mo_router_ps")
            logit = sem("mo_logit")
            top = sem("mo_top")
            topi = sem("mo_topi")
            diff = sem("mo_diff")
            exp = sem("mo_exp")
            w = sem("mo_w")
            sel = sem("mo_sel")
            gate = sem("mo_gate")
            gT_ps = sem("mo_gT_ps")
            gT = sem("mo_gT")
            b2_ps = sem("mo_b2_ps")
            b2 = sem("mo_b2")
            w1_ps = sem("mo_w1_ps")
            w1_free = sem("mo_w1_free")
            w2_ps = sem("mo_w2_ps")
            w2_free = sem("mo_w2_free")
            pad = sem("mo_pad")

        def pe_moe(pe):
            def rows_T(t, s):
                pe.wait_ge(rn_done, ROW_BASE["moe"] + t + 1)
                pe.wait_ge(MO.mT, t + 1)
                for k in range(KD):
                    last = nc.tensor.transpose(ps[:, s, k * P:k * P + P], h[:, k * P:k * P + P], ident)
                last.then_inc(MO.mT_ps, 1)

            tiles(pe, lambda t, s, nxt: rows_T(t, s))
            pe.wait_ge(MO.mT, T + 2)
            pe.wait_ge(ld["wg"], 16)
            for t in range(T):
                for k in range(KD):
                    last = nc.tensor.matmul(ps[:, 2 + t // 4, (t % 4) * P:(t % 4) * P + P], mT[:, k, t * P:t * P + P], wg[:, k, :],
                                            start=(k == 0), stop=(k == 1), skip_group_check=True)
            last.then_inc(MO.router_ps, 1)
            pe.wait_ge(MO.gate, 1)
            for t in range(T):
                last = nc.tensor.transpose(ps[:, t // 4, (t % 4) * P:(t % 4) * P + P], gate[:, t, :], ident)
            last.then_inc(MO.gT_ps, 1)
            pe.wait_ge(MO.gT, 1)
            pe.wait_ge(ld["b2"], 16)
            for t in range(T):
                last = nc.tensor.matmul(ps[:, 4 + t // 2, (t % 2) * D:(t % 2) * D + D], gate_T[:, t * P:t * P + P], b2[:, :],
                                        start=True, stop=True, skip_group_check=True)
            last.then_inc(MO.b2_ps, 1)

            def hidden(e, s, c):
                if c == 0:
                    pe.wait_ge(ld_e[s], 16 * (e - s) + 32)
                for f in range(FT):
                    pe.wait_ge(MO.w1_free, 16 * e + 8 * c + f + 1)
                    for k in range(KD):
                        last = nc.tensor.matmul(ps[:, f % 4, :], ew1[s][:, k, f * P:f * P + P], mT[:, k, 512 * c:512 * c + 512],
                                                start=(k == 0), stop=(k == 1))
                    last.then_inc(MO.w1_ps, 1)

            def outputs(e, s, c):
                pe.wait_ge(MO.w1_free, 16 * e + 8 * c + 8 + 4)
                for i in range(4):
                    pe.wait_ge(MO.w2_free, 8 * e + 4 * c + i + 1)
                    for f in range(FT):
                        last = nc.tensor.matmul(ps[:, 4 + i, 0:D], h1[c][:, f, i * P:i * P + P], ew2[s][:, f, :],
                                                start=(f == 0), stop=(f == FT - 1))
                    last.then_inc(MO.w2_ps, 1)

            pe.wait_ge(MO.b2, 1)
            hidden(0, 0, 0)

            def step(e, s, nxt):
                hidden(e, s, 1)
                outputs(e, s, 0)
                if nxt:
                    hidden(e + 1, 1 - s, 0)
                outputs(e, s, 1)

            tiles(pe, step)

        def act_moe(act):
            act.sem_inc(MO.mT, 2)
            act.sem_inc(MO.w1_free, 4)

            def rows_T(t, s, nxt):
                act.wait_ge(MO.mT_ps, t + 1)
                act.sem_inc(act_go, 1)
                for k in range(KD):
                    last = nc.scalar.activation(mT[:, k, bass.ds(t * P, P)], ps[:, s, k * P:k * P + P], ACT.Identity,
                                                bias=vec("ln2_b", k), scale=vec("ln2_g", k))
                last.then_inc(MO.mT, 1)

            tiles(act, rows_T)
            act.wait_ge(MO.diff, 1)
            nc.scalar.activation(gexp[:, :], gexp[:, :], ACT.Exp).then_inc(MO.exp, 1)
            act.wait_ge(MO.gT_ps, 1)
            for i in range(2):
                last = nc.scalar.activation(gate_T[:, 512 * i:512 * i + 512], ps[:, i, :], ACT.Copy)
            last.then_inc(MO.gT, 1)

            def hidden(e, s, c):
                for f in range(FT):
                    act.wait_ge(MO.w1_ps, 16 * e + 8 * c + f + 1)
                    act.sem_inc(act_go, 1)
                    nc.scalar.activation(h1[c][:, f, :], ps[:, f % 4, :], ACT.Gelu_apprx_tanh,
                                         bias=col[:, bass.ds(e * FT + (COLS["b1"][0] + f), 1)]).then_inc(MO.w1_free, 1)

            def step(e, s, nxt):
                for c in range(2):
                    hidden(e, s, c)

            tiles(act, step)

        def dve_moe(dve):
            def norm(t):
                row_apply(dve, t, u[:, bass.ds(t, 1), :].rearrange("p a d -> p (a d)"), [h[:, :]], "moe")

            dve.wait_ge(SA.x_done, 2 * T)
            norm(0)

            def step_norm(t, s, nxt):
                if nxt:
                    dve.wait_ge(MO.mT_ps, t + 1)
                    norm(t + 1)

            tiles(dve, step_norm)
            dve.wait_ge(MO.router_ps, 1)
            for i in range(2):
                last = nc.vector.tensor_copy(logit[:, 4 * i:4 * i + 4, :], ps[:, 2 + i, :].rearrange("p (t e) -> p t e", e=P)[:, :, 0:E])
            last.then_inc(MO.logit, 1)
            dve.wait_ge(MO.logit, 1)
            for t in range(T):
                last = nc.vector.max(top[:, t, :], logit[:, t, :])
            last.then_inc(MO.top, 1)
            dve.wait_ge(MO.top, 1)
            nc.vector.tensor_tensor(gexp[:, :], top[:, :, 1], top[:, :, 0], ALU.subtract).then_inc(MO.diff, 1)
            for t in range(T):
                last = nc.vector.max_index(topi[:, t, :], top[:, t, :], logit[:, t, :])
            last.then_inc(MO.topi, 1)
            dve.wait_ge(MO.topi, 1)
            nc.vector.tensor_copy(topf[:, :, :], topi[:, :, 0:2]).then_inc(MO.topi, 1)
            dve.wait_ge(MO.exp, 1)
            nc.vector.tensor_scalar(gw[:, :, 2], gexp[:, :], 1.0, None, ALU.add).then_inc(MO.w, 1)
            dve.wait_ge(MO.w, 1)
            nc.vector.reciprocal(gw[:, :, 0], gw[:, :, 2]).then_inc(MO.w, 1)
            dve.wait_ge(MO.w, 2)
            nc.vector.tensor_tensor(gw[:, :, 1], gexp[:, :], gw[:, :, 0], ALU.mult).then_inc(MO.w, 1)
            dve.wait_ge(MO.topi, 2)
            iota = cst[:, C_IOTA:C_IOTA + E].rearrange("p (o e) -> p o e", o=1).broadcast_to((P, T, E))
            for i in range(2):
                last = nc.vector.tensor_tensor(gsel[:, :, i, :], iota, topf[:, :, i:i + 1].broadcast_to((P, T, E)), ALU.is_equal)
            last.then_inc(MO.sel, 1)
            dve.wait_ge(MO.sel, 1)
            dve.wait_ge(MO.w, 3)
            for i in range(2):
                last = nc.vector.tensor_tensor(gsel[:, :, i, :], gsel[:, :, i, :], gw[:, :, i:i + 1].broadcast_to((P, T, E)), ALU.mult)
            last.then_inc(MO.sel, 1)
            dve.wait_ge(MO.sel, 2)
            dve.wait_ge(pool_setup, 7)
            nc.vector.tensor_tensor(gate[:, :, 0:E], gsel[:, :, 0, :], gsel[:, :, 1, :], ALU.add).then_inc(MO.gate, 1)
            dve.wait_ge(MO.b2_ps, 1)
            for i in range(4):
                last = nc.vector.tensor_tensor(x[:, 2 * i:2 * i + 2, :], ps[:, 4 + i, :].rearrange("p (t d) -> p t d", t=2), x[:, 2 * i:2 * i + 2, :], ALU.add)
            last.then_inc(MO.b2, 1)
            dve.wait_ge(MO.b2, 1)
            dve.sem_inc(MO.w2_free, 4)
            dve.wait_ge(ld["pad"], 32)
            for i in range(2):
                nc.vector.tensor_scalar(padneg[0:1, 8 * i:8 * i + 8, :], maskrow[i][0:1, :, :], 0.0, NEG, ALU.is_equal, ALU.mult).then_inc(MO.pad, 1)
            dve_ff_weights(dve)

            def step(e, s, nxt):
                for c in range(2):
                    for i in range(4):
                        n = 8 * e + 4 * c + i
                        dve.wait_ge(MO.w2_ps, n + 1)
                        dve.wait_ge(MO.w2_free, n + 1)
                        nc.vector.scalar_tensor_tensor(x[:, 4 * c + i, :], ps[:, 4 + i, 0:D], gate[:, 4 * c + i, bass.ds(e, 1)], x[:, 4 * c + i, :],
                                                       ALU.mult, ALU.add).then_inc(MO.w2_free, 1)
                        if not nxt:
                            dve.wait_ge(MO.w2_free, n + 5)
                            row_statistics(dve, x[:, 4 * c + i, :], i % 2, ROW_BASE["x1"] + 4 * c + i)

            tiles(dve, step)

        def pool_moe(pool):
            tiles(pool, lambda t, s, nxt: row_rstd(pool, t, s, "x1"))

        class FF:
            w0 = sem("ff_w0")
            w = sem("ff_w")
            scale = sem("ff_scale")
            xT_ps = sem("ff_xT_ps")
            xT_hi = sem("ff_xT_hi")
            xT = sem("ff_xT")
            r_ps = sem("ff_r_ps")
            r_free = sem("ff_r_free")
            h_free = sem("ff_h_free")
            hi = sem("ff_hi")
            split = sem("ff_split")
            y_ps = sem("ff_y_ps")
            y_free = sem("ff_y_free")
        PIECES = [("w0", 0), ("w0", 1), ("w1", 0), ("w1", 1), ("w1", 2), ("w1", 3), ("w2", 0)]

        def pool_ff_weights(pool):
            for n, (w, i) in enumerate(PIECES):
                if w == "w0":
                    continue
                pool.wait_ge(ld_ff[n % 2], 32 + 16 * (n // 2))
                raw = ffraw[:, n % 2, :, :]
                if w == "w1":
                    last = nc.gpsimd.tensor_scalar(ffw1[:, 2 * i:2 * i + 2, :], raw[:, :, :], 2.0, -1.0, ALU.mult, ALU.add)
                else:
                    last = nc.gpsimd.tensor_scalar(ffw2[:, :, :], raw.rearrange("p a n -> p (a n)").rearrange("p (k d) -> p k d", d=D), 2.0, -1.0, ALU.mult, ALU.add)
                last.then_inc(FF.w, 1)

        def dve_ff_weights(dve):
            for n in range(KD):
                dve.wait_ge(ld_ff[n], 32)
                nc.vector.tensor_tensor(ffw0[:, n, :], ffraw[:, n, 0, :], ffraw[:, n, 1, :], ALU.subtract).then_inc(FF.w0, 1)

        def pe_ff(pe):
            pe.wait_ge(FF.w0, KD)
            pe.wait_ge(FF.w, len(PIECES) - KD)
            with pe.Fori(0, 2) as c:
                for i in range(4):
                    pe.wait_ge(rn_done, ROW_BASE["mlp"] + 4 * c + i + 1)
                    pe.wait_ge(FF.xT, 4 * c + i + 1)
                    for k in range(KD):
                        last = nc.tensor.transpose(ps[:, i % 2, k * P:k * P + P], h[:, k * P:k * P + P], ident)
                    last.then_inc(FF.xT_ps, 1)
                pe.wait_ge(FF.xT, 4 * c + 6)
                for layer, (w, src, ks) in enumerate(((ffw0, fxT, KD), (ffw1, f0, FT))):
                    if layer == 1:
                        pe.wait_ge(FF.split, 16 * c + 8)
                    for f in range(FT):
                        n = 16 * c + 8 * layer + f
                        pe.wait_ge(FF.r_free, n + 1)
                        for k in range(ks):
                            for part in range(2):
                                last = nc.tensor.matmul(ps[:, 2 + f % 4, :], w[:, k, f * P:f * P + P], src[part][:, k, :],
                                                        start=(k == 0 and part == 0), stop=(k == ks - 1 and part == 1))
                        last.then_inc(FF.r_ps, 1)
                pe.wait_ge(FF.split, 16 * c + 16)
                for i in range(4):
                    pe.wait_ge(FF.y_free, 4 * c + i + 1)
                    for k in range(FT):
                        for part in range(2):
                            last = nc.tensor.matmul(ps[:, 6 + i % 2, 0:D], f1[part][:, k, i * P:i * P + P], ffw2[:, k, :],
                                                    start=(k == 0 and part == 0), stop=(k == FT - 1 and part == 1))
                    last.then_inc(FF.y_ps, 1)

        def act_ff(act):
            act.sem_inc(FF.r_free, 4)
            act.wait_ge(FF.scale, 2)
            with act.Fori(0, 2) as c:
                for i in range(4):
                    act.wait_ge(FF.xT_ps, 4 * c + i + 1)
                    nc.scalar.activation(fxT[0][:, :, i * P:i * P + P], ps[:, i % 2, 0:D].rearrange("p (k n) -> p k n", k=2), ACT.Copy).then_inc(FF.xT_hi, 1)
                for layer in range(2):
                    for f in range(FT):
                        n = 16 * c + 8 * layer + f
                        act.wait_ge(FF.r_ps, n + 1)
                        act.wait_ge(FF.h_free, n + 1)
                        nc.scalar.activation(fh[f % 2][:, :], ps[:, 2 + f % 4, :], ACT.Relu, scale=ffs[:, layer:layer + 1]).then_inc(FF.r_free, 1)

        def dve_ff(dve):
            nc.vector.tensor_scalar(ffs[:, 0:1], vec("s0"), 4.0, None, ALU.mult).then_inc(FF.scale, 1)
            nc.vector.tensor_scalar(ffs[:, 1:2], vec("s1"), 2.0, None, ALU.mult).then_inc(FF.scale, 1)
            for k, v in ((FF.xT, 2), (FF.h_free, 2), (FF.y_free, 2)):
                dve.sem_inc(k, v)
            dve.wait_ge(SA.y_free, 3 * T + 1)
            with dve.Fori(0, 2) as c:
                for i in range(4):
                    xt = x[:, bass.ds(4 * c + i, 1), :].rearrange("p a d -> p (a d)")
                    if i > 0:
                        dve.wait_ge(FF.xT_ps, 4 * c + i)
                    row_apply(dve, 4 * c + i, xt, [h[:, :]], "mlp")
                    dve.wait_ge(FF.xT_hi, 4 * c + i + 1)
                    nc.vector.tensor_tensor(fxT[1][:, :, i * P:i * P + P], ps[:, i % 2, 0:D].rearrange("p (k n) -> p k n", k=2),
                                            fxT[0][:, :, i * P:i * P + P].bitcast(F32), ALU.subtract).then_inc(FF.xT, 1)
                for layer, dst in enumerate((f0, f1)):
                    for f in range(FT):
                        n = 16 * c + 8 * layer + f
                        dve.wait_ge(FF.r_free, n + 5)
                        nc.vector.tensor_copy(dst[0][:, f, :], fh[f % 2][:, :]).then_inc(FF.hi, 1)
                        dve.wait_ge(FF.hi, n + 1)
                        nc.vector.tensor_tensor(dst[1][:, f, :], fh[f % 2][:, :], dst[0][:, f, :].bitcast(F32), ALU.subtract).then_inc(FF.split, 1)
                        dve.wait_ge(FF.split, n + 1)
                        dve.sem_inc(FF.h_free, 1)
                for i in range(4):
                    xt = x[:, bass.ds(4 * c + i, 1), :].rearrange("p a d -> p (a d)")
                    dve.wait_ge(FF.y_ps, 4 * c + i + 1)
                    nc.vector.scalar_tensor_tensor(xt, ps[:, 6 + i % 2, 0:D], vec("s2"), xt, ALU.mult, ALU.add).then_inc(FF.y_free, 1)

        @block.sync
        def _(sp):
            def whole(dst, src, s):
                sp.dma_start(dst, src).then_inc(s, 16)

            def weight(name):
                return a[name].rearrange("(k p) n -> p k n", p=P)

            def ctx_tile(l, t, s):
                sp.dma_start((X0, X1)[l]["cin"][:, s, :, :], y_at[bass.ds(t, 1), :, :, :].rearrange("o p k d -> p (o k) d")).then_inc(ld_ctx[l][s], 16)

            def expert(e, s):
                sp.dma_start(ew1[s][:, :, :], a["L0_ffn_W1"][bass.ds(e, 1), :, :].rearrange("o (k p) n -> p (o k) n", p=P)).then_inc(ld_e[s], 16)
                sp.dma_start(ew2[s][:, :, :], a["L0_ffn_W2"][bass.ds(e, 1), :, :].rearrange("o (k p) n -> p (o k) n", p=P)).then_inc(ld_e[s], 16)

            x_in = a["x"].rearrange("b n d -> (b n) d").rearrange("(t p) d -> p t d", p=P)
            ctx_tile(0, 0, 0)
            whole(x[:, 0:2, :], x_in[:, 0:2, :], ld["x"])
            whole(cst[:, :], a["consts"], ld["const"])
            whole(col[:, :], a["cols"], ld["const"])
            whole(X0["wq"][:, :, :], weight("L0_xattn_Wq"), ld["x0q"])
            for half, k in enumerate(("x0k", "x0v")):
                part = slice(half * INNER, half * INNER + INNER)
                whole(X0["wkv"][:, :, part], weight("L0_xattn_Wkv")[:, :, part], ld[k])
            ctx_tile(0, 1, 1)
            whole(X0["wo"][:, :, :], weight("L0_xattn_Wo"), ld["x0o"])
            whole(x[:, 2:T, :], x_in[:, 2:T, :], ld["x_rest"])
            whole(rows[:, :, :], a["rows"], ld["rows"])
            for i, w in enumerate(("wq", "wkv")):
                whole(w_mla[:, :, 64 * i:64 * i + 64], weight("L0_attn_" + w), ld["mla"])
            for i, w in enumerate(("wqr", "wqr_swapped", "wkr", "wkr_swapped")):
                whole(w_mla[:, :, P + P * i:2 * P + P * i], weight("L0_attn_" + w), ld["mla"])
            whole(w_mlao[:, :, :], weight("L0_attn_wo"), ld["mla"])
            sp.wait_ge(pool_setup, 4)
            whole(w_mlac[0:64, 0:P], a["L0_attn_wqc"], ld["mla"])
            whole(w_mlac[64:P, P:2 * P], a["L0_attn_wkc"], ld["mla"])
            whole(w_mlac[64:P, 2 * P:2 * P + D], a["L0_attn_wv"], ld["mla"])
            whole(wg[:, :, 0:E], weight("L0_ffn_Wg"), ld["wg"])
            for i, w in enumerate(("Wq", "Wk", "Wv", "Wo")):
                whole(w_sq[0][:, :, i, :], weight("L0_ffn_" + w), ld["sq0"])
            for i, w in enumerate("QKVO"):
                whole(w_sq[1][:, :, i, :], weight("L1_attn_W_" + w), ld["sq1"])
            with sp.Fori(0, T // 2 - 1) as i:
                for s in range(2):
                    sp.wait_ge(ln_done, 2 * (2 * i + s) + 2)
                    ctx_tile(0, 2 * i + s + 2, s)
            sp.wait_ge(X[0].x_done, T)
            sp.wait_ge(pool_setup, 6)
            whole(b2[0:E, :], a["L0_ffn_b2"], ld["b2"])
            for i, w in enumerate(("Wq", "Wk", "Wv", "Wo")):
                whole(xw[:, :, i, :], weight("L1_xattn_" + w), ld["xw"])
            for e in range(2):
                expert(e, e)
            sp.wait_ge(rn_done, ROW_BASE["moe"] + T)
            sp.wait_ge(SA.y_ps, 2 * T)
            for i in range(2):
                whole(maskrow[i][0:1, :, :], a["mask_BxS2_ik0"].rearrange("(o h b) s -> h o b s", o=1, h=2)[i], ld["pad"])
            for n, (w, i) in enumerate(PIECES):
                if n >= 2:
                    sp.wait_ge(FF.w0 if n < 4 else FF.w, n - 1 if n < 4 else n - 3)
                if w == "w0":
                    for half in range(2):
                        whole(ffraw[:, n % 2, half, :], a["L1_ffn_k0"][half * D + i * P:half * D + i * P + P, :], ld_ff[n % 2])
                elif w == "w1":
                    whole(ffraw[:, n % 2, :, :], weight("L1_ffn_k1")[:, 2 * i:2 * i + 2, :], ld_ff[n % 2])
                else:
                    whole(ffraw[:, n % 2, :, :].rearrange("p a n -> p (a n)").rearrange("p (k d) -> p k d", d=D), weight("L1_ffn_k2"), ld_ff[n % 2])
            with sp.Fori(0, E // 2 - 1) as i:
                for s in range(2):
                    sp.wait_ge(MO.w2_ps, 8 * (2 * i + s) + 8)
                    expert(2 * i + s + 2, s)
            sp.wait_ge(MO.w2_ps, 8 * E)
            ctx_tile(1, 0, 0)
            ctx_tile(1, 1, 1)
            with sp.Fori(0, T // 2 - 1) as i:
                for s in range(2):
                    for bank in range(2):
                        sp.wait_ge(X[1].fill_done[bank], X[1].per * (2 * i + s) + X[1].first["cT"] // 2 + 1)
                    ctx_tile(1, 2 * i + s + 2, s)
            out_v = out.rearrange("b n d -> (b n) d").rearrange("(t p) d -> p t d", p=P)
            for c in range(2):
                sp.wait_ge(FF.y_free, 4 * c + 6)
                sp.dma_start(out_v[:, 4 * c:4 * c + 4, :], x[:, 4 * c:4 * c + 4, :]).then_inc(stored, 16)
            sp.wait_ge(stored, 32)
            sp.wait_ge(dve_go, 2 * (2 * T + len(ROW_BASE) * T))
            sp.wait_ge(pool_go, len(ROW_BASE) * T + T)
            sp.wait_ge(act_go, T + 2 * E * FT)

        @block.gpsimd
        def _(pool):
            nc.gpsimd.memset(neghalf[:, :], -0.5).then_inc(pool_setup, 1)
            nc.gpsimd.memset(eps[:, :], EPS).then_inc(pool_setup, 1)
            nc.gpsimd.memset(w_mlac[:, :], 0.0).then_inc(pool_setup, 1)
            nc.gpsimd.memset(wg[:, :, :], 0.0).then_inc(pool_setup, 1)
            nc.gpsimd.memset(padneg[:, :, :], 0.0).then_inc(pool_setup, 1)
            pool.wait_ge(pool_setup, 5)
            pool_cross(pool, X[0])
            pool.wait_ge(X[0].x_done, T)
            nc.gpsimd.memset(b2[:, :], 0.0).then_inc(pool_setup, 1)
            nc.gpsimd.memset(gate[:, :, :], 0.0).then_inc(pool_setup, 1)
            pool_self(pool, 0)
            pool_self(pool, 1)
            pool_ff_weights(pool)
            pool_moe(pool)
            pool_cross(pool, X[1])
            pool_self(pool, 2)

        @block.scalar
        def _(act):
            act.wait_ge(ld["const"], 32)
            act_cross(act, X[0])
            act_self(act, 0)
            act_self(act, 1)
            act_moe(act)
            act_cross(act, X[1])
            act_self(act, 2)
            act_ff(act)

        @block.vector
        def _(dve):
            dve.wait_ge(ld["const"], 32)
            dve.wait_ge(ld["x"], 16)
            nc.vector.tensor_copy(identb[:, :], ident).then_inc(setup, 1)
            nc.vector.tensor_copy(causalb[:, :], cst[:, C_CAUSAL:C_CAUSAL + N]).then_inc(setup, 1)
            nc.vector.tensor_copy(row0b[:, :], cst[:, C_ROW0:C_ROW0 + P]).then_inc(setup, 1)
            dve_cross(dve, X[0])
            dve_self(dve, 0, X[0].x_done, T)
            dve_self(dve, 1, SA.x_done, T)
            dve_moe(dve)
            dve.wait_ge(MO.w2_free, 8 * E + 4)
            dve_cross(dve, X[1])
            dve_self(dve, 2, X[1].x_done, T)
            dve_ff(dve)

        @block.tensor
        def _(pe):
            pe.wait_ge(ld["const"], 32)
            pe_cross(pe, X[0])
            pe_self(pe, 0)
            pe_self(pe, 1)
            pe_moe(pe)
            pe_cross(pe, X[1])
            pe_self(pe, 2)
            pe_ff(pe)


def ctx_views(ctx):
    return ctx.rearrange("b s d -> (b s) d").rearrange("(t k p) d -> t p k d", k=4, p=P)


def _tables(i):
    p = np.arange(P)
    cst = np.zeros((P, C_ALL), np.float32)
    cst[:, C_IDENT:C_IDENT + P] = np.eye(P)
    cst[:, C_HEAD:C_HEAD + 8] = p[:, None] // 16 == np.arange(8)
    cst[:, C_PAR:C_PAR + 2] = p[:, None] // 16 % 2 == np.arange(2)
    cst[:, C_CAUSAL:C_CAUSAL + N] = np.where(np.arange(N)[None, :] > (p % N)[:, None], NEG, 0.0)
    inv = (1.0 / np.float32(10000.0) ** (np.arange(0, P, 2, dtype=np.float32) / np.float32(P))).astype(np.float32)
    ang = np.tile(np.arange(N, dtype=np.float32)[None, :] * inv[:, None], (2, 2))
    cst[:, C_COS:C_COS + P] = np.cos(ang)
    cst[:, C_SIN:C_SIN + P] = np.sin(ang) * np.where(p < 64, -1, 1)[:, None]
    cst[:, C_IOTA:C_IOTA + E] = np.arange(E)
    cst[0, C_ROW0:C_ROW0 + P] = 1.0
    half = lambda v: np.concatenate([v[64:], v[:64]])
    vecs = {"ln_l_w": i["L0_xattn_ln_l_w"], "ln_l_b": i["L0_xattn_ln_l_b"], "ln_c_w": i["L0_xattn_ln_c_w"], "ln_c_b": i["L0_xattn_ln_c_b"],
            "bqkv": np.concatenate([i["L0_attn_bq"], i["L0_attn_bkv"]]), "bqc": i["L0_attn_bqc"], "bkc": i["L0_attn_bkc"],
            "bqr": i["L0_attn_bqr"], "bqs": half(i["L0_attn_bqr"]), "bkr": i["L0_attn_bkr"], "bks": half(i["L0_attn_bkr"]),
            "bv0": i["L0_attn_bv"], "ln1_g": i["L0_ffn_ln1_g"], "ln1_b": i["L0_ffn_ln1_b"], "ln2_g": i["L0_ffn_ln2_g"], "ln2_b": i["L0_ffn_ln2_b"],
            "xbq": i["L1_xattn_bq"], "xbk": i["L1_xattn_bk"], "xbv": i["L1_xattn_bv"], "b1": i["L0_ffn_b1"].reshape(-1),
            "s0": np.broadcast_to(i["L1_ffn_s0"], (P,)), "s1": np.broadcast_to(i["L1_ffn_s1"], (P,)), "s2": np.broadcast_to(i["L1_ffn_s2"], (P,))}
    cols = np.concatenate([np.reshape(vecs[k], (-1, P)).T for k in COLS], 1)
    rows = np.stack([np.broadcast_to(i[k], (P, D)) for k in ("L0_xattn_bo", "L0_attn_bo", "L1_xattn_bo")], 1)
    return {"consts": cst, "cols": cols, "rows": rows}


def _inputs(i):
    ins = {k: v for k, v in i.items() if k in ("x", "ctx_1024", "mask_BxS2_ik0") or v.ndim >= 2}
    for k in "QKVO":
        ins[f"L1_attn_W_{k}"] = ins[f"L1_attn_W_{k}"].T
    for k in ("wqr", "wkr"):
        w = ins[f"L0_attn_{k}"]
        ins[f"L0_attn_{k}_swapped"] = np.concatenate([w[:, 64:], w[:, :64]], 1)
    ins.update(_tables(i))
    return {k: np.ascontiguousarray(v) for k, v in ins.items()}


def kernel(**inputs):
    import concourse.bacc as bacc
    from concourse.bass_utils import run_bass_kernel_spmd

    arrays = _inputs({k: np.asarray(v) for k, v in inputs.items()})
    nc = bacc.Bacc("TRN2", target_bir_lowering=False, num_devices=1)
    aps = {k: nc.dram_tensor(k + "_dram", v.shape, mybir.dt.from_np(v.dtype), kind="ExternalInput").ap() for k, v in arrays.items()}
    out = nc.dram_tensor("out_dram", (B, N, D), F32, kind="ExternalOutput").ap()
    build(nc, aps, out)
    r = run_bass_kernel_spmd(nc, [{k + "_dram": v for k, v in arrays.items()}], core_ids=[0])
    return r.results[0]["out_dram"]
```

```python
from contextlib import ExitStack

import numpy as np

import concourse.bass as bass
from concourse import mybir

F32 = mybir.dt.float32
F32R = mybir.dt.float32r
BF16 = mybir.dt.bfloat16
U8 = mybir.dt.uint8
U32 = mybir.dt.uint32
I32 = mybir.dt.int32
ALU = mybir.AluOpType
ACT = mybir.ActivationFunctionType
AX_X = mybir.AxisListType.X

P = 128
B, N, D, S = 16, 64, 256, 256
T = B * N // P
KD = D // P
H = 16
INNER = 1024
E, F = 8, 1024
FT = F // P
NEG = -1e30
EPS = 1e-5

C_IDENT, C_HEAD, C_PAR, C_CAUSAL, C_COS, C_SIN, C_IOTA, C_ROW0 = np.cumsum([0, 128, 8, 2, 64, 128, 128, 8])
C_ALL = C_ROW0 + 128
COLS = {}
for _name, _k in [("ln_l_w", 2), ("ln_l_b", 2), ("ln_c_w", 2), ("ln_c_b", 2), ("bqkv", 1), ("bqc", 1), ("bkc", 1),
                  ("bqr", 1), ("bqs", 1), ("bkr", 1), ("bks", 1), ("bv0", 2), ("ln1_g", 2), ("ln1_b", 2), ("ln2_g", 2), ("ln2_b", 2),
                  ("xbq", 2), ("xbk", 2), ("xbv", 2), ("b1", E * FT), ("s0", 1), ("s1", 1), ("s2", 1)]:
    COLS[_name] = (sum(k for _, k in COLS.values()), _k)
COL_ALL = sum(k for _, k in COLS.values())


def build(nc, a, out):
    with ExitStack() as ctx:
        at = [(nc.sbuf_base + 31) // 32 * 32]

        def sb(name, shape, dt=F32):
            size = int(np.prod(shape[1:])) * (1 if dt == U8 else 2 if dt == BF16 else 4)
            here = at[0]
            at[0] += (size + 31) // 32 * 32
            assert at[0] <= nc.sbuf_usable_end, (name, at[0])
            return nc.alloc_sbuf_tensor_at(name, shape, dt, offset=here)

        def sem(name):
            return ctx.enter_context(nc.semaphore(name))

        ps = ctx.enter_context(nc.psum_tensor("ps", [P, 8, 512], F32))

        x = sb("x_res", [P, T, D])
        cst = sb("cst", [P, C_ALL])
        col = sb("col", [P, COL_ALL])
        rows = sb("rows", [P, 3, D])
        ident = cst[:, C_IDENT:C_IDENT + P]
        identb = sb("identb", [P, P], BF16)
        causalb = sb("causalb", [P, N], BF16)
        row0b = sb("row0b", [P, P], BF16)
        padneg = sb("padneg", [P, B, S], BF16)
        head_of = cst[:, C_HEAD:C_HEAD + 8]
        par_of = cst[:, C_PAR:C_PAR + 2]
        w_sq_at = at[0]
        w_sq = [sb(f"w_sq{i}", [P, KD, 4, D]) for i in range(2)]
        w_mla = sb("w_mla", [P, KD, 128 + 4 * 128])
        w_mlac = sb("w_mlac", [P, 128 + 128 + D])
        w_mlao = sb("w_mlao", [P, KD, D])
        wg = sb("wg", [P, KD, P])
        ln_st = sb("ln_st", [P, 5, 6])
        ln_mv = sb("ln_mv", [P, 5, 2])
        ln_ve = sb("ln_ve", [P, 5])
        ln_rs = sb("ln_rs", [P, 5])
        neghalf = sb("neghalf", [P, 5])
        eps = sb("eps", [P, 5])
        rn_st = sb("rn_st", [P, 2, 6])
        rn_cur = sb("rn_cur", [P, 2, 2])
        rn_tmp = sb("rn_tmp", [P, 2, 4])
        rn_mean = sb("rn_mean", [P, T])
        rn_rs = sb("rn_rs", [P, T])
        rn_rs2 = sb("rn_rs2", [P, T])

        def vec(name, i=0):
            at0, _ = COLS[name]
            return col[:, at0 + i:at0 + i + 1]

        mark = at[0]

        def cross_buffers(tag, kg, vw, probs_at=None, cin_at=None, lat=None):
            g = {}
            g["cin"] = sb(tag + "cin", [P, 2, 4, D]) if cin_at is None else nc.alloc_sbuf_tensor_at(tag + "cin", [P, 2, 4, D], F32, offset=cin_at)
            g["cT"] = sb(tag + "cT", [P, KD, 512])
            g["lat"] = sb(tag + "lat", [P, D]) if lat is None else lat
            g["latT"] = sb(tag + "latT", [P, KD, P])
            g["qbd"] = [sb(f"{tag}qbd{i}", [P, 2, 8, P]) for i in range(2)]
            g["kT"] = [sb(f"{tag}kT{i}", [P, kg, 512]) for i in range(2)]
            g["v"] = [sb(f"{tag}v{i}", [P, 4, vw]) for i in range(1 if tag == "x0" else 2)] * (2 if tag == "x0" else 1)
            after, at[0] = at[0], at[0] if probs_at is None else probs_at
            g["p"] = [sb(f"{tag}p{i}", [P, 4, S]) for i in range(2)]
            g["pT"] = [sb(f"{tag}pT{i}", [P, 8, P]) for i in range(2)]
            at[0] = at[0] if probs_at is None else after
            g["attT"] = sb(tag + "attT", [P, kg, P])
            g["sum"] = sb(tag + "sum", [P, 2, 4])
            g["rinv"] = sb(tag + "rinv", [P, 2, 4])
            g["nmax"] = sb(tag + "nmax", [P, 2, 4])
            return g

        X0 = cross_buffers("x0", 8, INNER)
        X0["cn"] = sb("x0cn", [P, 4, D])
        X0["wq"] = sb("x0wq", [P, KD, INNER])
        X0["wkv_lo"] = nc.alloc_sbuf_tensor_at("x0wkv_lo", [P, KD, 2 * INNER], F32R, offset=at[0])
        X0["wkv"] = sb("x0wkv", [P, KD, 2 * INNER])
        X0["wkv_hi"] = sb("x0wkv_hi", [P, KD, 2 * INNER], F32R)
        X0["cT_hi"], X0["cT_lo"] = (sb(f"x0cT_{k}", [P, KD, 512], F32R) for k in ("hi", "lo"))
        X0["wo"] = sb("x0wo", [P, 8, D])

        at[0] = mark
        h = sb("h", [P, D])
        hT = sb("hT", [P, KD, P])
        qT = sb("qT", [P, KD, P])
        kTs = sb("kTs", [P, KD, P])
        cqkvT = sb("cqkvT", [P, P])
        rope = sb("rope", [P, 4, P])
        h1_at = at[0]
        kbd = sb("kbd", [P, KD, 2, 8, N])
        pr = sb("pr", [P, H, N])
        prT = sb("prT", [P, 8, P])
        vbd = [sb(f"vbd{i}", [P, 2, 8, 2, 16]) for i in range(2)]
        smax = sb("smax", [P, H])
        ssum = sb("ssum", [P, H])
        srinv = sb("srinv", [P, H])
        sattT = sb("sattT", [P, KD, P])
        u_at = at[0]
        u = sb("u", [P, T, D])
        xw = sb("xw", [P, KD, 4, D])
        ffs = sb("ffs", [P, 2])
        minus1 = sb("minus1", [P, 1])
        mark1 = at[0]
        ew1, ew2, ew1_hi, ew2_hi, ew1_lo, ew2_lo = [], [], [], [], [], []
        for i in range(2):
            for whole_, lo, hi, shape in ((ew1, ew1_lo, ew1_hi, [P, KD, F]), (ew2, ew2_lo, ew2_hi, [P, FT, D])):
                lo.append(nc.alloc_sbuf_tensor_at(f"ew_lo{i}{shape[1]}", shape, F32R, offset=at[0]))
                whole_.append(sb(f"ew{i}{shape[1]}", shape))
                hi.append(sb(f"ew_hi{i}{shape[1]}", shape, F32R))
        mT = sb("mT", [P, KD, T * P])
        mT_hi = sb("mT_hi", [P, KD, T * P], F32R)
        mT_lo = sb("mT_lo", [P, KD, T * P], F32R)
        eh = [sb(f"eh{i}", [P, 512]) for i in range(2)]
        eh_hi = [sb(f"eh_hi{i}", [P, 512], F32R) for i in range(2)]
        eh_lo = [sb(f"eh_lo{i}", [P, 512], F32R) for i in range(2)]
        logit = sb("logit", [P, T, E])
        top = sb("top", [P, T, 8])
        topi = sb("topi", [P, T, 8], U32)
        topf = sb("topf", [P, T, 2])
        gexp = sb("gexp", [P, T])
        gw = sb("gw", [P, T, 4])
        gsel = sb("gsel", [P, T, 2, E])
        gate = sb("gate", [P, T, P])
        b2 = sb("b2", [P, D])
        gate_T = sb("gate_T", [P, T * P])
        maskrow = [nc.alloc_sbuf_tensor_at(f"maskrow{i}", [P, B // 2, S], I32, offset=o) for i, o in enumerate((u_at, w_sq_at))]
        at[0] = mark1
        ffw0 = sb("ffw0", [P, KD, F], F32R)
        ffw1 = sb("ffw1", [P, FT, F], F32R)
        ffw2 = sb("ffw2", [P, FT, D], F32R)
        mark2 = at[0]
        X1 = cross_buffers("x1", KD, D, h1_at, u_at, h)
        X1["qs"] = sb("x1qs", [P, KD, P])
        X1["pv0"] = sb("x1pv0", [P, N])
        X1["wq"], X1["wkv"], X1["wo"] = xw[:, :, 0, :], None, xw[:, :, 3, :]
        at[0] = mark2
        fxT = [sb(f"fxT{i}", [P, KD, 512], F32R) for i in range(2)]
        fn = [h, sb("fn1", [P, D])]
        fh = [sb(f"fh{i}", [P, 512]) for i in range(2)]
        raw_at = at[0]
        f0 = [sb(f"f0_{i}", [P, FT, 512], F32R) for i in range(2)]
        f1 = [sb("f1_0", [P, FT, 512], F32R), nc.alloc_sbuf_tensor_at("f1_1", [P, FT, 512], F32R, offset=h1_at)]
        raw0, raw1, raw2 = (nc.alloc_sbuf_tensor_at(f"ffraw{i}", [P, k, n], U8, offset=raw_at + o)
                            for i, (k, n, o) in enumerate(((2 * KD, F, 0), (FT, F, 2 * KD * F), (FT, D, (2 * KD + FT) * F))))

        ld = {k: sem("ld_" + k) for k in ("x", "x_rest", "const", "rows", "x0q", "x0k", "x0v", "x0o", "mla", "sq0", "sq1", "xw", "pad", "wg", "b2")}
        ld_ctx = [[sem(f"ld_ctx{l}{i}") for i in range(2)] for l in range(2)]
        ld_e = [sem(f"ld_e{i}") for i in range(2)]
        ld_ff = sem("ld_ff")
        setup = sem("setup")
        pool_setup = sem("pool_setup")
        ln_stats, ln_aggr, ln_eps, ln_rstd = (sem(k) for k in ("ln_stats", "ln_aggr", "ln_eps", "ln_rstd"))
        ln_done = sem("ln_done")
        dve_go, act_go, pool_go = sem("dve_go"), sem("act_go"), sem("pool_go")
        rn_stats, rn_aggr, rn_eps, rn_twice, rn_rstd, rn_done = (sem(k) for k in ("rn_stats", "rn_aggr", "rn_eps", "rn_twice", "rn_rstd", "rn_done"))
        stored = sem("stored")

        block = ctx.enter_context(nc.Block())

        def tiles(e, step):
            with e.Fori(0, T // 2 - 1) as i:
                for s in range(2):
                    step(2 * i + s, s, True)
            step(T - 2, 0, True)
            step(T - 1, 1, False)

        def tiles2(e, step):
            with e.Fori(0, T // 2 - 1) as i:
                for s in range(2):
                    step(2 * i + s, s, True, True)
            step(T - 2, 0, True, False)
            step(T - 1, 1, False, False)

        def ln_first(dve, srcs):
            dve.sem_inc(dve_go, 1)
            for i, src in enumerate(srcs):
                nc.vector.bn_stats(ln_st[:, i, :], src)

        def ln_statistics(dve, srcs, idx, done=0):
            dve.sem_inc(dve_go, 1)
            for i, src in enumerate(srcs[done:]):
                last = nc.vector.bn_stats(ln_st[:, done + i, :], src)
            last.then_inc(ln_stats, 1)
            dve.wait_ge(ln_stats, idx + 1)
            dve.sem_inc(dve_go, 1)
            for i in range(len(srcs)):
                last = nc.vector.bn_aggr(ln_mv[:, i, :], ln_st[:, i, :])
            last.then_inc(ln_aggr, 1)

        def ln_rstd_pool(pool, k, idx):
            pool.wait_ge(ln_aggr, idx + 1)
            nc.gpsimd.tensor_tensor(ln_ve[:, 0:k], ln_mv[:, 0:k, 1], eps[:, 0:k], ALU.add).then_inc(ln_eps, 1)
            pool.wait_ge(ln_eps, idx + 1)
            nc.gpsimd.tensor_tensor(ln_rs[:, 0:k], ln_ve[:, 0:k], neghalf[:, 0:k], ALU.pow).then_inc(ln_rstd, 1)

        def ln_apply(dve, srcs, dsts, idx):
            dve.wait_ge(ln_rstd, idx + 1)
            for i, (src, dst) in enumerate(zip(srcs, dsts)):
                last = nc.vector.tensor_scalar(dst, src, ln_mv[:, i, 0:1], ln_rs[:, i:i + 1], ALU.subtract, ALU.mult)
            last.then_inc(ln_done, 1)

        ROW_BASE = {k: i * T for i, k in enumerate(("mla", "ffn", "moe", "x1", "attn", "mlp"))}

        def row_statistics(dve, src, s, idx):
            dve.wait_ge(rn_rstd, idx + 1)
            dve.sem_inc(dve_go, 1)
            nc.vector.bn_stats(rn_st[:, s, :], src).then_inc(rn_stats, 1)
            dve.wait_ge(rn_stats, idx + 1)
            dve.sem_inc(dve_go, 1)
            nc.vector.bn_aggr(rn_cur[:, s, :], rn_st[:, s, :]).then_inc(rn_aggr, 1)

        def row_rstd(pool, t, s, phase):
            idx = ROW_BASE[phase] + t
            var, one, tmp = rn_cur[:, s, 1:2], bass.ds(t, 1), rn_tmp[:, s, :]
            pool.wait_ge(rn_aggr, idx + 1)
            nc.gpsimd.tensor_tensor(tmp[:, 0:1], var, eps[:, 0:1], ALU.add).then_inc(rn_eps, 1)
            nc.gpsimd.tensor_copy(rn_mean[:, one], rn_cur[:, s, 0:1])
            pool.wait_ge(rn_eps, idx + 1)
            if phase != "ffn":
                pool.sem_inc(pool_go, 1)
                nc.gpsimd.tensor_tensor(rn_rs[:, one], tmp[:, 0:1], neghalf[:, 0:1], ALU.pow).then_inc(rn_rstd, 1)
                return
            rs, v2, rs2 = tmp[:, 1:2], tmp[:, 2:3], tmp[:, 3:4]
            for i, (dst, p, q, op) in enumerate(((rs, tmp[:, 0:1], neghalf[:, 0:1], ALU.pow), (v2, var, rs, ALU.mult), (v2, v2, rs, ALU.mult),
                                                 (v2, v2, eps[:, 0:1], ALU.add), (rs2, v2, neghalf[:, 0:1], ALU.pow))):
                nc.gpsimd.tensor_tensor(dst, p, q, op).then_inc(rn_twice, 1)
                pool.wait_ge(rn_twice, 5 * t + i + 1)
            pool.sem_inc(pool_go, 1)
            nc.gpsimd.tensor_copy(rn_rs[:, one], rs)
            nc.gpsimd.tensor_tensor(rn_rs2[:, one], rs2, rs, ALU.mult).then_inc(rn_rstd, 1)

        def row_apply(dve, t, src, dsts, phase):
            idx, one = ROW_BASE[phase] + t, bass.ds(t, 1)
            dve.wait_ge(rn_rstd, idx + 3)
            for dst, rs in zip(dsts, (rn_rs, rn_rs2)):
                last = nc.vector.tensor_scalar(dst, src, rn_mean[:, one], rs[:, one], ALU.subtract, ALU.mult)
            last.then_inc(rn_done, 1)

        XS, XF, XT, XV, XY = 0, (2, 3), (4, 5), 6, 7

        def cross(l):
            class c:
                fill_done0 = sem(f"x{l}_fill_done0")
                fill_done1 = sem(f"x{l}_fill_done1")
                fill_free0 = sem(f"x{l}_fill_free0")
                fill_free1 = sem(f"x{l}_fill_free1")
                s_done = sem(f"x{l}_s_done")
                s_free = sem(f"x{l}_s_free")
                clip_done = sem(f"x{l}_clip_done")
                exp_done = sem(f"x{l}_exp_done")
                rinv_done = sem(f"x{l}_rinv_done")
                norm_done = sem(f"x{l}_norm_done")
                pT_done0 = sem(f"x{l}_pT_done0")
                pT_done1 = sem(f"x{l}_pT_done1")
                pT_free0 = sem(f"x{l}_pT_free0")
                pT_free1 = sem(f"x{l}_pT_free1")
                p_free = sem(f"x{l}_p_free")
                pv_done = sem(f"x{l}_pv_done")
                pv_free = sem(f"x{l}_pv_free")
                y_done = sem(f"x{l}_y_done")
                y_free = sem(f"x{l}_y_free")
                x_done = sem(f"x{l}_x_done")
                q_spread = sem(f"x{l}_q_spread")
                if l == 0:
                    w_hi = sem("x0_w_hi")
                    w_lo = sem("x0_w_lo")
                    cT_hi = sem("x0_cT_hi")
                    cT_lo = sem("x0_cT_lo")
                else:
                    max_done = sem("x1_max_done")
                    pv0_done = sem("x1_pv0_done")

            c.l, c.g, c.next = l, (X0, X1)[l], ("mla", "attn")[l]
            c.kg = 8 if l == 0 else KD
            c.fills = ["lat"] * 2 + ["cT"] * 2 + ["q"] * 2 + ["k"] * c.kg + ["v"] * c.kg
            c.groups = ((0, 8), (8, 14), (14, 18), (18, 22)) if l == 0 else ((0, 6), (6, 8), (8, 9), (9, 10))
            c.per = len(c.fills) // 2
            c.first = {k: c.fills.index(k) for k in ("cT", "lat", "k", "v", "q")}
            c.fill_done, c.fill_free = (c.fill_done0, c.fill_done1), (c.fill_free0, c.fill_free1)
            c.pT_done, c.pT_free = (c.pT_done0, c.pT_done1), (c.pT_free0, c.pT_free1)
            return c

        X = [cross(0), cross(1)]


        def pe_cross(pe, c):
            g, l = c.g, c.l

            def fill(t, s, j):
                kind, i, bank, m = c.fills[j], j - c.first[c.fills[j]], j % 2, c.per * t + j // 2
                dst = ps[:, XF[bank], :]
                if j == 0:
                    if l == 0:
                        pe.wait_ge(ln_done, 2 * t + 2)
                    else:
                        pe.wait_ge(ld_ctx[1][s], 8 * (t - s) + 16)
                        pe.wait_ge(rn_done, ROW_BASE["x1"] + t + 1)
                if kind == "k" and i == 0 and l == 0:
                    pe.wait_ge(c.cT_lo, t + 1)
                elif kind == "k" and i == 0:
                    pe.wait_ge(c.fill_free[1], c.per * t + c.first["cT"] // 2 + 2)
                pe.wait_ge(c.fill_free[bank], m + 1)
                if kind == "cT":
                    src = g["cn"] if l == 0 else g["cin"][:, s]
                    for tok in range(4):
                        last = nc.tensor.transpose(dst[:, tok * P:tok * P + P], src[:, tok, i * P:i * P + P], ident)
                elif kind == "lat":
                    last = nc.tensor.transpose(dst[:, 0:P], g["lat"][:, i * P:i * P + P], ident)
                elif kind == "k":
                    for k in range(KD):
                        if l == 0:
                            for n, (w, m) in enumerate((("wkv_hi", "cT_hi"), ("wkv_hi", "cT_lo"), ("wkv_lo", "cT_hi"))):
                                last = nc.tensor.matmul(dst, g[w][:, k, i * P:i * P + P], g[m][:, k, :],
                                                        start=(k == 0 and n == 0), stop=(k == KD - 1 and n == 2))
                        else:
                            last = nc.tensor.matmul(dst, xw[:, k, 1, i * P:i * P + P], g["cT"][:, k, :], start=(k == 0), stop=(k == KD - 1))
                elif kind == "v":
                    if l == 0:
                        tok, half = i // 2, i % 2
                        for k in range(KD):
                            for n, (m, w) in enumerate((("cT_hi", "wkv_hi"), ("cT_hi", "wkv_lo"), ("cT_lo", "wkv_hi"))):
                                last = nc.tensor.matmul(dst, g[m][:, k, tok * P:tok * P + P],
                                                        g[w][:, k, INNER + half * 512:INNER + half * 512 + 512],
                                                        start=(k == 0 and n == 0), stop=(k == KD - 1 and n == 2))
                    else:
                        for tok in (2 * i, 2 * i + 1):
                            for k in range(KD):
                                last = nc.tensor.matmul(dst[:, (tok % 2) * D:(tok % 2) * D + D], g["cT"][:, k, tok * P:tok * P + P],
                                                        xw[:, k, 2, :], start=(k == 0), stop=(k == KD - 1))
                else:
                    if i == 0:
                        pe.wait_ge(c.fill_free[1], c.per * t + c.first["lat"] // 2 + 2)
                    for j4 in range(4 if l == 0 else 1):
                        grp = 4 * i + j4 if l == 0 else i
                        for k in range(KD):
                            last = nc.tensor.matmul(dst[:, j4 * P:j4 * P + P], g["wq"][:, k, grp * P:grp * P + P], g["latT"][:, k, :],
                                                    start=(k == 0), stop=(k == KD - 1))
                last.then_inc(c.fill_done[bank], 1)

            def scores(t, s, un):
                n, b, hf = 4 * t + un, un // 2, un % 2
                if un == 0:
                    for bank in range(2):
                        pe.wait_ge(c.fill_free[bank], c.per * t + c.first["v"] // 2 + 1)
                    if l == 1:
                        pe.wait_ge(c.q_spread, 2 * t + 2)
                pe.wait_ge(c.s_free if l == 0 else c.exp_done, n + 1)
                if l == 1:
                    for two in range(2):
                        nc.tensor.matmul(ps[:, XS + two, :], row0b[:, :],
                                         pad2(t, b), start=True, stop=False, skip_group_check=True)
                for j in range(4):
                    p = 4 * hf + j
                    last = nc.tensor.matmul(ps[:, XS + j // 2, (j % 2) * S:(j % 2) * S + S], g["qbd"][s][:, b, p, :],
                                            g["kT"][s][:, p if l == 0 else hf, b * S:b * S + S],
                                            start=(l == 0), stop=True, skip_group_check=True)
                last.then_inc(c.s_done, 1)

            def pad2(t, b):
                one = padneg[:, bass.ds(2 * t + b, 1), :]
                return one.broadcast_to((P, 2, S))

            def transposed(t, un):
                n = 4 * t + un
                pe.wait_ge(c.norm_done, n + 1)
                for bank in range(2):
                    pe.wait_ge(c.pT_free[bank], n + 1)
                    for i in range(4):
                        j, kt = 2 * bank + i // 2, i % 2
                        last = nc.tensor.transpose(ps[:, XT[bank], i * P:i * P + P], g["p"][un % 2][:, j, kt * P:kt * P + P], ident)
                    last.then_inc(c.pT_done[bank], 1)

            def values(t, s, un):
                n, b, hf = 4 * t + un, un // 2, un % 2
                for bank in range(2):
                    if un == 0:
                        pe.wait_ge(c.fill_free[bank], c.per * (t + 1) + 1)
                    pe.wait_ge(c.pT_free[bank], n + 2)
                pe.wait_ge(c.pv_free, n + 1)
                for j in range(4):
                    p = 4 * hf + j
                    for kt in range(2):
                        if l == 0:
                            dst, w = ps[:, XV, j * P:j * P + P], g["v"][s][:, 2 * b + kt, p * P:p * P + P]
                        else:
                            dst, w = ps[32 * j:32 * j + 32, XV, 0:P], g["v"][s][:, 2 * b + kt, p * 32:p * 32 + 32]
                        last = nc.tensor.matmul(dst, w, g["pT"][un % 2][:, 2 * j + kt, :], start=(kt == 0), stop=(kt == 1))
                last.then_inc(c.pv_done, 1)

            def project(t):
                pe.wait_ge(c.y_free, t + 1)
                pe.wait_ge(c.pv_free, 4 * t + 5)
                for k in range(c.kg):
                    last = nc.tensor.matmul(ps[:, XY, 0:D], g["attT"][:, k, :], g["wo"][:, k, :], start=(k == 0), stop=(k == c.kg - 1))
                last.then_inc(c.y_done, 1)

            if l == 1:
                pe.wait_ge(ld["xw"], 64)
                pe.wait_ge(MO.pad, 2)
            for j in range(len(c.fills)):
                if l == 0 and c.fills[j] in "qkv" and j == c.first[c.fills[j]]:
                    pe.wait_ge(*{"q": (ld["x0q"], 16), "k": (c.w_lo, KD), "v": (c.w_lo, 2 * KD)}[c.fills[j]])
                fill(0, 0, j)
            scores(0, 0, 0)
            scores(0, 0, 1)
            if l == 0:
                pe.wait_ge(ld["x0o"], 16)

            def step(t, s, nxt):
                for un in range(4):
                    transposed(t, un)
                    if un < 2:
                        scores(t, s, un + 2)
                    elif nxt:
                        scores(t + 1, 1 - s, un - 2)
                    values(t, s, un)
                    if nxt:
                        for j in range(*c.groups[un]):
                            fill(t + 1, 1 - s, j)
                project(t)

            tiles(pe, step)

        def evacuate(eng, c, t, s, j):
            g, l = c.g, c.l
            kind, i, bank, m = c.fills[j], j - c.first[c.fills[j]], j % 2, c.per * t + j // 2
            src = ps[:, XF[bank], :]

            def put(dst, src, scale=None, bias=None):
                if bank == 0:
                    if scale is None and bias is None:
                        return nc.scalar.activation(dst, src, ACT.Copy)
                    return nc.scalar.activation(dst, src, ACT.Identity, bias=bias, scale=1.0 if scale is None else scale)
                if scale is None and bias is None:
                    return nc.vector.tensor_copy(dst, src)
                if scale is None:
                    return nc.vector.tensor_scalar(dst, src, bias, None, ALU.add)
                return nc.vector.tensor_scalar(dst, src, scale, bias, ALU.mult, ALU.add)

            eng.wait_ge(c.fill_done[bank], m + 1)
            if kind == "cT":
                last = put(g["cT"][:, i, :], src, vec("ln_c_w", i), vec("ln_c_b", i)) if l == 0 else put(g["cT"][:, i, :], src)
            elif kind == "lat":
                last = put(g["latT"][:, i, :], src[:, 0:P], vec("ln_l_w", i), vec("ln_l_b", i)) if l == 0 else put(g["latT"][:, i, :], src[:, 0:P])
            elif kind == "k":
                last = put(g["kT"][s][:, i, :], src) if l == 0 else put(g["kT"][s][:, i, :], src, None, vec("xbk", i))
            elif kind == "v":
                if l == 0:
                    last = put(g["v"][s][:, i // 2, (i % 2) * 512:(i % 2) * 512 + 512], src)
                else:
                    last = put(g["v"][s][:, 2 * i:2 * i + 2, :], src)
            elif l == 0:
                for par in range(2):
                    r = slice(64 * par, 64 * par + 64)
                    last = put(g["qbd"][s][r, :, 4 * i:4 * i + 4, 64 * par:64 * par + 64].rearrange("p b j n -> p j b n"),
                               src[r, :].rearrange("p (j b n) -> p j b n", j=4, b=2))
            else:
                last = put(g["qs"][:, i, :], src[:, 0:P], None, vec("xbq", i))
            last.then_inc(c.fill_free[bank], 1)

        def act_cross(act, c):
            g, l = c.g, c.l

            def exps(t, un):
                n, slot = 4 * t + un, un % 2
                act.wait_ge(c.clip_done, n + 1)
                for j in range(4):
                    if l == 0:
                        last = nc.scalar.activation(g["p"][slot][:, j, :], g["p"][slot][:, j, :], ACT.Exp, scale=64.0 ** -0.5,
                                                    accum_out=g["sum"][:, slot, j:j + 1])
                    else:
                        if j == 0:
                            act.wait_ge(c.p_free, n + 1)
                        last = nc.scalar.activation(g["p"][slot][:, j, :], ps[:, XS + j // 2, (j % 2) * S:(j % 2) * S + S], ACT.Exp,
                                                    bias=g["nmax"][:, slot, j:j + 1], scale=0.25, accum_out=g["sum"][:, slot, j:j + 1])
                last.then_inc(c.exp_done, 1)

            def move_pT(t, un):
                n = 4 * t + un
                act.wait_ge(c.pT_done[0], n + 1)
                nc.scalar.activation(g["pT"][un % 2][:, 0:4, :], ps[:, XT[0], :], ACT.Copy).then_inc(c.pT_free[0], 1)

            act.sem_inc(c.fill_free[0], 1)
            act.sem_inc(c.pT_free[0], 1)
            if l == 1:
                act.sem_inc(c.exp_done, 1)
            for j in range(0, len(c.fills), 2):
                if l == 0 and c.fills[j] in "kv" and j == c.first[c.fills[j]]:
                    act.wait_ge(ld["x0" + c.fills[j]], 16)
                    part = slice(0, INNER) if c.fills[j] == "k" else slice(INNER, 2 * INNER)
                    for k in range(KD):
                        nc.scalar.activation(g["wkv_hi"][:, k, part], g["wkv"][:, k, part], ACT.Copy).then_inc(c.w_hi, 1)
                evacuate(act, c, 0, 0, j)
            exps(0, 0)
            exps(0, 1)

            def step(t, s, nxt):
                for un in range(4):
                    move_pT(t, un)
                    todo = [j for j in range(*c.groups[un]) if j % 2 == 0] if nxt else []
                    early = 2 if un == 0 else 1 if l == 0 or un < 2 else 0
                    for j in todo[:early]:
                        evacuate(act, c, t + 1, 1 - s, j)
                    if un < 2:
                        exps(t, un + 2)
                    elif nxt:
                        exps(t + 1, un - 2)
                    for j in todo[early:]:
                        evacuate(act, c, t + 1, 1 - s, j)

            tiles(act, step)

        def dve_cross(dve, c):
            g, l = c.g, c.l

            def norm(t, s, part):
                xt = x[:, bass.ds(t, 1), :].rearrange("p a d -> p (a d)")
                if l == 0:
                    srcs = [g["cin"][:, s, k, :] for k in range(4)] + [xt]
                    dsts = [g["cn"][:, k, :] for k in range(4)] + [g["lat"][:, :]]
                    if part == 0:
                        dve.wait_ge(ld_ctx[0][s], 8 * (t - s) + 16)
                        ln_first(dve, srcs[:3])
                    elif part == 1:
                        ln_statistics(dve, srcs, 2 * t, 3)
                    elif part == 2:
                        ln_apply(dve, srcs, dsts, 2 * t)
                        dve.wait_ge(ln_done, 2 * t + 1)
                        ln_statistics(dve, [g["lat"][:, :]], 2 * t + 1)
                    else:
                        ln_apply(dve, [g["lat"][:, :]], [g["lat"][:, :]], 2 * t + 1)
                elif part == 1:
                    row_apply(dve, t, xt, [g["lat"][:, :]], "x1")

            def split_cT(t):
                for bank in range(2):
                    dve.wait_ge(c.fill_free[bank], c.per * t + c.first["cT"] // 2 + 2)
                nc.vector.tensor_copy(g["cT_hi"][:, :, :], g["cT"][:, :, :]).then_inc(c.cT_hi, 1)
                dve.wait_ge(c.cT_hi, t + 1)
                nc.vector.tensor_tensor(g["cT_lo"][:, :, :], g["cT"][:, :, :], g["cT_hi"][:, :, :].bitcast(F32), ALU.subtract).then_inc(c.cT_lo, 1)

            def read_scores(t, un):
                n, slot = 4 * t + un, un % 2
                dve.wait_ge(c.s_done, n + 1)
                sc = ps[:, XS:XS + 2, :].rearrange("p a (j k) -> p (a j) k", j=2)
                if l == 0:
                    nc.vector.tensor_scalar(g["p"][slot][:, :, :], sc, 11.0 * 8.0, -11.0 * 8.0, ALU.min, ALU.max).then_inc(c.clip_done, 1)
                    dve.wait_ge(c.clip_done, n + 1)
                    dve.sem_inc(c.s_free, 1)
                else:
                    nc.vector.tensor_reduce(g["sum"][:, slot, :], sc, AX_X, ALU.max).then_inc(c.max_done, 1)
                    dve.wait_ge(c.max_done, n + 1)
                    nc.vector.tensor_scalar(g["nmax"][:, slot, :], g["sum"][:, slot, :], -0.25, None, ALU.mult).then_inc(c.clip_done, 1)

            def invert(t, un):
                n, slot = 4 * t + un, un % 2
                dve.wait_ge(c.exp_done, n + 1 + l)
                nc.vector.reciprocal(g["rinv"][:, slot, :], g["sum"][:, slot, :]).then_inc(c.rinv_done, 1)

            def move_pT(t, un):
                n = 4 * t + un
                dve.wait_ge(c.pT_done[1], n + 1)
                dve.sem_inc(c.p_free, 1)
                nc.vector.tensor_copy(g["pT"][un % 2][:, 4:8, :], ps[:, XT[1], :]).then_inc(c.pT_free[1], 1)

            def pick(t, un):
                n, b, hf = 4 * t + un, un // 2, un % 2
                dve.wait_ge(c.pv_done, n + 1)
                cols = slice(64 * b, 64 * b + 64)
                if l == 0:
                    for par in range(2):
                        r = slice(64 * par, 64 * par + 64)
                        last = nc.vector.tensor_copy(g["attT"][r, 4 * hf:4 * hf + 4, cols],
                                                     ps[r, XV, :].rearrange("p (j m) -> p j m", j=4)[:, :, 64 * par:64 * par + 64])
                else:
                    nc.vector.tensor_scalar(g["pv0"][:, :], ps[:, XV, 0:N], par_of[:, 0:1], vec("xbv", hf), ALU.mult, ALU.add).then_inc(c.pv0_done, 1)
                    dve.wait_ge(c.pv0_done, n + 1)
                    last = nc.vector.scalar_tensor_tensor(g["attT"][:, hf, cols], ps[:, XV, N:2 * N], par_of[:, 1:2], g["pv0"][:, :], ALU.mult, ALU.add)
                last.then_inc(c.pv_free, 1)

            def residual(t, s):
                xt = x[:, bass.ds(t, 1), :].rearrange("p a d -> p (a d)")
                dve.wait_ge(c.y_done, t + 1)
                nc.vector.tensor_tensor(xt, ps[:, XY, 0:D], xt, ALU.add).then_inc(c.y_free, 1)
                dve.wait_ge(c.y_free, t + 2)
                nc.vector.tensor_tensor(xt, xt, rows[:, 0 if l == 0 else 2, :], ALU.add).then_inc(c.x_done, 1)
                dve.wait_ge(c.x_done, t + 1)
                row_statistics(dve, xt, s, ROW_BASE[c.next] + t)

            if l == 0:
                dve.sem_inc(rn_rstd, 2)
            for k, v in ((c.fill_free[1], 1), (c.s_free, 1), (c.pT_free[1], 1), (c.pv_free, 1), (c.y_free, 1), (c.p_free, 2)):
                dve.sem_inc(k, v)
            if l == 0:
                for s in range(2):
                    nc.vector.memset(g["qbd"][s][:, :, :, :], 0.0).then_inc(c.q_spread, 1)
                dve.wait_ge(c.q_spread, 2)
            if l == 0:
                for part in range(4):
                    norm(0, 0, part)
            for j in range(1, len(c.fills), 2):
                if l == 0 and c.fills[j] in "kv" and j == c.first[c.fills[j]] + 1:
                    part = slice(0, INNER) if c.fills[j] == "k" else slice(INNER, 2 * INNER)
                    for k in range(KD):
                        dve.wait_ge(c.w_hi, (0 if c.fills[j] == "k" else KD) + k + 1)
                        nc.vector.tensor_tensor(g["wkv_lo"][:, k, part], g["wkv"][:, k, part], g["wkv_hi"][:, k, part].bitcast(F32),
                                                ALU.subtract).then_inc(c.w_lo, 1)
                evacuate(dve, c, 0, 0, j)
                if l == 1 and j < 8:
                    row_statistics(dve, x[:, 4 + j // 2, :], j // 2 % 2, ROW_BASE["x1"] + 4 + j // 2)
                if l == 0 and j == c.first["cT"] + 1:
                    split_cT(0)
                if l == 0 and c.fills[j] == "v":
                    part = (j - c.first["v"]) // 2
                    if part == 2:
                        dve.wait_ge(c.fill_done[0], 2)
                        dve.wait_ge(c.fill_done[1], 2)
                    norm(1, 1, part)
            read_scores(0, 0)
            if l == 1:
                for bank in range(2):
                    dve.wait_ge(c.fill_done[bank], 2)
                norm(1, 1, 1)
            invert(0, 0)
            read_scores(0, 1)
            if l == 0:
                dve.wait_ge(ld["x_rest"], 16)
                dve.wait_ge(ld["rows"], 16)

            def step(t, s, nxt, more):
                for un in range(4):
                    move_pT(t, un)
                    if un < 3:
                        invert(t, un + 1)
                    elif nxt:
                        invert(t + 1, 0)
                    if un < 2:
                        read_scores(t, un + 2)
                    elif nxt:
                        read_scores(t + 1, un - 2)
                    pick(t, un)
                    if nxt:
                        for j in range(*c.groups[un]):
                            if j % 2 == 1:
                                evacuate(dve, c, t + 1, 1 - s, j)
                            if l == 0 and j == c.first["cT"] + 1:
                                split_cT(t + 1)
                    if more:
                        if un == 2 - l:
                            dve.wait_ge(c.fill_done[0], c.per * (t + 1) + 2)
                            dve.wait_ge(c.fill_done[1], c.per * (t + 1) + 2)
                        norm(t + 2, s, un)
                residual(t, s)

            tiles2(dve, step)

        def pool_cross(pool, c):
            g, l = c.g, c.l

            def norm(t, part):
                if l == 0:
                    ln_rstd_pool(pool, (5, 1)[part], 2 * t + part)

            def spread_q(t, s):
                for i in range(KD):
                    if i == 0:
                        for bank in range(2):
                            pool.wait_ge(c.fill_free[bank], c.per * t + c.first["q"] // 2 + 2)
                    q = g["qs"][:, i, :].rearrange("p (b n) -> p b n", b=2)
                    for b in range(2):
                        last = nc.gpsimd.tensor_tensor(g["qbd"][s][:, b, 4 * i:4 * i + 4, :].rearrange("p j (a n) -> p (j a) n", a=2),
                                                q[:, b:b + 1, :].broadcast_to((P, 8, N)),
                                                head_of.rearrange("p (h o) -> p h o", o=1).broadcast_to((P, 8, N)), ALU.mult)
                    last.then_inc(c.q_spread, 1)

            def scale_p(t, un):
                n, slot = 4 * t + un, un % 2
                pool.wait_ge(c.rinv_done, n + 1)
                nc.gpsimd.tensor_tensor(g["p"][slot][:, :, :], g["p"][slot][:, :, :],
                                        g["rinv"][:, slot, :].rearrange("p (j o) -> p j o", o=1).broadcast_to((P, 4, S)),
                                        ALU.mult).then_inc(c.norm_done, 1)

            norm(0, 0)
            norm(0, 1)
            norm(1, 0)
            norm(1, 1)
            if l == 1:
                spread_q(0, 0)
            scale_p(0, 0)
            with pool.Fori(0, T // 2 - 1) as i:
                for s in range(2):
                    t = 2 * i + s
                    scale_p(t, 1)
                    if l == 1:
                        spread_q(t + 1, 1 - s)
                    scale_p(t, 2)
                    norm(t + 2, 0)
                    scale_p(t, 3)
                    norm(t + 2, 1)
                    scale_p(t + 1, 0)
                    row_rstd(pool, t, s, c.next)
            for un in range(1, 8):
                scale_p(T - 2 + un // 4, un % 4)
                if l == 1 and un == 1:
                    spread_q(T - 1, 1)
                if un == 4:
                    row_rstd(pool, T - 2, 0, c.next)
            row_rstd(pool, T - 1, 1, c.next)

        y_at = ctx_views(a["ctx_1024"])

        LAYERS, NEXT = ("mla", "ffn", "attn"), ("ffn", "moe", "mlp")
        class SA:
            hT_ps = sem("sa_hT_ps")
            hT = sem("sa_hT")
            lat_ps = sem("sa_lat_ps")
            lat = sem("sa_lat")
            rope_ps = sem("sa_rope_ps")
            roped0 = sem("sa_roped0")
            rope = sem("sa_rope")
            q_ps = sem("sa_q_ps")
            q = sem("sa_q")
            k_ps = sem("sa_k_ps")
            v_ps = sem("sa_v_ps")
            kbd = sem("sa_kbd")
            vbd = sem("sa_vbd")
            s_ps = sem("sa_s_ps")
            max = sem("sa_max")
            sub = sem("sa_sub")
            exp = sem("sa_exp")
            sum = sem("sa_sum")
            rinv = sem("sa_rinv")
            norm = sem("sa_norm")
            pT_ps = sem("sa_pT_ps")
            pT = sem("sa_pT")
            att_ps = sem("sa_att_ps")
            att = sem("sa_att")
            y_ps = sem("sa_y_ps")
            y_free = sem("sa_y_free")
            x_done = sem("sa_x_done")

        def pe_self(pe, L):
            sq = w_sq[0 if L == 1 else 1]
            g0, v_bank = T * L, 1 if L == 0 else 2

            def rows_T(t):
                pe.wait_ge(rn_done, ROW_BASE[LAYERS[L]] + t + 1)
                if not isinstance(t, int) or t > 0:
                    pe.wait_ge(SA.q, g0 + t)
                for k in range(KD):
                    last = nc.tensor.transpose(ps[:, 0, k * P:k * P + P], h[:, k * P:k * P + P], ident)
                last.then_inc(SA.hT_ps, 1)

            def project_qk(t):
                g = g0 + t
                pe.wait_ge(SA.hT, g + 1)
                if L == 0:
                    for k in range(KD):
                        last = nc.tensor.matmul(ps[:, 0, 256:384], w_mla[:, k, 0:P], hT[:, k, :], start=(k == 0), stop=(k == 1))
                    last.then_inc(SA.lat_ps, 1)
                    for i in range(4):
                        for k in range(KD):
                            last = nc.tensor.matmul(ps[:, 2, i * P:i * P + P], w_mla[:, k, P + i * P:2 * P + i * P], hT[:, k, :],
                                                    start=(k == 0), stop=(k == 1))
                    last.then_inc(SA.rope_ps, 1)
                else:
                    for bank, at0, w, done in ((1, 0, 1, SA.k_ps), (0, 256, 0, SA.q_ps)):
                        for i in range(KD):
                            for k in range(KD):
                                last = nc.tensor.matmul(ps[:, bank, at0 + i * P:at0 + i * P + P], sq[:, k, w, i * P:i * P + P], hT[:, k, :],
                                                        start=(k == 0), stop=(k == 1))
                        last.then_inc(done, 1)

            def project_v(t):
                g = g0 + t
                if L == 0:
                    pe.wait_ge(SA.lat, g + 1)
                    nc.tensor.matmul(ps[:, 0, 384:512], w_mlac[:, 0:P], cqkvT[:, :], start=True, stop=True)
                    nc.tensor.matmul(ps[:, 0, 0:P], w_mlac[:, P:2 * P], cqkvT[:, :], start=True, stop=True).then_inc(SA.q_ps, 1)
                pe.wait_ge(SA.vbd, g + 1)
                ks = 1 if L == 0 else KD
                for b in range(2):
                    for k in range(ks):
                        for par in range(2):
                            w = w_mlac[:, 2 * P:2 * P + D] if L == 0 else sq[:, k, 2, :]
                            v_in = cqkvT[:, 64 * b:64 * b + 64] if L == 0 else hT[:, k, 64 * b:64 * b + 64]
                            last = nc.tensor.matmul(ps[64 * par:64 * par + 64, v_bank, 256 + P * b:256 + P * b + P], v_in,
                                                    w.rearrange("p (j a d) -> p a j d", a=2, d=16)[:, par, :, :],
                                                    start=(k == 0), stop=(k == ks - 1), skip_group_check=True)
                last.then_inc(SA.v_ps, 1)

            def scores(t):
                g = g0 + t
                pe.wait_ge(SA.q, g + 1)
                pe.wait_ge(SA.kbd, g + 1)
                for hf in range(KD):
                    if L != 1:
                        nc.tensor.matmul(ps[:, 3 + hf, :], identb[:, :], causalb[:, :].rearrange("p (o n) -> p o n", o=1).broadcast_to((P, 8, N)),
                                         start=True, stop=False, skip_group_check=True)
                    for b in range(2):
                        last = nc.tensor.matmul(ps[64 * b:64 * b + 64, 3 + hf, :], qT[:, hf, 64 * b:64 * b + 64],
                                                kbd[:, hf, b, :, :].rearrange("p h n -> p (h n)"), start=(L == 1), stop=True, skip_group_check=True)
                last.then_inc(SA.s_ps, 1)

            def probs_T(t):
                g = g0 + t
                pe.wait_ge(SA.norm, g + 1)
                for j in range(8):
                    last = nc.tensor.transpose(ps[:, 5 + j // 4, (j % 4) * P:(j % 4) * P + P],
                                               pr[:, 2 * j:2 * j + 2, :].rearrange("p h n -> p (h n)"), ident)
                last.then_inc(SA.pT_ps, 1)

            def values(t, s):
                g = g0 + t
                pe.wait_ge(SA.pT, g + 1)
                pe.wait_ge(SA.vbd, g + 2)
                pe.wait_ge(SA.y_free, g + 1)
                for j in range(8):
                    for b in range(2):
                        last = nc.tensor.matmul(ps[32 * (j % 4):32 * (j % 4) + 32, 7, (j // 4) * P + 64 * b:(j // 4) * P + 64 * b + 64],
                                                vbd[s][:, b, j, :, :].rearrange("p a d -> p (a d)"), prT[:, j, 64 * b:64 * b + 64],
                                                start=True, stop=True, skip_group_check=True)
                last.then_inc(SA.att_ps, 1)

            def output(t):
                g = g0 + t
                pe.wait_ge(SA.att, g + 1)
                for k in range(KD):
                    w = w_mlao[:, k, :] if L == 0 else sq[:, k, 3, :]
                    last = nc.tensor.matmul(ps[:, 7, 256:512], sattT[:, k, :], w, start=(k == 0), stop=(k == 1))
                last.then_inc(SA.y_ps, 1)

            pe.wait_ge(ld["mla"] if L == 0 else ld["sq0"] if L == 1 else ld["sq1"], 160 if L == 0 else 64)
            pe.wait_ge(setup, 5)
            rows_T(0)
            project_qk(0)
            project_v(0)
            rows_T(1)
            scores(0)
            project_qk(1)
            project_v(1)

            def step(t, s, nxt, more):
                probs_T(t)
                if more and L == 0:
                    rows_T(t + 2)
                if nxt:
                    scores(t + 1)
                if more and L == 0:
                    project_qk(t + 2)
                values(t, s)
                output(t)
                if more:
                    if L > 0:
                        rows_T(t + 2)
                        project_qk(t + 2)
                    project_v(t + 2)

            tiles2(pe, step)

        def act_self(act, L):
            g0 = T * L

            def rows_T(t):
                act.wait_ge(SA.hT_ps, g0 + t + 1)
                if L == 1:
                    for k in range(KD):
                        last = nc.scalar.activation(hT[:, k, :], ps[:, 0, k * P:k * P + P], ACT.Identity, bias=vec("ln1_b", k), scale=vec("ln1_g", k))
                else:
                    last = nc.scalar.activation(hT[:, :, :], ps[:, 0, 0:256], ACT.Copy)
                last.then_inc(SA.hT, 1)

            def latent(t):
                act.wait_ge(SA.lat_ps, g0 + t + 1)
                nc.scalar.activation(cqkvT[:, :], ps[:, 0, 256:384], ACT.Gelu, bias=vec("bqkv")).then_inc(SA.lat, 1)

            def project(t):
                g = g0 + t
                act.wait_ge(SA.q_ps, g + 1)
                if L == 0:
                    nc.scalar.activation(qT[:, 0, :], ps[:, 0, 384:512], ACT.Gelu, bias=vec("bqc"))
                    nc.scalar.activation(kTs[:, 0, :], ps[:, 0, 0:P], ACT.Gelu, bias=vec("bkc"))
                    act.wait_ge(SA.rope, g + 1)
                    nc.scalar.activation(qT[:, 1, :], rope[:, 0, :], ACT.Gelu)
                    nc.scalar.activation(kTs[:, 1, :], rope[:, 2, :], ACT.Gelu).then_inc(SA.q, 1)
                else:
                    nc.scalar.activation(qT[:, :, :], ps[:, 0, 256:512], ACT.Copy).then_inc(SA.q, 1)

            def exps(t):
                act.wait_ge(SA.sub, g0 + t + 1)
                nc.scalar.activation(pr[:, :, :], pr[:, :, :], ACT.Exp, scale=0.25).then_inc(SA.exp, 1)

            def probs_T(t):
                act.wait_ge(SA.pT_ps, g0 + t + 1)
                for i in range(2):
                    last = nc.scalar.activation(prT[:, 4 * i:4 * i + 4, :], ps[:, 5 + i, :], ACT.Copy)
                last.then_inc(SA.pT, 1)

            def spread_v(t, s):
                act.wait_ge(SA.v_ps, g0 + t + 1)
                v = ps[:, 1 if L == 0 else 2, 256:512].rearrange("p (b j d) -> p b j d", b=2, j=8)
                for par in range(2):
                    r = slice(64 * par, 64 * par + 64)
                    last = nc.scalar.activation(vbd[s][r, :, :, par, :], v[r, :, :, :], ACT.Copy)
                last.then_inc(SA.vbd, 1)

            def attention(t):
                act.wait_ge(SA.att_ps, g0 + t + 1)
                if L == 0:
                    for k in range(KD):
                        last = nc.scalar.activation(sattT[:, k, :], ps[:, 7, k * P:k * P + P], ACT.Identity, bias=vec("bv0", k))
                else:
                    last = nc.scalar.activation(sattT[:, :, :], ps[:, 7, 0:256], ACT.Copy)
                last.then_inc(SA.att, 1)

            if L == 2:
                act.wait_ge(pool_setup, 8)
            if L == 0:
                act.sem_inc(SA.vbd, 1)
                act.wait_ge(setup, 5)
            for t in range(2):
                rows_T(t)
                if L == 0:
                    latent(t)
                if t == 1:
                    exps(0)
                project(t)
                spread_v(t, t)

            def step(t, s, nxt, more):
                probs_T(t)
                if more and L == 0:
                    rows_T(t + 2)
                    latent(t + 2)
                if L > 0:
                    attention(t)
                if nxt:
                    exps(t + 1)
                if L == 0:
                    attention(t)
                if more:
                    if L > 0:
                        rows_T(t + 2)
                    project(t + 2)
                    spread_v(t + 2, s)
                if L == 2:
                    act_ff_weights(act, t)
                if L == 1 and nxt and not more:
                    for i in range(4):
                        expert_upper(act, 0, 0, i)

            tiles2(act, step)

        def dve_self(dve, L, x_sem, x_val):
            g0 = T * L

            def norm(t):
                xt = x[:, bass.ds(t, 1), :].rearrange("p a d -> p (a d)")
                ut = u[:, bass.ds(t, 1), :].rearrange("p a d -> p (a d)")
                if not isinstance(t, int) or g0 + t > 0:
                    dve.wait_ge(SA.hT_ps, g0 + t)
                row_apply(dve, t, xt, [ut, h[:, :]] if L == 1 else [h[:, :]], LAYERS[L])

            def rotate(t):
                g = g0 + t
                dve.wait_ge(SA.rope_ps, g + 1)
                cos, sin = cst[:, C_COS:C_COS + P], cst[:, C_SIN:C_SIN + P]
                for i, (bias, tab) in enumerate((("bqr", cos), ("bqs", sin), ("bkr", cos), ("bks", sin))):
                    last = nc.vector.scalar_tensor_tensor(rope[:, i, :], ps[:, 2, i * P:i * P + P], vec(bias), tab, ALU.add, ALU.mult)
                last.then_inc(SA.roped0, 1)
                dve.wait_ge(SA.roped0, g + 1)
                nc.vector.tensor_tensor(rope[:, 0, :], rope[:, 0, :], rope[:, 1, :], ALU.add)
                nc.vector.tensor_tensor(rope[:, 2, :], rope[:, 2, :], rope[:, 3, :], ALU.add).then_inc(SA.rope, 1)

            def spread_k(t):
                if L == 0:
                    dve.wait_ge(SA.q, g0 + t + 1)
                else:
                    dve.wait_ge(SA.k_ps, g0 - T + t + 1)
                for hf in range(KD):
                    for b in range(2):
                        src = kTs[:, hf, 64 * b:64 * b + 64] if L == 0 else ps[:, 1, hf * P + 64 * b:hf * P + 64 * b + 64]
                        last = nc.vector.tensor_tensor(kbd[:, hf, b, :, :], src.rearrange("p (o n) -> p o n", o=1).broadcast_to((P, 8, N)),
                                                       head_of.rearrange("p (h o) -> p h o", o=1).broadcast_to((P, 8, N)), ALU.mult)
                last.then_inc(SA.kbd, 1)

            def softmax_a(t):
                g = g0 + t
                sc = ps[:, 3:5, :].rearrange("p a (h n) -> p (a h) n", n=N)
                dve.wait_ge(SA.s_ps, g + 1)
                nc.vector.tensor_reduce(smax[:, :], sc, AX_X, ALU.max).then_inc(SA.max, 1)
                dve.wait_ge(SA.max, g + 1)
                nc.vector.tensor_tensor(pr[:, :, :], sc, smax[:, :].rearrange("p (h o) -> p h o", o=1).broadcast_to((P, H, N)),
                                        ALU.subtract).then_inc(SA.sub, 1)

            def softmax_b(t):
                g = g0 + t
                dve.wait_ge(SA.exp, g + 1)
                nc.vector.tensor_reduce(ssum[:, :], pr[:, :, :], AX_X, ALU.add).then_inc(SA.sum, 1)
                dve.wait_ge(SA.sum, g + 1)
                nc.vector.reciprocal(srinv[:, :], ssum[:, :]).then_inc(SA.rinv, 1)

            def residual(t, s):
                g = g0 + t
                xt = x[:, bass.ds(t, 1), :].rearrange("p a d -> p (a d)")
                ut = u[:, bass.ds(t, 1), :].rearrange("p a d -> p (a d)")
                dve.wait_ge(SA.y_ps, g + 1)
                first = ut if L == 1 else xt
                nc.vector.tensor_tensor(first, ps[:, 7, 256:512], first, ALU.add).then_inc(SA.y_free, 1)
                dve.wait_ge(SA.y_free, g + 2)
                if L == 0:
                    nc.vector.tensor_tensor(xt, xt, rows[:, 1, :], ALU.add).then_inc(SA.x_done, 1)
                elif L == 2:
                    dve.sem_inc(SA.x_done, 1)
                if L == 0:
                    dve.wait_ge(SA.x_done, g + 1)
                row_statistics(dve, ut if L == 1 else xt, s, ROW_BASE[NEXT[L]] + t)

            dve.wait_ge(x_sem, x_val)
            if L == 0:
                dve.sem_inc(SA.y_free, 1)
                for s in range(2):
                    nc.vector.memset(vbd[s][:, :, :, :, :], 0.0).then_inc(setup, 1)

            norm(0)
            norm(1)
            for t in range(2):
                if t == 1:
                    softmax_a(0)
                    softmax_b(0)
                if L == 0:
                    rotate(t)
                spread_k(t)

            def step(t, s, nxt, more):
                if more and L == 0:
                    norm(t + 2)
                if not isinstance(t, int) or t > 0:
                    residual(t - 1, 1 - s)
                if nxt:
                    softmax_a(t + 1)
                if more:
                    if L == 0:
                        rotate(t + 2)
                    else:
                        norm(t + 2)
                if nxt:
                    softmax_b(t + 1)
                if more:
                    spread_k(t + 2)
                elif L == 2:
                    dve_ff_weights(dve, t - (T - KD))
                elif L == 1:
                    for i in range(2):
                        expert_lower(dve, 0, 0, 2 * (t - (T - 2)) + i)

            step(0, 0, True, True)
            with dve.Fori(0, T // 2 - 2) as i:
                for s in range(2):
                    step(2 * i + s + 1, 1 - s, True, True)
            step(T - 3, 1, True, True)
            step(T - 2, 0, True, False)
            step(T - 1, 1, False, False)
            residual(T - 1, 1)

        def pool_self(pool, L):
            def scale_p(t):
                pool.wait_ge(SA.rinv, T * L + t + 1)
                nc.gpsimd.tensor_tensor(pr[:, :, :], pr[:, :, :], srinv[:, :].rearrange("p (h o) -> p h o", o=1).broadcast_to((P, H, N)),
                                        ALU.mult).then_inc(SA.norm, 1)

            def add_u(t):
                xt = x[:, bass.ds(t, 1), :].rearrange("p a d -> p (a d)")
                ut = u[:, bass.ds(t, 1), :].rearrange("p a d -> p (a d)")
                pool.wait_ge(SA.y_free, T * L + t + 2)
                pool.sem_inc(pool_go, 1)
                nc.gpsimd.tensor_tensor(xt, xt, ut, ALU.add).then_inc(SA.x_done, 1)

            def step(t, s, nxt):
                if nxt:
                    scale_p(t + 1)
                if L == 1:
                    add_u(t)
                row_rstd(pool, t, s, NEXT[L])

            scale_p(0)
            tiles(pool, step)

        class MO:
            mT_ps = sem("mo_mT_ps")
            mT = sem("mo_mT")
            router_ps = sem("mo_router_ps")
            logit = sem("mo_logit")
            top = sem("mo_top")
            topi = sem("mo_topi")
            diff = sem("mo_diff")
            exp = sem("mo_exp")
            w = sem("mo_w")
            sel = sem("mo_sel")
            gate = sem("mo_gate")
            gT_ps = sem("mo_gT_ps")
            gT = sem("mo_gT")
            b2_ps = sem("mo_b2_ps")
            b2 = sem("mo_b2")
            w1_ps = sem("mo_w1_ps")
            w1_free = sem("mo_w1_free")
            w_hi = sem("mo_w_hi")
            w_lo = sem("mo_w_lo")
            m_hi = sem("mo_m_hi")
            m_lo = sem("mo_m_lo")
            hi = sem("mo_hi")
            split = sem("mo_split")
            out_ps = sem("mo_out_ps")
            w2_free = sem("mo_w2_free")
            pad = sem("mo_pad")

        def expert_upper(act, e, s, i):
            if i == 0:
                act.wait_ge(ld_e[s], 16 * (e - s) + 32)
            hi, w, sl = ((ew1_hi, ew1, slice(i, i + 1)), (ew2_hi, ew2, slice(4 * i - 8, 4 * i - 4)))[i // 2]
            nc.scalar.activation(hi[s][:, sl, :], w[s][:, sl, :], ACT.Copy).then_inc(MO.w_hi, 1)

        def expert_lower(dve, e, s, i):
            dve.wait_ge(MO.w_hi, 4 * e + i + 1)
            lo, hi, w, sl = ((ew1_lo, ew1_hi, ew1, slice(i, i + 1)), (ew2_lo, ew2_hi, ew2, slice(4 * i - 8, 4 * i - 4)))[i // 2]
            nc.vector.tensor_tensor(lo[s][:, sl, :], w[s][:, sl, :], hi[s][:, sl, :].bitcast(F32), ALU.subtract).then_inc(MO.w_lo, 1)

        def pe_moe(pe):
            for t in range(T):
                pe.wait_ge(rn_done, ROW_BASE["moe"] + t + 1)
                pe.wait_ge(MO.mT, t + 1)
                for k in range(KD):
                    last = nc.tensor.transpose(ps[:, t % 2, k * P:k * P + P], u[:, t, k * P:k * P + P], ident)
                last.then_inc(MO.mT_ps, 1)
            pe.wait_ge(MO.mT, T + 2)
            pe.wait_ge(ld["wg"], 16)
            for t in range(T):
                for k in range(KD):
                    last = nc.tensor.matmul(ps[:, 4 + t // 4, (t % 4) * P:(t % 4) * P + P], mT[:, k, t * P:t * P + P], wg[:, k, :],
                                            start=(k == 0), stop=(k == 1), skip_group_check=True)
            last.then_inc(MO.router_ps, 1)

            def biases():
                pe.wait_ge(MO.gate, 1)
                for t in range(T):
                    last = nc.tensor.transpose(ps[:, 2 + t // 4, (t % 4) * P:(t % 4) * P + P], gate[:, t, :], ident)
                last.then_inc(MO.gT_ps, 1)
                pe.wait_ge(MO.gT, 1)
                pe.wait_ge(ld["b2"], 16)
                for t in range(T):
                    last = nc.tensor.matmul(ps[:, 4 + t // 2, (t % 2) * D:(t % 2) * D + D], gate_T[:, t * P:t * P + P], b2[:, :],
                                            start=True, stop=True, skip_group_check=True)
                last.then_inc(MO.b2_ps, 1)

            def hidden(e, s, k):
                c, f = divmod(k, FT)
                if k == 0:
                    pe.wait_ge(MO.w_lo, 4 * e + 4)
                pe.wait_ge(MO.w1_free, 2 * FT * e + k + 1)
                for i in range(KD):
                    for n, (w, m) in enumerate(((ew1_hi, mT_hi), (ew1_hi, mT_lo), (ew1_lo, mT_hi))):
                        last = nc.tensor.matmul(ps[:, k % 4, :], w[s][:, i, f * P:f * P + P], m[:, i, 512 * c:512 * c + 512],
                                                start=(i == 0 and n == 0), stop=(i == KD - 1 and n == 2))
                last.then_inc(MO.w1_ps, 1)

            def outputs(e, s, k):
                c, f = divmod(k, FT)
                pe.wait_ge(MO.split, 2 * FT * e + k + 3)
                for i in range(4):
                    if f == 0:
                        pe.wait_ge(MO.w2_free, 8 * e + 4 * c + i + 1)
                    for n, (m, w) in enumerate(((eh_hi, ew2_hi), (eh_hi, ew2_lo), (eh_lo, ew2_hi))):
                        last = nc.tensor.matmul(ps[:, 4 + i, 0:D], m[k % 2][:, i * P:i * P + P], w[s][:, f, :],
                                                start=(f == 0 and n == 0), stop=(f == FT - 1 and n == 2))
                last.then_inc(MO.out_ps, 1)

            pe.sem_inc(MO.out_ps, 2)
            pe.wait_ge(MO.m_lo, 2)
            hidden(0, 0, 0)
            hidden(0, 0, 1)
            biases()

            def step(e, s, nxt):
                for k in range(2 * FT):
                    if k + 2 < 2 * FT:
                        hidden(e, s, k + 2)
                    elif nxt:
                        hidden(e + 1, 1 - s, k + 2 - 2 * FT)
                    outputs(e, s, k)

            tiles(pe, step)

        def act_moe(act):
            act.sem_inc(MO.mT, 2)
            act.sem_inc(MO.w1_free, 4)

            for t in range(T):
                act.wait_ge(MO.mT_ps, t + 1)
                for k in range(KD):
                    last = nc.scalar.activation(mT[:, k, t * P:t * P + P], ps[:, t % 2, k * P:k * P + P], ACT.Identity,
                                                bias=vec("ln2_b", k), scale=vec("ln2_g", k))
                last.then_inc(MO.mT, 1)
            act.wait_ge(MO.diff, 1)
            nc.scalar.activation(gexp[:, :], gexp[:, :], ACT.Exp).then_inc(MO.exp, 1)

            def hidden(e, s, k):
                act.wait_ge(MO.w1_ps, 2 * FT * e + k + 1)
                act.wait_ge(MO.split, 2 * FT * e + k + 1)
                act.sem_inc(act_go, 1)
                nc.scalar.activation(eh[k % 2][:, :], ps[:, k % 4, :], ACT.Gelu_apprx_tanh,
                                     bias=col[:, bass.ds(e * FT + (COLS["b1"][0] + k % FT), 1)]).then_inc(MO.w1_free, 1)

            def step(e, s, nxt):
                for k in range(2, 2 * FT):
                    hidden(e, s, k)
                    if nxt and k >= FT and k % 2 == 0:
                        expert_upper(act, e + 1, 1 - s, (k - FT) // 2)
                if nxt:
                    hidden(e + 1, 1 - s, 0)
                    hidden(e + 1, 1 - s, 1)

            hidden(0, 0, 0)
            hidden(0, 0, 1)
            act.wait_ge(MO.gT_ps, 1)
            for i in range(2):
                last = nc.scalar.activation(gate_T[:, 512 * i:512 * i + 512], ps[:, 2 + i, :], ACT.Copy)
            last.then_inc(MO.gT, 1)
            tiles(act, step)

        def dve_moe(dve):
            dve.wait_ge(SA.x_done, 2 * T)
            dve.sem_inc(MO.split, 2)
            for t in range(T):
                row_apply(dve, t, u[:, t, :], [u[:, t, :]], "moe")

            for c in range(2):
                part = slice(512 * c, 512 * c + 512)
                dve.wait_ge(MO.mT, 4 * c + 6)
                nc.vector.tensor_copy(mT_hi[:, :, part], mT[:, :, part]).then_inc(MO.m_hi, 1)
                dve.wait_ge(MO.m_hi, c + 1)
                nc.vector.tensor_tensor(mT_lo[:, :, part], mT[:, :, part], mT_hi[:, :, part].bitcast(F32), ALU.subtract).then_inc(MO.m_lo, 1)
            dve.wait_ge(MO.router_ps, 1)
            for i in range(2):
                last = nc.vector.tensor_copy(logit[:, 4 * i:4 * i + 4, :], ps[:, 4 + i, :].rearrange("p (t e) -> p t e", e=P)[:, :, 0:E])
            last.then_inc(MO.logit, 1)
            dve.wait_ge(MO.logit, 1)
            for t in range(T):
                last = nc.vector.max(top[:, t, :], logit[:, t, :])
            last.then_inc(MO.top, 1)
            dve.wait_ge(MO.top, 1)
            nc.vector.tensor_tensor(gexp[:, :], top[:, :, 1], top[:, :, 0], ALU.subtract).then_inc(MO.diff, 1)
            for t in range(T):
                last = nc.vector.max_index(topi[:, t, :], top[:, t, :], logit[:, t, :])
            last.then_inc(MO.topi, 1)
            dve.wait_ge(MO.topi, 1)
            nc.vector.tensor_copy(topf[:, :, :], topi[:, :, 0:2]).then_inc(MO.topi, 1)
            dve.wait_ge(MO.exp, 1)
            nc.vector.tensor_scalar(gw[:, :, 2], gexp[:, :], 1.0, None, ALU.add).then_inc(MO.w, 1)
            dve.wait_ge(MO.w, 1)
            nc.vector.reciprocal(gw[:, :, 0], gw[:, :, 2]).then_inc(MO.w, 1)
            dve.wait_ge(MO.w, 2)
            nc.vector.tensor_tensor(gw[:, :, 1], gexp[:, :], gw[:, :, 0], ALU.mult).then_inc(MO.w, 1)
            dve.wait_ge(MO.topi, 2)
            iota = cst[:, C_IOTA:C_IOTA + E].rearrange("p (o e) -> p o e", o=1).broadcast_to((P, T, E))
            for i in range(2):
                last = nc.vector.tensor_tensor(gsel[:, :, i, :], iota, topf[:, :, i:i + 1].broadcast_to((P, T, E)), ALU.is_equal)
            last.then_inc(MO.sel, 1)
            dve.wait_ge(MO.sel, 1)
            dve.wait_ge(MO.w, 3)
            for i in range(2):
                last = nc.vector.tensor_tensor(gsel[:, :, i, :], gsel[:, :, i, :], gw[:, :, i:i + 1].broadcast_to((P, T, E)), ALU.mult)
            last.then_inc(MO.sel, 1)
            dve.wait_ge(MO.sel, 2)
            dve.wait_ge(pool_setup, 7)
            nc.vector.tensor_tensor(gate[:, :, 0:E], gsel[:, :, 0, :], gsel[:, :, 1, :], ALU.add).then_inc(MO.gate, 1)
            def rows(e, k):
                n = 2 * FT * e + k
                dve.wait_ge(MO.w1_free, n + 5)
                dve.wait_ge(MO.out_ps, n + 1)
                nc.vector.tensor_copy(eh_hi[k % 2][:, :], eh[k % 2][:, :]).then_inc(MO.hi, 1)
                dve.wait_ge(MO.hi, n + 1)
                nc.vector.tensor_tensor(eh_lo[k % 2][:, :], eh[k % 2][:, :], eh_hi[k % 2][:, :].bitcast(F32), ALU.subtract).then_inc(MO.split, 1)

            def add(e, c, final):
                dve.wait_ge(MO.out_ps, 2 * FT * e + FT * c + FT + 2)
                for i in range(4):
                    n = 8 * e + 4 * c + i
                    dve.wait_ge(MO.w2_free, n + 1)
                    nc.vector.scalar_tensor_tensor(x[:, 4 * c + i, :], ps[:, 4 + i, 0:D], gate[:, 4 * c + i, bass.ds(e, 1)], x[:, 4 * c + i, :],
                                                   ALU.mult, ALU.add).then_inc(MO.w2_free, 1)
                    if final and c == 0:
                        dve.wait_ge(MO.w2_free, n + 5)
                        row_statistics(dve, x[:, i, :], i % 2, ROW_BASE["x1"] + i)
                if final and c == 0:
                    row_apply(dve, 0, x[:, 0, :], [h[:, :]], "x1")

            def step(e, s, nxt):
                for k in range(2, 2 * FT):
                    rows(e, k)
                    if k == FT + 1:
                        add(e, 0, not nxt)
                    if nxt and k >= FT and k % 2 == 0:
                        expert_lower(dve, e + 1, 1 - s, (k - FT) // 2)
                if nxt:
                    rows(e + 1, 0)
                    rows(e + 1, 1)
                add(e, 1, not nxt)

            rows(0, 0)
            rows(0, 1)
            dve.wait_ge(MO.b2_ps, 1)
            for i in range(4):
                last = nc.vector.tensor_tensor(x[:, 2 * i:2 * i + 2, :], ps[:, 4 + i, :].rearrange("p (t d) -> p t d", t=2), x[:, 2 * i:2 * i + 2, :], ALU.add)
            last.then_inc(MO.b2, 1)
            dve.wait_ge(MO.b2, 1)
            dve.sem_inc(MO.w2_free, 4)
            dve.wait_ge(ld["pad"], 32)
            for i in range(2):
                nc.vector.tensor_scalar(padneg[0:1, 8 * i:8 * i + 8, :], maskrow[i][0:1, :, :], 0.0, NEG, ALU.is_equal, ALU.mult).then_inc(MO.pad, 1)
            tiles(dve, step)

        def pool_moe(pool):
            tiles(pool, lambda t, s, nxt: row_rstd(pool, t, s, "x1"))

        class FF:
            w0 = sem("ff_w0")
            w = sem("ff_w")
            scale = sem("ff_scale")
            xT_ps = sem("ff_xT_ps")
            xT_hi = sem("ff_xT_hi")
            xT = sem("ff_xT")
            r_ps = sem("ff_r_ps")
            r_free = sem("ff_r_free")
            h_free = sem("ff_h_free")
            hi = sem("ff_hi")
            hi_odd = sem("ff_hi_odd")
            split = sem("ff_split")
            y_ps = sem("ff_y_ps")
            y_free = sem("ff_y_free")
        def dve_ff_weights(dve, i):
            dve.wait_ge(ld_ff, 48)
            nc.vector.tensor_tensor(ffw0[:, i, :], raw0[:, i, :], raw0[:, KD + i, :], ALU.subtract).then_inc(FF.w0, 1)

        def act_ff_weights(act, t):
            act.wait_ge(ld_ff, 48)
            one = bass.ds(t, 1)
            nc.scalar.activation(ffw1[:, one, :], raw1[:, one, :], ACT.Identity, bias=minus1[:, :], scale=2.0).then_inc(FF.w, 1)
            nc.scalar.activation(ffw2[:, one, :], raw2[:, one, :], ACT.Identity, bias=minus1[:, :], scale=2.0).then_inc(FF.w, 1)

        def pe_ff(pe):
            def rows_T(t):
                pe.wait_ge(rn_done, ROW_BASE["mlp"] + t + 1)
                pe.wait_ge(FF.xT, t + 1)
                for k in range(KD):
                    last = nc.tensor.transpose(ps[:, t % 2, k * P:k * P + P], fn[t % 2][:, k * P:k * P + P], ident)
                last.then_inc(FF.xT_ps, 1)

            pe.wait_ge(FF.w0, KD)
            pe.wait_ge(FF.w, 2 * FT)
            for t in range(4):
                rows_T(t)
            for c in range(2):
                pe.wait_ge(FF.xT, 4 * c + 6)
                for layer, (w, src, ks) in enumerate(((ffw0, fxT, KD), (ffw1, f0, FT))):
                    for f in range(FT):
                        n = 16 * c + 8 * layer + f
                        if c == 0 and layer == 1 and f in (0, 4):
                            rows_T(4 + f // 2)
                            rows_T(5 + f // 2)
                        pe.wait_ge(FF.r_free, n + 1)
                        for k in range(ks):
                            if layer == 1 and f == 0:
                                pe.wait_ge(FF.split, 16 * c + k + 1)
                            for part in range(2):
                                last = nc.tensor.matmul(ps[:, 2 + f % 4, :], w[:, k, f * P:f * P + P], src[part][:, k, :],
                                                        start=(k == 0 and part == 0), stop=(k == ks - 1 and part == 1))
                        last.then_inc(FF.r_ps, 1)
                for i in range(4):
                    pe.wait_ge(FF.y_free, 4 * c + i + 1)
                    for k in range(FT):
                        if i == 0:
                            pe.wait_ge(FF.split, 16 * c + 8 + k + 1)
                        for part in range(2):
                            last = nc.tensor.matmul(ps[:, 6 + i % 2, 0:D], f1[part][:, k, i * P:i * P + P], ffw2[:, k, :],
                                                    start=(k == 0 and part == 0), stop=(k == FT - 1 and part == 1))
                    last.then_inc(FF.y_ps, 1)

        def act_ff(act):
            def upper(t):
                i = t % 4
                act.wait_ge(FF.xT_ps, t + 1)
                nc.scalar.activation(fxT[0][:, :, i * P:i * P + P], ps[:, t % 2, 0:D].rearrange("p (k n) -> p k n", k=2), ACT.Copy).then_inc(FF.xT_hi, 1)

            act.sem_inc(FF.r_free, 4)
            act.wait_ge(FF.scale, 2)
            for t in range(4):
                upper(t)
            for c in range(2):
                for layer, dst in enumerate((f0, f1)):
                    for f in range(FT):
                        n = 16 * c + 8 * layer + f
                        if c == 0 and layer == 1 and f in (0, 4):
                            upper(4 + f // 2)
                            upper(5 + f // 2)
                        act.wait_ge(FF.r_ps, n + 1)
                        act.wait_ge(FF.h_free, n + 1)
                        nc.scalar.activation(fh[f % 2][:, :], ps[:, 2 + f % 4, :], ACT.Relu, scale=ffs[:, layer:layer + 1]).then_inc(FF.r_free, 1)
                        if f % 2 == 1:
                            act.wait_ge(FF.r_free, n + 5)
                            nc.scalar.activation(dst[0][:, f, :], fh[1][:, :], ACT.Copy).then_inc(FF.hi_odd, 1)

        def dve_ff(dve):
            nc.vector.tensor_scalar(ffs[:, 0:1], vec("s0"), 4.0, None, ALU.mult).then_inc(FF.scale, 1)
            nc.vector.tensor_scalar(ffs[:, 1:2], vec("s1"), 2.0, None, ALU.mult).then_inc(FF.scale, 1)
            for k, v in ((FF.xT, 2), (FF.h_free, 2), (FF.y_free, 2)):
                dve.sem_inc(k, v)

            def norm(t):
                if t > 1:
                    dve.wait_ge(FF.xT_ps, t - 1)
                row_apply(dve, t, x[:, t, :], [fn[t % 2][:, :]], "mlp")

            def lower(t):
                i = t % 4
                dve.wait_ge(FF.xT_hi, t + 1)
                nc.vector.tensor_tensor(fxT[1][:, :, i * P:i * P + P], ps[:, t % 2, 0:D].rearrange("p (k n) -> p k n", k=2),
                                        fxT[0][:, :, i * P:i * P + P].bitcast(F32), ALU.subtract).then_inc(FF.xT, 1)

            dve.wait_ge(SA.y_free, 3 * T + 1)
            norm(0)
            norm(1)
            for t in range(4):
                lower(t)
                if t < 2:
                    norm(t + 2)
            for c in range(2):
                for layer, dst in enumerate((f0, f1)):
                    for f in range(FT):
                        n = 16 * c + 8 * layer + f
                        dve.wait_ge(FF.r_free, n + 5)
                        if f % 2 == 0:
                            nc.vector.tensor_copy(dst[0][:, f, :], fh[0][:, :]).then_inc(FF.hi, 1)
                            dve.wait_ge(FF.hi, n // 2 + 1)
                        else:
                            dve.wait_ge(FF.hi_odd, n // 2 + 1)
                        nc.vector.tensor_tensor(dst[1][:, f, :], fh[f % 2][:, :], dst[0][:, f, :].bitcast(F32), ALU.subtract).then_inc(FF.split, 1)
                        dve.wait_ge(FF.split, n + 1)
                        dve.sem_inc(FF.h_free, 1)
                        if c == 0 and layer == 0 and f in (4, 5):
                            norm(f)
                        if c == 0 and layer == 1 and f in (0, 1):
                            lower(4 + f)
                            norm(6 + f)
                        if c == 0 and layer == 1 and f in (4, 5):
                            lower(2 + f)
                for i in range(4):
                    t = 4 * c + i
                    dve.wait_ge(FF.y_ps, t + 1)
                    nc.vector.scalar_tensor_tensor(x[:, t, :], ps[:, 6 + i % 2, 0:D], vec("s2"), x[:, t, :], ALU.mult, ALU.add).then_inc(FF.y_free, 1)

        @block.sync
        def _(sp):
            def whole(dst, src, s):
                sp.dma_start(dst, src).then_inc(s, 16)

            def weight(name):
                return a[name].rearrange("(k p) n -> p k n", p=P)

            def ctx_tile(l, t, s):
                sp.dma_start((X0, X1)[l]["cin"][:, s, :, :], y_at[bass.ds(t, 1), :, :, :].rearrange("o p k d -> p (o k) d")).then_inc(ld_ctx[l][s], 16)

            def expert(e, s):
                sp.dma_start(ew1[s][:, :, :], a["L0_ffn_W1"][bass.ds(e, 1), :, :].rearrange("o (k p) n -> p (o k) n", p=P)).then_inc(ld_e[s], 16)
                sp.dma_start(ew2[s][:, :, :], a["L0_ffn_W2"][bass.ds(e, 1), :, :].rearrange("o (k p) n -> p (o k) n", p=P)).then_inc(ld_e[s], 16)

            x_in = a["x"].rearrange("b n d -> (b n) d").rearrange("(t p) d -> p t d", p=P)
            ctx_tile(0, 0, 0)
            whole(x[:, 0:2, :], x_in[:, 0:2, :], ld["x"])
            whole(cst[:, :], a["consts"], ld["const"])
            whole(col[:, :], a["cols"], ld["const"])
            whole(X0["wq"][:, :, :], weight("L0_xattn_Wq"), ld["x0q"])
            for half, k in enumerate(("x0k", "x0v")):
                part = slice(half * INNER, half * INNER + INNER)
                whole(X0["wkv"][:, :, part], weight("L0_xattn_Wkv")[:, :, part], ld[k])
            ctx_tile(0, 1, 1)
            whole(X0["wo"][:, :, :], weight("L0_xattn_Wo"), ld["x0o"])
            whole(x[:, 2:T, :], x_in[:, 2:T, :], ld["x_rest"])
            whole(rows[:, :, :], a["rows"], ld["rows"])
            for i, w in enumerate(("wq", "wkv")):
                whole(w_mla[:, :, 64 * i:64 * i + 64], weight("L0_attn_" + w), ld["mla"])
            for i, w in enumerate(("wqr", "wqr_swapped", "wkr", "wkr_swapped")):
                whole(w_mla[:, :, P + P * i:2 * P + P * i], weight("L0_attn_" + w), ld["mla"])
            whole(w_mlao[:, :, :], weight("L0_attn_wo"), ld["mla"])
            sp.wait_ge(pool_setup, 4)
            whole(w_mlac[0:64, 0:P], a["L0_attn_wqc"], ld["mla"])
            whole(w_mlac[64:P, P:2 * P], a["L0_attn_wkc"], ld["mla"])
            whole(w_mlac[64:P, 2 * P:2 * P + D], a["L0_attn_wv"], ld["mla"])
            whole(wg[:, :, 0:E], weight("L0_ffn_Wg"), ld["wg"])
            for i, w in enumerate(("Wq", "Wk", "Wv", "Wo")):
                whole(w_sq[0][:, :, i, :], weight("L0_ffn_" + w), ld["sq0"])
            for i, w in enumerate("QKVO"):
                whole(w_sq[1][:, :, i, :], weight("L1_attn_W_" + w), ld["sq1"])
            with sp.Fori(0, T // 2 - 1) as i:
                for s in range(2):
                    sp.wait_ge(ln_done, 2 * (2 * i + s) + 2)
                    ctx_tile(0, 2 * i + s + 2, s)
            sp.wait_ge(X[0].x_done, T)
            sp.wait_ge(pool_setup, 6)
            whole(b2[0:E, :], a["L0_ffn_b2"], ld["b2"])
            for i, w in enumerate(("Wq", "Wk", "Wv", "Wo")):
                whole(xw[:, :, i, :], weight("L1_xattn_" + w), ld["xw"])
            for e in range(2):
                expert(e, e)
            sp.wait_ge(MO.mT_ps, T)
            sp.wait_ge(SA.y_ps, 2 * T)
            for i in range(2):
                whole(maskrow[i][0:1, :, :], a["mask_BxS2_ik0"].rearrange("(o h b) s -> h o b s", o=1, h=2)[i], ld["pad"])
            with sp.Fori(0, E // 2 - 1) as i:
                for s in range(2):
                    sp.wait_ge(MO.out_ps, 2 * FT * (2 * i + s) + 2 * FT + 2)
                    expert(2 * i + s + 2, s)
            sp.wait_ge(MO.pad, 2)
            ctx_tile(1, 0, 0)
            ctx_tile(1, 1, 1)
            with sp.Fori(0, T // 2 - 1) as i:
                for s in range(2):
                    for bank in range(2):
                        sp.wait_ge(X[1].fill_done[bank], X[1].per * (2 * i + s) + X[1].first["cT"] // 2 + 1)
                    ctx_tile(1, 2 * i + s + 2, s)
            sp.wait_ge(X[1].x_done, T)
            whole(raw0[:, :, :], weight("L1_ffn_k0"), ld_ff)
            whole(raw1[:, :, :], weight("L1_ffn_k1"), ld_ff)
            whole(raw2[:, :, :], weight("L1_ffn_k2"), ld_ff)
            out_v = out.rearrange("b n d -> (b n) d").rearrange("(t p) d -> p t d", p=P)
            for c in range(4):
                sp.wait_ge(FF.y_free, 2 * c + 4)
                sp.dma_start(out_v[:, 2 * c:2 * c + 2, :], x[:, 2 * c:2 * c + 2, :]).then_inc(stored, 16)
            sp.wait_ge(stored, 64)
            sp.wait_ge(dve_go, T + 2 * (2 * T + len(ROW_BASE) * T))
            sp.wait_ge(pool_go, len(ROW_BASE) * T + T)
            sp.wait_ge(act_go, 2 * E * FT)

        @block.gpsimd
        def _(pool):
            nc.gpsimd.memset(neghalf[:, :], -0.5).then_inc(pool_setup, 1)
            nc.gpsimd.memset(eps[:, :], EPS).then_inc(pool_setup, 1)
            nc.gpsimd.memset(w_mlac[:, :], 0.0).then_inc(pool_setup, 1)
            nc.gpsimd.memset(wg[:, :, :], 0.0).then_inc(pool_setup, 1)
            nc.gpsimd.memset(padneg[:, :, :], 0.0).then_inc(pool_setup, 1)
            pool.wait_ge(pool_setup, 5)
            pool_cross(pool, X[0])
            pool.wait_ge(X[0].x_done, T)
            nc.gpsimd.memset(b2[:, :], 0.0).then_inc(pool_setup, 1)
            nc.gpsimd.memset(gate[:, :, :], 0.0).then_inc(pool_setup, 1)
            nc.gpsimd.memset(minus1[:, :], -1.0).then_inc(pool_setup, 1)
            pool_self(pool, 0)
            pool_self(pool, 1)
            pool_moe(pool)
            pool_cross(pool, X[1])
            pool_self(pool, 2)

        @block.scalar
        def _(act):
            act.wait_ge(ld["const"], 32)
            act_cross(act, X[0])
            act_self(act, 0)
            act_self(act, 1)
            act_moe(act)
            act_cross(act, X[1])
            act_self(act, 2)
            act_ff(act)

        @block.vector
        def _(dve):
            dve.wait_ge(ld["const"], 32)
            dve.wait_ge(ld["x"], 16)
            nc.vector.tensor_copy(identb[:, :], ident).then_inc(setup, 1)
            nc.vector.tensor_copy(causalb[:, :], cst[:, C_CAUSAL:C_CAUSAL + N]).then_inc(setup, 1)
            nc.vector.tensor_copy(row0b[:, :], cst[:, C_ROW0:C_ROW0 + P]).then_inc(setup, 1)
            dve_cross(dve, X[0])
            dve_self(dve, 0, X[0].x_done, T)
            dve_self(dve, 1, SA.x_done, T)
            dve_moe(dve)
            dve.wait_ge(MO.w2_free, 8 * E + 4)
            dve_cross(dve, X[1])
            dve_self(dve, 2, X[1].x_done, T)
            dve_ff(dve)

        @block.tensor
        def _(pe):
            pe.wait_ge(ld["const"], 32)
            pe_cross(pe, X[0])
            pe_self(pe, 0)
            pe_self(pe, 1)
            pe_moe(pe)
            pe_cross(pe, X[1])
            pe_self(pe, 2)
            pe_ff(pe)


def ctx_views(ctx):
    return ctx.rearrange("b s d -> (b s) d").rearrange("(t k p) d -> t p k d", k=4, p=P)


def _tables(i):
    p = np.arange(P)
    cst = np.zeros((P, C_ALL), np.float32)
    cst[:, C_IDENT:C_IDENT + P] = np.eye(P)
    cst[:, C_HEAD:C_HEAD + 8] = p[:, None] // 16 == np.arange(8)
    cst[:, C_PAR:C_PAR + 2] = p[:, None] // 16 % 2 == np.arange(2)
    cst[:, C_CAUSAL:C_CAUSAL + N] = np.where(np.arange(N)[None, :] > (p % N)[:, None], NEG, 0.0)
    inv = (1.0 / np.float32(10000.0) ** (np.arange(0, P, 2, dtype=np.float32) / np.float32(P))).astype(np.float32)
    ang = np.tile(np.arange(N, dtype=np.float32)[None, :] * inv[:, None], (2, 2))
    cst[:, C_COS:C_COS + P] = np.cos(ang)
    cst[:, C_SIN:C_SIN + P] = np.sin(ang) * np.where(p < 64, -1, 1)[:, None]
    cst[:, C_IOTA:C_IOTA + E] = np.arange(E)
    cst[0, C_ROW0:C_ROW0 + P] = 1.0
    half = lambda v: np.concatenate([v[64:], v[:64]])
    vecs = {"ln_l_w": i["L0_xattn_ln_l_w"], "ln_l_b": i["L0_xattn_ln_l_b"], "ln_c_w": i["L0_xattn_ln_c_w"], "ln_c_b": i["L0_xattn_ln_c_b"],
            "bqkv": np.concatenate([i["L0_attn_bq"], i["L0_attn_bkv"]]), "bqc": i["L0_attn_bqc"], "bkc": i["L0_attn_bkc"],
            "bqr": i["L0_attn_bqr"], "bqs": half(i["L0_attn_bqr"]), "bkr": i["L0_attn_bkr"], "bks": half(i["L0_attn_bkr"]),
            "bv0": i["L0_attn_bv"], "ln1_g": i["L0_ffn_ln1_g"], "ln1_b": i["L0_ffn_ln1_b"], "ln2_g": i["L0_ffn_ln2_g"], "ln2_b": i["L0_ffn_ln2_b"],
            "xbq": i["L1_xattn_bq"], "xbk": i["L1_xattn_bk"], "xbv": i["L1_xattn_bv"], "b1": i["L0_ffn_b1"].reshape(-1),
            "s0": np.broadcast_to(i["L1_ffn_s0"], (P,)), "s1": np.broadcast_to(i["L1_ffn_s1"], (P,)), "s2": np.broadcast_to(i["L1_ffn_s2"], (P,))}
    cols = np.concatenate([np.reshape(vecs[k], (-1, P)).T for k in COLS], 1)
    rows = np.stack([np.broadcast_to(i[k], (P, D)) for k in ("L0_xattn_bo", "L0_attn_bo", "L1_xattn_bo")], 1)
    return {"consts": cst, "cols": cols, "rows": rows}


def _inputs(i):
    ins = {k: v for k, v in i.items() if k in ("x", "ctx_1024", "mask_BxS2_ik0") or v.ndim >= 2}
    for k in "QKVO":
        ins[f"L1_attn_W_{k}"] = ins[f"L1_attn_W_{k}"].T
    for k in ("wqr", "wkr"):
        w = ins[f"L0_attn_{k}"]
        ins[f"L0_attn_{k}_swapped"] = np.concatenate([w[:, 64:], w[:, :64]], 1)
    ins.update(_tables(i))
    return {k: np.ascontiguousarray(v) for k, v in ins.items()}


def kernel(**inputs):
    import concourse.bacc as bacc
    from concourse.bass_utils import run_bass_kernel_spmd

    arrays = _inputs({k: np.asarray(v) for k, v in inputs.items()})
    nc = bacc.Bacc("TRN2", target_bir_lowering=False, num_devices=1)
    aps = {k: nc.dram_tensor(k + "_dram", v.shape, mybir.dt.from_np(v.dtype), kind="ExternalInput").ap() for k, v in arrays.items()}
    out = nc.dram_tensor("out_dram", (B, N, D), F32, kind="ExternalOutput").ap()
    build(nc, aps, out)
    r = run_bass_kernel_spmd(nc, [{k + "_dram": v for k, v in arrays.items()}], core_ids=[0])
    return r.results[0]["out_dram"]
```
